# Optimizing a Trainium2 kernel written in Bass

```python
import numpy as np
import jax
import jax.numpy as jnp

def _softmax(x, axis=-1):
    return jax.nn.softmax(x, axis=axis)

def _gelu(x):
    return jax.nn.gelu(x, approximate=True)

def _silu(x):
    return jax.nn.silu(x)

def _sigmoid(x):
    return jax.nn.sigmoid(x)

def _layernorm(x, axis=-1, eps=1e-05):
    m = jnp.mean(x, axis=axis, keepdims=True)
    v = jnp.var(x, axis=axis, keepdims=True)
    return (x - m) / jnp.sqrt(v + eps)

def _scatter_add(tgt, idx, src, axis=0):
    return tgt.at[idx].add(src)

def _segment_sum(src, seg, n):
    return jax.ops.segment_sum(src, seg, n)
kernel_name = 'mk_decoder_postln_d2_seqx_r8_140e3f'

def setup_inputs(seed: int=0):
    np.random.seed(seed)
    _w = jnp.asarray

    def _rec_inputs():
        import jax
        import jax.numpy as jnp
        _rk = jax.random.key(seed)
        x = 7.22e-05 + 1 * jax.random.normal(jax.random.fold_in(_rk, 1), (16, 56, 512), jnp.float32)
        _lenS = 56 - jax.random.randint(jax.random.fold_in(_rk, 7), (16,), 0, max(1, 56 // 4) + 1, jnp.int32)
        _lenS2 = 1500 - jax.random.randint(jax.random.fold_in(_rk, 8), (16,), 0, max(1, 1500 // 4) + 1, jnp.int32)
        _ctx_4096P = jax.random.normal(jax.random.fold_in(_rk, 11), (16, 16, 512), jnp.float32)
        _ctx_4096c = jax.random.dirichlet(jax.random.fold_in(_rk, 511), 0.3 * jnp.ones((16,), jnp.float32), (16, 1500))
        _ctx_4096t = jnp.einsum('bsk,bkd->bsd', _ctx_4096c, _ctx_4096P)
        _ctx_4096t = _ctx_4096t * jax.lax.rsqrt(jnp.mean(jnp.square(_ctx_4096t)) + 1e-12) * 0.953939
        ctx_4096 = 4.13588e-05 + 0.999923 * (_ctx_4096t + 0.3 * jax.random.normal(jax.random.fold_in(_rk, 611), (16, 1500, 512), jnp.float32))
        _validS = jnp.arange(56)[None, :] < _lenS[:, None]
        _validS2 = jnp.arange(1500)[None, :] < _lenS2[:, None]
        _causal = jnp.tril(jnp.ones((56, 56), dtype=bool))
        mask_SxS2_bk0 = jnp.logical_not(jnp.broadcast_to(_validS2[0:1, :], (56, 1500)))
        return (x, ctx_4096, mask_SxS2_bk0)
    x, ctx_4096, mask_SxS2_bk0 = _rec_inputs()

    def _L0_attn_setup():
        import jax, jax.numpy as jnp
        import numpy as np
        import math
        B, L, D, H = (32, 64, 512, 32)
        HD = D // H
        key = jax.random.key(seed)
        ks = jax.random.split(key, 9)
        s = 1.0 / math.sqrt(D)
        return {'x': jax.random.normal(ks[0], (B, L, D), jnp.float32), 'Wq': jax.random.normal(ks[1], (D, D), jnp.float32) * s, 'bq': jax.random.normal(ks[2], (D,), jnp.float32) * s, 'Wk': jax.random.normal(ks[3], (D, D), jnp.float32) * s, 'bk': jax.random.normal(ks[4], (D,), jnp.float32) * s, 'Wv': jax.random.normal(ks[5], (D, D), jnp.float32) * s, 'bv': jax.random.normal(ks[6], (D,), jnp.float32) * s, 'Wo': jax.random.normal(ks[7], (D, D), jnp.float32) * s, 'bo': jax.random.normal(ks[8], (D,), jnp.float32) * s}
    _L0_attn_all = _L0_attn_setup()
    _L0_attn_in = {k: v for k, v in _L0_attn_all.items() if k in ('Wq', 'bq', 'Wk', 'bk', 'Wv', 'bv', 'Wo', 'bo')}
    del _L0_attn_all

    def _L0_xattn_setup():
        import jax, jax.numpy as jnp
        import numpy as np
        DIM = 512
        NUM_HEADS = 32
        NUM_KV_HEADS = 8
        HEAD_DIM = DIM // NUM_HEADS
        KV_DIM = DIM // (NUM_HEADS // NUM_KV_HEADS)
        B, S = (1, 256)
        key = jax.random.key(seed)
        ks = jax.random.split(key, 7)
        w_scale = DIM ** (-0.5)
        return {'query': jax.random.normal(ks[0], (B, S, DIM), jnp.float32), 'key': jax.random.normal(ks[1], (B, S, DIM), jnp.float32), 'value': jax.random.normal(ks[2], (B, S, DIM), jnp.float32), 'Wq': jax.random.normal(ks[3], (DIM, DIM), jnp.float32) * w_scale, 'Wk': jax.random.normal(ks[4], (DIM, KV_DIM), jnp.float32) * w_scale, 'Wv': jax.random.normal(ks[5], (DIM, KV_DIM), jnp.float32) * w_scale, 'Wo': jax.random.normal(ks[6], (DIM, DIM), jnp.float32) * w_scale}
    _L0_xattn_all = _L0_xattn_setup()
    _L0_xattn_in = {k: v for k, v in _L0_xattn_all.items() if k in ('Wq', 'Wk', 'Wv', 'Wo')}
    del _L0_xattn_all

    def _L0_ffn_setup():
        import jax, jax.numpy as jnp
        import numpy as np
        HID, INT, LAT, NE, K = (512, 1024, 256, 8, 2)
        LN_EPS = 1e-05

        def _layernorm(x, gamma, beta):
            mu = jnp.mean(x, axis=-1, keepdims=True)
            var = jnp.var(x, axis=-1, keepdims=True)
            return (x - mu) * jax.lax.rsqrt(var + LN_EPS) * gamma + beta
        key = jax.random.key(seed)
        ks = jax.random.split(key, 8)
        s = lambda d: 1.0 / np.sqrt(d)
        return {'hidden_states': jax.random.normal(ks[0], (4, 256, HID), jnp.float32), 'gate_w': jax.random.normal(ks[1], (HID, NE), jnp.float32) * s(HID), 'up_w': jax.random.normal(ks[2], (HID, INT), jnp.float32) * s(HID), 'down_w': jax.random.normal(ks[3], (INT, HID), jnp.float32) * s(INT), 'fc1_w': jax.random.normal(ks[4], (HID, LAT), jnp.float32) * s(HID), 'fc2_w': jax.random.normal(ks[5], (LAT, HID), jnp.float32) * s(LAT), 'expert_w': jax.random.normal(ks[6], (LAT, LAT), jnp.float32), 'ln_gamma': jnp.ones((HID,), jnp.float32), 'ln_beta': jnp.zeros((HID,), jnp.float32)}
    _L0_ffn_all = _L0_ffn_setup()
    _L0_ffn_in = {k: v for k, v in _L0_ffn_all.items() if k in ('gate_w', 'up_w', 'down_w', 'fc1_w', 'fc2_w', 'expert_w', 'ln_gamma', 'ln_beta')}
    del _L0_ffn_all

    def _L1_attn_setup():
        import jax, jax.numpy as jnp
        import numpy as np
        DIM = 512
        NUM_HEAD = 32
        NUM_KV_HEAD = 8
        ROPE_THETA = 10000.0
        B, T = (2, 256)

        def apply_rope(x, start_pos=0, theta=ROPE_THETA):
            d = x.shape[-1]
            half = d // 2
            inv_freq = 1.0 / theta ** (jnp.arange(0, half, dtype=jnp.float32) / half)
            pos = jnp.arange(x.shape[1], dtype=jnp.float32) + start_pos
            ang = pos[:, None] * inv_freq[None, :]
            cos = jnp.cos(ang)[None, :, None, :]
            sin = jnp.sin(ang)[None, :, None, :]
            x1, x2 = (x[..., :half], x[..., half:])
            return jnp.concatenate([x1 * cos - x2 * sin, x1 * sin + x2 * cos], axis=-1)
        key = jax.random.key(seed)
        ks = jax.random.split(key, 5)
        scale = 0.02
        X = jax.random.normal(ks[0], (B, T, DIM), dtype=jnp.float32)
        Wq = jax.random.normal(ks[1], (DIM, DIM), dtype=jnp.float32) * scale
        Wk = jax.random.normal(ks[2], (DIM, DIM // NUM_HEAD * NUM_KV_HEAD), dtype=jnp.float32) * scale
        Wv = jax.random.normal(ks[3], (DIM, DIM // NUM_HEAD * NUM_KV_HEAD), dtype=jnp.float32) * scale
        Wo = jax.random.normal(ks[4], (DIM, DIM), dtype=jnp.float32) * scale
        return {'X': X, 'Wq': Wq, 'Wk': Wk, 'Wv': Wv, 'Wo': Wo}
    _L1_attn_all = _L1_attn_setup()
    _L1_attn_in = {k: v for k, v in _L1_attn_all.items() if k in ('Wq', 'Wk', 'Wv', 'Wo')}
    del _L1_attn_all

    def _L1_xattn_setup():
        import jax, jax.numpy as jnp
        import numpy as np
        N_HEAD = 32
        D_MODEL = 512
        N_KV_GROUPS = 8
        D_HEAD = D_MODEL // N_HEAD
        H_PER_G = N_HEAD // N_KV_GROUPS
        KV_DIM = N_KV_GROUPS * D_HEAD
        B, S = (2, 256)
        key = jax.random.key(seed)
        ks = jax.random.split(key, 8)
        q = jax.random.normal(ks[0], (B, S, D_MODEL), dtype=jnp.float32)
        k = jax.random.normal(ks[1], (B, S, D_MODEL), dtype=jnp.float32)
        v = jax.random.normal(ks[2], (B, S, D_MODEL), dtype=jnp.float32)
        mask = jnp.tril(jnp.ones((S, S), dtype=bool))
        w_q = jax.random.uniform(ks[3], (D_MODEL, D_MODEL), dtype=jnp.float32) * 0.02
        w_k = jax.random.uniform(ks[4], (KV_DIM, D_MODEL), dtype=jnp.float32) * 0.02
        w_v = jax.random.uniform(ks[5], (KV_DIM, D_MODEL), dtype=jnp.float32) * 0.02
        w_out = jax.random.uniform(ks[6], (D_MODEL, D_MODEL), dtype=jnp.float32) * 0.02
        return {'q': q, 'k': k, 'v': v, 'w_q': w_q, 'w_k': w_k, 'w_v': w_v, 'w_out': w_out, 'mask': mask}
    _L1_xattn_all = _L1_xattn_setup()
    _L1_xattn_in = {k: v for k, v in _L1_xattn_all.items() if k in ('w_q', 'w_k', 'w_v', 'w_out')}
    del _L1_xattn_all

    def _L1_ffn_setup():
        import jax, jax.numpy as jnp
        import numpy as np
        LORA_SCALE = 16.0 / jnp.sqrt(16.0)
        TOP_K = 2
        key = jax.random.key(seed)
        k1, k2, k3, k4 = jax.random.split(key, 4)
        B_, S, D, O, E, R = (4, 256, 512, 512, 4, 16)
        x = jax.random.normal(k1, (B_, S, D), dtype=jnp.float32)
        router_w = jax.random.normal(k2, (E, D), dtype=jnp.float32) * 0.02
        A = jax.random.normal(k3, (E, R, D), dtype=jnp.float32) * 0.02
        B = jax.random.normal(k4, (O,), dtype=jnp.float32)
        B = jax.random.normal(k4, (E, O, R), dtype=jnp.float32) * 0.02
        return {'x': x, 'router_w': router_w, 'A': A, 'B': B}
    _L1_ffn_all = _L1_ffn_setup()
    _L1_ffn_in = {k: v for k, v in _L1_ffn_all.items() if k in ('router_w', 'A', 'B')}
    del _L1_ffn_all
    return {'x': x, 'ctx_4096': ctx_4096, 'mask_SxS2_bk0': mask_SxS2_bk0, 'L0_attn_Wq': _L0_attn_in['Wq'], 'L0_attn_bq': _L0_attn_in['bq'], 'L0_attn_Wk': _L0_attn_in['Wk'], 'L0_attn_bk': _L0_attn_in['bk'], 'L0_attn_Wv': _L0_attn_in['Wv'], 'L0_attn_bv': _L0_attn_in['bv'], 'L0_attn_Wo': _L0_attn_in['Wo'], 'L0_attn_bo': _L0_attn_in['bo'], 'L0_xattn_Wq': _L0_xattn_in['Wq'], 'L0_xattn_Wk': _L0_xattn_in['Wk'], 'L0_xattn_Wv': _L0_xattn_in['Wv'], 'L0_xattn_Wo': _L0_xattn_in['Wo'], 'L0_ffn_gate_w': _L0_ffn_in['gate_w'], 'L0_ffn_up_w': _L0_ffn_in['up_w'], 'L0_ffn_down_w': _L0_ffn_in['down_w'], 'L0_ffn_fc1_w': _L0_ffn_in['fc1_w'], 'L0_ffn_fc2_w': _L0_ffn_in['fc2_w'], 'L0_ffn_expert_w': _L0_ffn_in['expert_w'], 'L0_ffn_ln_gamma': _L0_ffn_in['ln_gamma'], 'L0_ffn_ln_beta': _L0_ffn_in['ln_beta'], 'L1_attn_Wq': _L1_attn_in['Wq'], 'L1_attn_Wk': _L1_attn_in['Wk'], 'L1_attn_Wv': _L1_attn_in['Wv'], 'L1_attn_Wo': _L1_attn_in['Wo'], 'L1_xattn_w_q': _L1_xattn_in['w_q'], 'L1_xattn_w_k': _L1_xattn_in['w_k'], 'L1_xattn_w_v': _L1_xattn_in['w_v'], 'L1_xattn_w_out': _L1_xattn_in['w_out'], 'L1_ffn_router_w': _L1_ffn_in['router_w'], 'L1_ffn_A': _L1_ffn_in['A'], 'L1_ffn_B': _L1_ffn_in['B']}

def reference(x, ctx_4096, mask_SxS2_bk0, L0_attn_Wq, L0_attn_bq, L0_attn_Wk, L0_attn_bk, L0_attn_Wv, L0_attn_bv, L0_attn_Wo, L0_attn_bo, L0_xattn_Wq, L0_xattn_Wk, L0_xattn_Wv, L0_xattn_Wo, L0_ffn_gate_w, L0_ffn_up_w, L0_ffn_down_w, L0_ffn_fc1_w, L0_ffn_fc2_w, L0_ffn_expert_w, L0_ffn_ln_gamma, L0_ffn_ln_beta, L1_attn_Wq, L1_attn_Wk, L1_attn_Wv, L1_attn_Wo, L1_xattn_w_q, L1_xattn_w_k, L1_xattn_w_v, L1_xattn_w_out, L1_ffn_router_w, L1_ffn_A, L1_ffn_B):
    import jax
    import jax.numpy as jnp

    def _L0_attn_ref(x, Wq, bq, Wk, bk, Wv, bv, Wo, bo):
        import jax, jax.numpy as jnp
        import numpy as np
        import math
        B, L, D, H = (32, 64, 512, 32)
        HD = D // H
        b, l, d = x.shape
        h, hd = (H, HD)
        q = (x @ Wq.T + bq).reshape(b, l, h, hd).transpose(0, 2, 1, 3)
        k = (x @ Wk.T + bk).reshape(b, l, h, hd).transpose(0, 2, 1, 3)
        v = (x @ Wv.T + bv).reshape(b, l, h, hd).transpose(0, 2, 1, 3)
        scores = jnp.einsum('bhqd,bhkd->bhqk', q, k) / math.sqrt(hd)
        causal = jnp.tril(jnp.ones((l, l), bool))
        scores = jnp.where(causal, scores, -jnp.inf)
        att = jax.nn.softmax(scores, axis=-1)
        out = jnp.einsum('bhqk,bhkd->bhqd', att, v)
        out = out.transpose(0, 2, 1, 3).reshape(b, l, d)
        return out @ Wo.T + bo

    def _L0_xattn_ref(query, key, value, Wq, Wk, Wv, Wo):
        import jax, jax.numpy as jnp
        import numpy as np
        DIM = 512
        NUM_HEADS = 32
        NUM_KV_HEADS = 8
        HEAD_DIM = DIM // NUM_HEADS
        KV_DIM = DIM // (NUM_HEADS // NUM_KV_HEADS)
        B, S = (1, 256)
        b, sq, _ = query.shape
        _, sk, _ = key.shape
        rep = NUM_HEADS // NUM_KV_HEADS
        q = (query @ Wq).reshape(b, sq, NUM_HEADS, HEAD_DIM).transpose(0, 2, 1, 3)
        k = (key @ Wk).reshape(b, sk, NUM_KV_HEADS, HEAD_DIM).transpose(0, 2, 1, 3)
        v = (value @ Wv).reshape(b, sk, NUM_KV_HEADS, HEAD_DIM).transpose(0, 2, 1, 3)
        k = jnp.repeat(k, rep, axis=1)
        v = jnp.repeat(v, rep, axis=1)
        scale = HEAD_DIM ** (-0.5)
        scores = jnp.einsum('bhqd,bhkd->bhqk', q, k) * scale
        probs = jax.nn.softmax(scores, axis=-1)
        out = jnp.einsum('bhqk,bhkd->bhqd', probs, v)
        out = out.transpose(0, 2, 1, 3).reshape(b, sq, DIM)
        return out @ Wo

    def _L0_ffn_ref(hidden_states, gate_w, up_w, down_w, fc1_w, fc2_w, expert_w, ln_gamma, ln_beta):
        import jax, jax.numpy as jnp
        import numpy as np
        HID, INT, LAT, NE, K = (512, 1024, 256, 8, 2)
        LN_EPS = 1e-05

        def _layernorm(x, gamma, beta):
            mu = jnp.mean(x, axis=-1, keepdims=True)
            var = jnp.var(x, axis=-1, keepdims=True)
            return (x - mu) * jax.lax.rsqrt(var + LN_EPS) * gamma + beta
        logits = jnp.einsum('bsh,he->bse', hidden_states, gate_w)
        routing_weights, selected_experts = jax.lax.top_k(logits, K)
        h = jax.nn.relu(jnp.einsum('bsh,hi->bsi', hidden_states, up_w)) ** 2
        shared_out = jnp.einsum('bsi,ih->bsh', h, down_w)
        x_latent = jnp.einsum('bsh,hl->bsl', hidden_states, fc1_w)
        expert_out = jnp.einsum('bsl,lm->bsm', x_latent, expert_w)
        moe_out = expert_out * jnp.sum(routing_weights, axis=-1, keepdims=True)
        routed_out = jnp.einsum('bsl,lh->bsh', moe_out, fc2_w)
        return _layernorm(shared_out + routed_out, ln_gamma, ln_beta)

    def _L1_attn_ref(X, Wq, Wk, Wv, Wo):
        import jax, jax.numpy as jnp
        import numpy as np
        DIM = 512
        NUM_HEAD = 32
        NUM_KV_HEAD = 8
        ROPE_THETA = 10000.0
        B, T = (2, 256)

        def apply_rope(x, start_pos=0, theta=ROPE_THETA):
            d = x.shape[-1]
            half = d // 2
            inv_freq = 1.0 / theta ** (jnp.arange(0, half, dtype=jnp.float32) / half)
            pos = jnp.arange(x.shape[1], dtype=jnp.float32) + start_pos
            ang = pos[:, None] * inv_freq[None, :]
            cos = jnp.cos(ang)[None, :, None, :]
            sin = jnp.sin(ang)[None, :, None, :]
            x1, x2 = (x[..., :half], x[..., half:])
            return jnp.concatenate([x1 * cos - x2 * sin, x1 * sin + x2 * cos], axis=-1)
        Bs, Ts, C = X.shape
        H, Hkv = (NUM_HEAD, NUM_KV_HEAD)
        dh = C // H
        G = H // Hkv
        Q = apply_rope((X @ Wq).reshape(Bs, Ts, H, dh))
        K = apply_rope((X @ Wk).reshape(Bs, Ts, Hkv, dh))
        V = (X @ Wv).reshape(Bs, Ts, Hkv, dh)
        Qh = Q.transpose(0, 2, 1, 3).reshape(Bs, Hkv, G, Ts, dh)
        Kh = K.transpose(0, 2, 1, 3)
        Vh = V.transpose(0, 2, 1, 3)
        scores = jnp.einsum('bkgtd,bksd->bkgts', Qh, Kh) / jnp.sqrt(jnp.float32(dh))
        causal = jnp.tril(jnp.ones((Ts, Ts), dtype=bool))
        scores = jnp.where(causal[None, None, None], scores, -jnp.inf)
        attn = jax.nn.softmax(scores, axis=-1)
        out = jnp.einsum('bkgts,bksd->bkgtd', attn, Vh)
        out = out.reshape(Bs, H, Ts, dh).transpose(0, 2, 1, 3).reshape(Bs, Ts, C)
        return out @ Wo

    def _L1_xattn_ref(q, k, v, w_q, w_k, w_v, w_out, mask):
        import jax, jax.numpy as jnp
        import numpy as np
        N_HEAD = 32
        D_MODEL = 512
        N_KV_GROUPS = 8
        D_HEAD = D_MODEL // N_HEAD
        H_PER_G = N_HEAD // N_KV_GROUPS
        KV_DIM = N_KV_GROUPS * D_HEAD
        B, S = (2, 256)
        b, n, _ = q.shape
        s = k.shape[1]
        query = q @ w_q.T
        key = k @ w_k.T
        value = v @ w_v.T
        query = query.reshape(b, n, N_HEAD, D_HEAD).transpose(0, 2, 1, 3)
        query = query.reshape(b, N_KV_GROUPS, H_PER_G, n, D_HEAD)
        key = key.reshape(b, s, N_KV_GROUPS, D_HEAD).transpose(0, 2, 1, 3)
        value = value.reshape(b, s, N_KV_GROUPS, D_HEAD).transpose(0, 2, 1, 3)
        scores = jnp.einsum('bghnd,bgsd->bghns', query, key) / D_HEAD ** 0.5
        scores = jnp.where(mask, scores, jnp.finfo(scores.dtype).min)
        attention = jax.nn.softmax(scores, axis=-1)
        out = jnp.einsum('bghns,bgsd->bghnd', attention, value)
        out = out.transpose(0, 3, 1, 2, 4).reshape(b, n, D_MODEL)
        return out @ w_out.T

    def _L1_ffn_ref(x, router_w, A, B):
        import jax, jax.numpy as jnp
        import numpy as np
        LORA_SCALE = 16.0 / jnp.sqrt(16.0)
        TOP_K = 2
        D = x.shape[-1]
        flat = x.reshape(-1, D)
        logits = flat @ router_w.T
        topk_vals, topk_idx = jax.lax.top_k(logits, TOP_K)
        sparse = jnp.full_like(logits, -jnp.inf)
        rows = jnp.arange(logits.shape[0])[:, None]
        sparse = sparse.at[rows, topk_idx].set(topk_vals)
        gates = jax.nn.softmax(sparse, axis=-1)
        mid = jnp.einsum('tf,erf->ter', flat, A)
        all_deltas = jnp.einsum('ter,eor->teo', mid, B) * LORA_SCALE
        delta = jnp.einsum('te,teo->to', gates, all_deltas)
        return delta.reshape(*x.shape[:-1], -1)
    x = _layernorm(x + _L0_attn_ref(x, L0_attn_Wq, L0_attn_bq, L0_attn_Wk, L0_attn_bk, L0_attn_Wv, L0_attn_bv, L0_attn_Wo, L0_attn_bo), axis=-1)
    x = _layernorm(x + _L0_xattn_ref(x, ctx_4096, ctx_4096, L0_xattn_Wq, L0_xattn_Wk, L0_xattn_Wv, L0_xattn_Wo), axis=-1)
    x = _layernorm(x + _L0_ffn_ref(x, L0_ffn_gate_w, L0_ffn_up_w, L0_ffn_down_w, L0_ffn_fc1_w, L0_ffn_fc2_w, L0_ffn_expert_w, L0_ffn_ln_gamma, L0_ffn_ln_beta), axis=-1)
    x = _layernorm(x + _L1_attn_ref(x, L1_attn_Wq, L1_attn_Wk, L1_attn_Wv, L1_attn_Wo), axis=-1)
    x = _layernorm(x + _L1_xattn_ref(x, ctx_4096, ctx_4096, L1_xattn_w_q, L1_xattn_w_k, L1_xattn_w_v, L1_xattn_w_out, mask_SxS2_bk0), axis=-1)
    x = _layernorm(x + _L1_ffn_ref(x, L1_ffn_router_w, L1_ffn_A, L1_ffn_B), axis=-1)
    return x

_drawn_inputs = setup_inputs


def setup_inputs(seed=0):
    import zlib

    import numpy as np

    out = dict(_drawn_inputs(seed))
    spreads = {'L0_ffn_ln_gamma': (1.0, 0.2), 'L0_ffn_ln_beta': (0.0, 0.1)}
    factors = {'L0_attn_bq': 4.498,
     'L0_attn_bk': 8.0,
     'L1_attn_Wq': 6.733,
     'L1_attn_Wk': 6.773,
     'L1_xattn_w_q': 8.0,
     'L1_xattn_w_k': 8.0,
     'L1_xattn_w_v': 5.542,
     'L1_xattn_w_out': 3.236}
    for name, (base, spread) in spreads.items():
        noise = np.random.default_rng([zlib.crc32(name.encode()), seed]).standard_normal(out[name].shape)
        drawn = base * np.exp(spread * noise) if base else spread * noise
        out[name] = jnp.asarray(drawn.astype(out[name].dtype))
    for name, factor in factors.items():
        out[name] = (out[name] * factor).astype(out[name].dtype)
    return out
```

```python
from contextlib import ExitStack

import concourse.bass as bass
from concourse import mybir

F32 = mybir.dt.float32
F16 = mybir.dt.float16
BF16 = mybir.dt.bfloat16
U8 = mybir.dt.uint8
ALU = mybir.AluOpType
ACT = mybir.ActivationFunctionType
AX = mybir.AxisListType

B, S, D = 16, 56, 512
KC = D // 128
SK = 1500
CH, NCH = 125, 12
NP, PT = 500, 3
H, G, J, HD = 32, 8, 4, 16
SP_ = 64
TILES = B // 2
U = 2
QG = J * S
QP = 2 * QG
NEG = -1e30
WSCALE = 64.0
VS = HD + 1
VW = NCH * G * VS + 16


class Arena:

    def __init__(self, nc, ctx, tag):
        self.nc, self.ctx, self.tag, self.sems = nc, ctx, tag, []
        ctx.callback(self.give_back)

    def give_back(self):
        self.nc.clear_and_free_semaphores(self.sems)
        self.nc.all_engine_barrier()

    def sb(self, name, shape, dt=F32):
        return self.ctx.enter_context(self.nc.sbuf_tensor(f"{self.tag}_{name}", shape, dt))

    def ps(self, name, shape=(128, 512)):
        return self.ctx.enter_context(self.nc.psum_tensor(f"{self.tag}_{name}", list(shape), F32))

    def sem(self, name):
        self.sems.append(self.nc.alloc_semaphore(f"{self.tag}_{name}"))
        return self.sems[-1]


class Chain:

    def __init__(self, eng, sem, per_round, pad):
        self.eng, self.sem, self.per_round, self.pad = eng, sem, per_round, pad
        self.start, self.k = 0, 0

    def link(self, ins):
        self.k += 1
        ins.then_inc(self.sem, 1)
        self.eng.wait_ge(self.sem, self.start + self.k)

    def carry(self, u):
        self.eng.memset(self.pad[:, u:u + 1], 0.0)


def wcols(w):
    return w.rearrange("(c p) n -> p c n", p=128)


def project_context(nc, io, scr):
    with ExitStack() as ctx:
        a = Arena(nc, ctx, "kv")
        ctx32 = [a.sb(f"ctx32_{u}", [128, KC, SK]) for u in range(U)]
        chi = [a.sb(f"chi{u}", [128, KC, SK], F16) for u in range(U)]
        clo = [a.sb(f"clo{u}", [128, KC, SK], F16) for u in range(U)]
        w32 = ctx32[0][:, :, 0:512]
        whi = a.sb("whi", [128, KC, 512], F16)
        wlo = a.sb("wlo", [128, KC, 512], F16)
        khi = a.sb("khi", [128, 2, SK], F16)
        klo = a.sb("klo", [128, 2, SK], F16)
        vout = [a.sb(f"vout{u}", [CH, 2, VW]) for u in range(U)]
        kps = [a.ps(f"kps{n}") for n in range(3)]
        vps = [a.ps(f"vps{n}") for n in range(4)]

        w_in, w_hi, w_lo = a.sem("w_in"), a.sem("w_hi"), a.sem("w_lo")
        ctx_in = [a.sem(f"ctx_in{u}") for u in range(U)]
        hi_done = a.sem("hi_done")
        lo_done = [a.sem(f"lo_done{u}") for u in range(U)]
        k_ps, k_hi, k_lo = a.sem("k_ps"), a.sem("k_hi"), a.sem("k_lo")
        v_ps, v_sb = [a.sem(f"v_ps{u}") for u in range(U)], a.sem("v_sb")
        k_out = a.sem("k_out")
        v_out = [a.sem(f"v_out{u}") for u in range(U)]
        ones = a.sem("ones")
        block = ctx.enter_context(nc.Block())
        NK, NV = 2 * PT, NCH

        @block.sync
        def _(sp):
            sp.dma_start(w32, wcols(io["wkv"])).then_inc(w_in, 16)
            sp.wait_ge(w_lo, KC)
            with sp.Fori(0, B // U) as i:
                for u in range(U):
                    sp.wait_ge(lo_done[u], KC * i)
                    sp.dma_start(ctx32[u][:, :, :],
                                 io["ctxT"][U * i + u].rearrange("(c p) t -> p c t", p=128)).then_inc(ctx_in[u], 16)

        @block.tensor
        def _(pe):
            pe.wait_ge(w_hi, KC)
            pe.wait_ge(w_lo, KC)
            terms = lambda u: ((whi, chi[u]), (wlo, chi[u]), (whi, clo[u]))
            with pe.Fori(0, B // U) as i:
                for u in range(U):
                    n = U * i + u
                    pe.wait_ge(lo_done[u], KC * i + KC)
                    for m in range(NK):
                        layer, part = m // PT, m % PT
                        if u or m >= 3:
                            pe.wait_ge(k_lo, NK * n + m - 2)
                        else:
                            pe.wait_ge(k_lo, NK * n)
                        for t, (w, c) in enumerate(terms(u)):
                            for k in range(KC):
                                mm = pe.matmul(kps[m % 3][:, 0:NP], w[:, k, layer * 128:layer * 128 + 128],
                                               c[:, k, part * NP:(part + 1) * NP],
                                               start=(t == 0 and k == 0), stop=(t == 2 and k == KC - 1))
                        mm.then_inc(k_ps, 1)
                    for m in range(NV):
                        if u or m >= 4:
                            pe.wait_ge(v_sb, NV * n + m - 3)
                        else:
                            pe.wait_ge(v_sb, NV * n)
                        for k in range(KC):
                            for t, (w, c) in enumerate(terms(u)):
                                mm = pe.matmul(vps[m % 4][0:CH, 0:256], c[:, k, m * CH:(m + 1) * CH],
                                               w[:, k, 256:512],
                                               start=(t == 0 and k == 0), stop=(t == 2 and k == KC - 1))
                        mm.then_inc(v_ps[u], 1)

        @block.scalar
        def _(act):
            act.wait_ge(w_in, 16)
            for k in range(KC):
                nc.scalar.activation(whi[:, k, :], w32[:, k, :], ACT.Copy, scale=WSCALE).then_inc(w_hi, 1)
            act.wait_ge(ones, U)
            with act.Fori(0, B // U) as i:
                for u in range(U):
                    n = U * i + u
                    act.wait_ge(ctx_in[u], 16 * i + 16)
                    act.wait_ge(v_ps[u], NV * i)
                    for k in range(KC):
                        nc.scalar.activation(chi[u][:, k, :], ctx32[u][:, k, :], ACT.Copy).then_inc(hi_done, 1)
                    for m in range(NK):
                        layer, part = m // PT, m % PT
                        act.wait_ge(k_ps, NK * n + m + 1)
                        if m == 0:
                            act.wait_ge(k_out, 32 * n)
                        nc.scalar.activation(khi[:, layer, part * NP:(part + 1) * NP], kps[m % 3][:, 0:NP],
                                             ACT.Copy, scale=1.0 / WSCALE).then_inc(k_hi, 1)
                    act.wait_ge(v_out[u], 32 * i)
                    for m in range(NV):
                        act.wait_ge(v_ps[u], NV * i + m + 1)
                        nc.scalar.activation(
                            vout[u][:, :, m * G * VS:(m + 1) * G * VS].rearrange("p l (g v) -> p l g v", v=VS)[:, :, :, 0:HD],
                            vps[m % 4][0:CH, 0:256].rearrange("p (l g v) -> p l g v", l=2, v=HD),
                            ACT.Copy, scale=1.0 / WSCALE).then_inc(v_sb, 1)

        @block.vector
        def _(dve):
            for u in range(U):
                nc.vector.memset(vout[u][:, :, :], 1.0).then_inc(ones, 1)
            for k in range(KC):
                dve.wait_ge(w_hi, k + 1)
                nc.vector.scalar_tensor_tensor(out=wlo[:, k, :], in0=w32[:, k, :], scalar=WSCALE,
                                               in1=whi[:, k, :], op0=ALU.mult, op1=ALU.subtract).then_inc(w_lo, 1)
            with dve.Fori(0, B // U) as i:
                for u in range(U):
                    n = U * i + u
                    for k in range(KC):
                        dve.wait_ge(hi_done, KC * n + k + 1)
                        nc.vector.tensor_tensor(clo[u][:, k, :], ctx32[u][:, k, :], chi[u][:, k, :],
                                                ALU.subtract).then_inc(lo_done[u], 1)
                    for m in range(NK):
                        layer, part = m // PT, m % PT
                        cols = slice(part * NP, (part + 1) * NP)
                        dve.wait_ge(k_hi, NK * n + m + 1)
                        nc.vector.scalar_tensor_tensor(out=klo[:, layer, cols], in0=kps[m % 3][:, 0:NP],
                                                       scalar=1.0 / WSCALE, in1=khi[:, layer, cols],
                                                       op0=ALU.mult, op1=ALU.subtract).then_inc(k_lo, 1)

        @block.gpsimd
        def _(pool):
            with pool.Fori(0, B // U) as i:
                for u in range(U):
                    n = U * i + u
                    pool.wait_ge(k_lo, NK * n + NK)
                    pool.dma_start(scr["k"][n, 0].rearrange("l p t -> p l t"), khi[:, :, :]).then_inc(k_out, 16)
                    pool.dma_start(scr["k"][n, 1].rearrange("l p t -> p l t"), klo[:, :, :]).then_inc(k_out, 16)
                    pool.wait_ge(v_sb, NV * n + NV)
                    for layer in range(2):
                        pool.dma_start(scr["v"][layer, n], vout[u][:, layer, :]).then_inc(v_out[u], 16)
            pool.wait_ge(k_out, 32 * B)
            for u in range(U):
                pool.wait_ge(v_out[u], 32 * (B // U))


class Norm:

    def __init__(self, a, eps):
        self.stats = [a.sb(f"stats{u}", [128, 6]) for u in range(U)]
        self.mv = [a.sb(f"mv{u}", [128, 2]) for u in range(U)]
        self.std = [a.sb(f"std{u}", [128, 1]) for u in range(U)]
        self.rstd = [a.sb(f"rstd{u}", [128, 1]) for u in range(U)]
        self.eps = eps
        self.var_ready, self.std_ready = a.sem("var_ready"), a.sem("std_ready")

    def statistics(self, nc, chain, u, src):
        chain.link(nc.vector.bn_stats(self.stats[u][:, :], src))
        chain.carry(u)
        nc.vector.bn_aggr(self.mv[u][:, :], self.stats[u][:, :]).then_inc(self.var_ready, 1)

    def root(self, nc, act, u, count):
        act.wait_ge(self.var_ready, count)
        nc.scalar.activation(self.std[u][:, :], self.mv[u][:, 1:2], ACT.Sqrt, bias=self.eps[:, 0:1]).then_inc(self.std_ready, 1)

    def apply(self, nc, dve, chain, u, dst, src, count):
        dve.wait_ge(self.std_ready, count)
        chain.link(nc.vector.reciprocal(self.rstd[u][:, :], self.std[u][:, :]))
        return nc.vector.tensor_scalar(dst, src, self.mv[u][:, 0:1], self.rstd[u][:, 0:1],
                                       ALU.subtract, ALU.mult)


def self_attention(nc, io, scr, layer, x_src):
    with ExitStack() as ctx:
        a = Arena(nc, ctx, f"sa{layer}")
        L0 = layer == 0
        NQ = D if L0 else 2 * D
        NKC = D if L0 else 2 * 128
        NVC = D if L0 else 128
        KT = 4 if L0 else 1
        wq = a.sb("wq", [128, KC, NQ])
        wk = a.sb("wk", [128, KC, NKC])
        wv = a.sb("wv", [128, KC, NVC])
        wo = a.sb("wo", [128, KC, D])
        wxq = a.sb("wxq", [128, KC, D])
        ident = a.sb("ident", [128, 128])
        blockmask = a.sb("blockmask", [128, 8, SP_])
        causal = a.sb("causal", [128, SP_])
        eps = a.sb("eps", [128, 1])
        loads = [(wq[:, :, :], wcols(io[f"sa{layer}_wq"])), (wk[:, :, :], wcols(io[f"sa{layer}_wk"])),
                 (wv[:, :, :], wcols(io[f"sa{layer}_wv"])), (wo[:, :, :], wcols(io[f"sa{layer}_wo"])),
                 (wxq[:, :, :], wcols(io[f"xa{layer}_wq"])), (ident[:, :], io["ident"]),
                 (blockmask[:, :, :], io["blockmask"].rearrange("p (h k) -> p h k", h=8)),
                 (causal[:, :], io["causal"])]
        if L0:
            bq, bk = a.sb("bq", [128, 4]), a.sb("bk", [128, 4])
            bv, bo = a.sb("bv", [1, D]), a.sb("bo", [1, D])
            ones = a.sb("ones", [1, 128])
            loads += [(bq[:, :], io["sa0_bq"]),
                      (bk[:, :], io["sa0_bk"]),
                      (bv[:, :], io["sa0_bv"].rearrange("(a n) -> a n", a=1)),
                      (bo[:, :], io["sa0_bo"].rearrange("(a n) -> a n", a=1))]
        else:
            rope = a.sb("rope", [128, 4, SP_])
            mask_u8 = a.sb("mask_u8", [S, SK], U8)
            mask32 = a.sb("mask32", [S, SK])
            maxkeep = a.sb("maxkeep", [S, 1])
            keepq = a.sb("keepq", [S, 128])
            keep_bc = a.sb("keep_bc", [128, SP_])
            rot = [a.sb(f"rot{u}", [128, 512]) for u in range(U)]
            loads += [(rope[:, :, :], io["rope"].rearrange("p (a q) -> p a q", a=4)),
                      (mask_u8[:, :], io["mask"])]

        def two(name, shape, dt=F32):
            return [a.sb(f"{name}{u}", shape, dt) for u in range(U)]

        x = two("x", [128, D])
        xT = two("xT", [128, KC, 128])
        qT = two("qT", [128, 4, 128])
        kT = two("kT", [128, KT, 128])
        kbd = two("kbd", [128, KT, 2, 8, SP_])
        hp = 16 if L0 else 4
        vbd = two("vbd", [128, 2, hp, 2, HD])
        sc = two("sc", [128, 4, 8, SP_])
        mx = two("mx", [128, 4, 8])
        sm = two("sm", [128, 4, 8])
        rs = two("rs", [128, 4, 8])
        pT = two("pT", [128, 4, 512])
        att = two("att", [128, 512])
        attT = two("attT", [128, KC, 128])
        y = two("y", [128, D])
        x1 = two("x1", [128, D])
        q32 = two("q32", [128, 512])
        qhi, qlo = two("qhi", [128, 512], F16), two("qlo", [128, 512], F16)
        bank = [[a.ps(f"bank{u}_{n}") for n in range(4)] for u in range(U)]

        w_in, setup = a.sem("w_in"), a.sem("setup")
        x_in = [a.sem(f"x_in{u}") for u in range(U)]
        names = ["xT_ps", "xT_sb", "qk_ps", "q_sb", "k_sb", "v_ps", "v_sb", "kbd_sb", "s_ps", "s_sub",
                 "s_add", "p_sb", "pT_ps", "pT_sb", "att_ps", "att_sb", "attT_ps", "attT_sb", "y_ps", "y_sb",
                 "x1_sb", "x1T_ps", "x1T_sb", "xq_ps", "q32_sb", "qhi_sb", "qlo_sb", "chain_dve", "chain_pool",
                 "keep_ps"]
        s = {n: a.sem(n) for n in names}
        x_out = [a.sem(f"x_out{u}") for u in range(U)]
        norm = Norm(a, eps)
        pad = a.sb("pad", [1, U])
        block = ctx.enter_context(nc.Block())
        SETUP = 3 if L0 else 6

        @block.sync
        def _(sp):
            for dst, src in loads:
                sp.dma_start(dst, src).then_inc(w_in, 16)
            with sp.Fori(0, TILES // U) as i:
                for u in range(U):
                    sp.wait_ge(x_out[u], 80 * i)
                    sp.dma_start(x[u][:, :], x_src[U * i + u]).then_inc(x_in[u], 16)
                for u in range(U):
                    n = U * i + u
                    sp.wait_ge(s["x1_sb"], n + 1)
                    sp.dma_start(scr["x"][n], x1[u][:, :]).then_inc(x_out[u], 16)
                    for part, (sem_, q) in enumerate(((s["qhi_sb"], qhi), (s["qlo_sb"], qlo))):
                        sp.wait_ge(sem_, n + 1)
                        for b in range(2):
                            sp.dma_start(scr["q"][part, U * U * i + 2 * u + b],
                                         q[u][:, :].rearrange("p (j b q) -> p j b q", b=2, j=4)[:, :, b, 0:S]
                                         ).then_inc(x_out[u], 16)
            for u in range(U):
                sp.wait_ge(x_out[u], 80 * (TILES // U))

        @block.tensor
        def _(pe):
            pe.wait_ge(w_in, 16 * len(loads))
            if not L0:
                pe.wait_ge(s["setup"] if "setup" in s else setup, 5)
                pe.matmul(bank[0][0][:, 0:S], keepq[:, :], ident[0:S, 0:S], start=True, stop=True).then_inc(s["keep_ps"], 1)
                pe.wait_ge(setup, SETUP)

            def transposed(u, n, src, dst, ready, done, done_of):
                pe.wait_ge(ready, n + 1)
                for k in range(KC):
                    mm = pe.transpose(dst[:, k * 128:(k + 1) * 128], src[:, k * 128:(k + 1) * 128], ident[:, :])
                mm.then_inc(done, 1)

            with pe.Fori(0, TILES // U) as i:
                for u in range(U):
                    pe.wait_ge(x_in[u], 16 * i + 16)
                    for k in range(KC):
                        mm = pe.transpose(bank[u][0][:, k * 128:(k + 1) * 128], x[u][:, k * 128:(k + 1) * 128], ident[:, :])
                    mm.then_inc(s["xT_ps"], 1)
                for u in range(U):
                    n = U * i + u
                    pe.wait_ge(s["xT_sb"], n + 1)
                    jobs = [(bank[u][1], wq, 4, 0), (bank[u][2], wk, 4, 0)] if L0 else \
                           [(bank[u][1], wq, 4, 0), (bank[u][2], wq, 4, 4), (bank[u][3], wk, 2, 0)]
                    for dst, w, tiles, first in jobs:
                        for t in range(tiles):
                            for k in range(KC):
                                mm = pe.matmul(dst[:, t * 128:(t + 1) * 128], w[:, k, (first + t) * 128:(first + t + 1) * 128],
                                               xT[u][:, k, :], start=(k == 0), stop=(k == KC - 1))
                    mm.then_inc(s["qk_ps"], 1)
                    for b in range(2):
                        out = bank[u][3 if b == 0 else 0][:, 0:D] if L0 else bank[u][0][:, b * 128:(b + 1) * 128]
                        for k in range(KC):
                            for half in range(2):
                                mm = pe.matmul(out[half * SP_:(half + 1) * SP_, :], xT[u][:, k, b * SP_:(b + 1) * SP_],
                                               wv[:, k, :], start=(k == 0), stop=(k == KC - 1 and not L0))
                        if L0:
                            for half in range(2):
                                mm = pe.matmul(out[half * SP_:(half + 1) * SP_, :], ones[0:1, 0:SP_], bv[0:1, :],
                                               start=False, stop=True)
                    mm.then_inc(s["v_ps"], 1)
                for t in range(4):
                    for u in range(U):
                        n = U * i + u
                        if t == 0:
                            pe.wait_ge(s["q_sb"], n + 1)
                            pe.wait_ge(s["k_sb"], n + 1)
                        pe.wait_ge(s["kbd_sb"], KT * U * i + (U * min(t, KT - 1) + u) + 1)
                        if t >= 2:
                            pe.wait_ge(s["s_add"], 4 * U * i + U * (t - 2) + u + 1)
                        for b in range(2):
                            mm = pe.matmul(bank[u][1 + t % 2][b * SP_:(b + 1) * SP_, :], qT[u][:, t, b * SP_:(b + 1) * SP_],
                                           kbd[u][:, min(t, KT - 1), b, :, :], start=True, stop=True)
                        mm.then_inc(s["s_ps"], 1)
                for t in range(4):
                    for u in range(U):
                        n = U * i + u
                        pe.wait_ge(s["p_sb"], 4 * U * i + U * t + u + 1)
                        if t == 0:
                            pe.wait_ge(s["v_sb"], n + 1)
                        if t >= 2:
                            pe.wait_ge(s["pT_sb"], 4 * U * i + U * (t - 2) + u + 1)
                        for k in range(4):
                            mm = pe.transpose(bank[u][3 if t % 2 == 0 else 0][:, k * 128:(k + 1) * 128],
                                              sc[u][:, t, 2 * k:2 * k + 2, :], ident[:, :])
                        mm.then_inc(s["pT_ps"], 1)
                for u in range(U):
                    n = U * i + u
                    pe.wait_ge(s["s_add"], 4 * U * i + 4 * U)
                    for t in range(4):
                        pe.wait_ge(s["pT_sb"], 4 * U * i + U * t + u + 1)
                        for k in range(4):
                            for b in range(2):
                                c = t * 128 + k * 32
                                mm = pe.matmul(bank[u][1][b * SP_:(b + 1) * SP_, c:c + 32],
                                               pT[u][:, t, k * 128 + b * SP_:k * 128 + (b + 1) * SP_],
                                               vbd[u][:, b, t * 4 + k if L0 else k, :, :], start=True, stop=True)
                    mm.then_inc(s["att_ps"], 1)
                for u in range(U):
                    transposed(u, U * i + u, att[u], bank[u][2], s["att_sb"], s["attT_ps"], None)
                for u in range(U):
                    n = U * i + u
                    pe.wait_ge(s["attT_sb"], n + 1)
                    for k in range(KC):
                        mm = pe.matmul(bank[u][3][:, :], attT[u][:, k, :], wo[:, k, :], start=(k == 0), stop=(k == KC - 1 and not L0))
                    if L0:
                        mm = pe.matmul(bank[u][3][:, :], ones[0:1, :], bo[0:1, :], start=False, stop=True)
                    mm.then_inc(s["y_ps"], 1)
                for u in range(U):
                    transposed(u, U * i + u, x1[u], bank[u][0], s["x1_sb"], s["x1T_ps"], None)
                for u in range(U):
                    n = U * i + u
                    pe.wait_ge(s["x1T_sb"], n + 1)
                    for t in range(4):
                        for k in range(KC):
                            mm = pe.matmul(bank[u][1][:, t * 128:(t + 1) * 128], wxq[:, k, t * 128:(t + 1) * 128],
                                           xT[u][:, k, :], start=(k == 0), stop=(k == KC - 1))
                    mm.then_inc(s["xq_ps"], 1)

        @block.vector
        def _(dve):
            dve.wait_ge(w_in, 16 * len(loads))
            for u in range(U):
                nc.vector.memset(vbd[u][:, :, :, :, :], 0.0).then_inc(setup, 1)
            if L0:
                nc.vector.memset(ones[:, :], 1.0).then_inc(setup, 1)
            else:
                nc.vector.tensor_copy(mask32[:, :], mask_u8[:, :]).then_inc(setup, 1)
                dve.wait_ge(setup, 3)
                nc.vector.reduce_max(maxkeep[:, :], mask32[:, :], AX.X).then_inc(setup, 1)
                dve.wait_ge(setup, 4)
                nc.vector.tensor_copy(keepq[:, :], maxkeep[:, 0:1].to_broadcast([S, 128])).then_inc(setup, 1)
                dve.wait_ge(s["keep_ps"], 1)
                nc.vector.tensor_copy(keep_bc[:, 0:S], bank[0][0][:, 0:S]).then_inc(setup, 1)
            nc.vector.memset(eps[:, :], 1e-5).then_inc(s["chain_dve"], 1)
            if not L0:
                nc.vector.memset(keep_bc[:, S:SP_], 1.0).then_inc(setup, 1)
            chain = Chain(dve, s["chain_dve"], U * ((0 if L0 else 5) + 4 * 2 + 1 + 2), pad)
            with dve.Fori(0, TILES // U) as i:
                chain.k = 0
                chain.start = chain.per_round * i + 1
                for u in range(U):
                    dve.wait_ge(s["xT_ps"], U * i + u + 1)
                    nc.vector.tensor_copy(xT[u][:, :, :], bank[u][0][:, :].rearrange("p (c t) -> p c t", c=KC)).then_inc(s["xT_sb"], 1)
                for u in range(U):
                    n = U * i + u
                    dve.wait_ge(s["qk_ps"], n + 1)
                    if L0:
                        for t in range(4):
                            last = nc.vector.tensor_scalar(qT[u][:, t, :], bank[u][1][:, t * 128:(t + 1) * 128],
                                                           bq[:, t:t + 1], 0.25, ALU.add, ALU.mult)
                        last.then_inc(s["q_sb"], 1)
                    else:
                        def tab(r, reps):
                            return rope[:, r, :].unsqueeze(1).to_broadcast([128, reps, SP_])
                        def by(ap):
                            return ap.rearrange("p (r q) -> p r q", q=SP_)
                        chain.link(nc.vector.tensor_tensor(by(rot[u][:, :]), by(bank[u][2][:, :]), tab(1, 8), ALU.mult))
                        chain.link(nc.vector.tensor_tensor(by(qT[u][:, :, :].rearrange("p a b -> p (a b)")), by(bank[u][1][:, :]), tab(0, 8), ALU.mult))
                        nc.vector.tensor_tensor(qT[u][:, :, :].rearrange("p a b -> p (a b)"), qT[u][:, :, :].rearrange("p a b -> p (a b)"),
                                                rot[u][:, :], ALU.add).then_inc(s["q_sb"], 1)
                        dve.wait_ge(s["q_sb"], n + 1)
                        chain.link(nc.vector.tensor_tensor(by(rot[u][:, 0:128]), by(bank[u][3][:, 128:256]), tab(3, 2), ALU.mult))
                        chain.link(nc.vector.tensor_tensor(by(kT[u][:, 0, :]), by(bank[u][3][:, 0:128]), tab(2, 2), ALU.mult))
                        nc.vector.tensor_tensor(kT[u][:, 0, :], kT[u][:, 0, :], rot[u][:, 0:128], ALU.add).then_inc(s["k_sb"], 1)
                for t in range(4):
                    for u in range(U):
                        dve.wait_ge(s["s_ps"], 4 * U * i + U * t + u + 1)
                        nc.vector.tensor_tensor(sc[u][:, t, :, :], bank[u][1 + t % 2][:, :].rearrange("p (h k) -> p h k", h=8),
                                                causal[:, :].unsqueeze(1).to_broadcast([128, 8, SP_]), ALU.add).then_inc(s["s_add"], 1)
                        dve.wait_ge(s["s_add"], 4 * U * i + U * t + u + 1)
                        chain.link(nc.vector.tensor_reduce(mx[u][:, t, :], sc[u][:, t, :, :], AX.X, ALU.max))
                        nc.vector.tensor_tensor(sc[u][:, t, :, :], sc[u][:, t, :, :],
                                                mx[u][:, t, :].unsqueeze(2).to_broadcast([128, 8, SP_]),
                                                ALU.subtract).then_inc(s["s_sub"], 1)
                for t in range(4):
                    for u in range(U):
                        dve.wait_ge(s["p_sb"], 4 * U * i + U * t + u + 1)
                        chain.link(nc.vector.tensor_reduce(sm[u][:, t, :], sc[u][:, t, :, :], AX.X, ALU.add))
                for u in range(U):
                    n = U * i + u
                    chain.link(nc.vector.reciprocal(rs[u][:, :, :], sm[u][:, :, :]))
                    dve.wait_ge(s["att_ps"], n + 1)
                    nc.vector.tensor_tensor(att[u][:, :].rearrange("p (h d) -> p h d", d=HD),
                                            bank[u][1][:, :].rearrange("p (h d) -> p h d", d=HD),
                                            rs[u][:, :, :].rearrange("p t h -> p (t h)").unsqueeze(2).to_broadcast([128, 32, HD]),
                                            ALU.mult).then_inc(s["att_sb"], 1)
                for u in range(U):
                    n = U * i + u
                    dve.wait_ge(s["y_ps"], n + 1)
                    nc.vector.tensor_tensor(y[u][:, :], bank[u][3][:, :], x[u][:, :], ALU.add).then_inc(s["y_sb"], 1)
                    dve.wait_ge(s["y_sb"], n + 1)
                    norm.statistics(nc, chain, u, y[u][:, :])
                for u in range(U):
                    n = U * i + u
                    norm.apply(nc, dve, chain, u, x1[u][:, :], y[u][:, :], n + 1).then_inc(s["x1_sb"], 1)
                for u in range(U):
                    n = U * i + u
                    dve.wait_ge(s["x1T_ps"], n + 1)
                    nc.vector.tensor_copy(xT[u][:, :, :], bank[u][0][:, :].rearrange("p (c t) -> p c t", c=KC)).then_inc(s["x1T_sb"], 1)
                for u in range(U):
                    n = U * i + u
                    dve.wait_ge(s["xq_ps"], n + 1)
                    if L0:
                        nc.vector.tensor_scalar(q32[u][:, :], bank[u][1][:, :], 0.25, None, ALU.mult).then_inc(s["q32_sb"], 1)
                    else:
                        chain.link(nc.vector.tensor_tensor(q32[u][:, :].rearrange("p (r q) -> p r q", q=SP_),
                                                           bank[u][1][:, :].rearrange("p (r q) -> p r q", q=SP_),
                                                           keep_bc[:, :].unsqueeze(1).to_broadcast([128, 8, SP_]), ALU.mult))
                        nc.vector.tensor_scalar(q32[u][:, :], q32[u][:, :], 0.25, None, ALU.mult).then_inc(s["q32_sb"], 1)
                for u in range(U):
                    n = U * i + u
                    dve.wait_ge(s["qhi_sb"], n + 1)
                    nc.vector.tensor_tensor(qlo[u][:, :], q32[u][:, :], qhi[u][:, :], ALU.subtract).then_inc(s["qlo_sb"], 1)
                assert chain.k == chain.per_round, (chain.k, chain.per_round)

        @block.scalar
        def _(act):
            act.wait_ge(w_in, 16 * len(loads))
            act.wait_ge(setup, U)
            act.wait_ge(s["chain_dve"], 1)
            with act.Fori(0, TILES // U) as i:
                for u in range(U):
                    n = U * i + u
                    if L0:
                        act.wait_ge(s["qk_ps"], n + 1)
                        for t in range(4):
                            last = nc.scalar.activation(kT[u][:, t, :], bank[u][2][:, t * 128:(t + 1) * 128],
                                                        ACT.Identity, bias=bk[:, t:t + 1])
                        last.then_inc(s["k_sb"], 1)
                    act.wait_ge(s["v_ps"], n + 1)
                    for b in range(2):
                        src = bank[u][3 if b == 0 else 0][:, 0:D] if L0 else bank[u][0][:, b * 128:(b + 1) * 128]
                        for half in range(2):
                            rows = slice(64 * half, 64 * half + 64)
                            last = nc.scalar.activation(vbd[u][rows, b, :, half, :],
                                                        src[rows, :].rearrange("p (m s d) -> p m s d", s=2, d=HD)[:, :, half, :],
                                                        ACT.Copy)
                    last.then_inc(s["v_sb"], 1)
                for t in range(4):
                    for u in range(U):
                        act.wait_ge(s["s_sub"], 4 * U * i + U * t + u + 1)
                        nc.scalar.activation(sc[u][:, t, :, :], sc[u][:, t, :, :], ACT.Exp).then_inc(s["p_sb"], 1)
                for t in range(4):
                    for u in range(U):
                        act.wait_ge(s["pT_ps"], 4 * U * i + U * t + u + 1)
                        nc.scalar.activation(pT[u][:, t, :], bank[u][3 if t % 2 == 0 else 0][:, :], ACT.Copy).then_inc(s["pT_sb"], 1)
                for u in range(U):
                    n = U * i + u
                    act.wait_ge(s["attT_ps"], n + 1)
                    nc.scalar.activation(attT[u][:, :, :], bank[u][2][:, :].rearrange("p (c t) -> p c t", c=KC), ACT.Copy).then_inc(s["attT_sb"], 1)
                for u in range(U):
                    norm.root(nc, act, u, U * i + u + 1)
                for u in range(U):
                    n = U * i + u
                    act.wait_ge(s["q32_sb"], n + 1)
                    nc.scalar.activation(qhi[u][:, :], q32[u][:, :], ACT.Copy).then_inc(s["qhi_sb"], 1)

        @block.gpsimd
        def _(pool):
            pool.wait_ge(w_in, 16 * len(loads))
            with pool.Fori(0, TILES // U) as i:
                for t in range(KT):
                    for u in range(U):
                        n = U * i + u
                        pool.wait_ge(s["k_sb"], n + 1)
                        for b in range(2):
                            last = nc.gpsimd.tensor_tensor(
                                kbd[u][:, t, b, :, :], kT[u][:, t, b * SP_:(b + 1) * SP_].unsqueeze(1).to_broadcast([128, 8, SP_]),
                                blockmask[:, :, :], ALU.mult)
                        last.then_inc(s["kbd_sb"], 1)


def cross_attention(nc, io, scr, layer):
    NU = 2 * 2 * NCH
    with ExitStack() as ctx:
        a = Arena(nc, ctx, f"xa{layer}")
        masked = layer == 1
        KR = 98
        kst = [a.sb(f"kst{u}", [KR, 4, SK], F16) for u in range(U)]
        qst = [a.sb(f"qst{u}", [KR, 4, QP], F16) for u in range(U)]
        v = [a.sb(f"v{u}", [CH, VW]) for u in range(U)]
        PR, SR, MR = 6, 3, 2
        p = a.sb("p", [CH, PR, QP])
        mxp = [a.sb(f"mxp{h}", [112, 8, PT]) for h in range(2)]
        mneg = [a.sb(f"mneg{h}", [112, 8]) for h in range(2)]
        mhi = [a.sb(f"mhi{h}", [8, 112], F16) for h in range(2)]
        mlo = [a.sb(f"mlo{h}", [8, 112], F16) for h in range(2)]
        osb = [a.sb(f"osb{h}", [128, QG]) for h in range(2)]
        rden = [a.sb(f"rden{h}", [112, 2, 4, 1]) for h in range(2)]
        att = [a.sb(f"att{h}", [112, 2, 4, HD]) for h in range(2)]
        ident = a.sb("ident", [128, 128])
        if masked:
            mask_u8 = a.sb("mask_u8", [112, SK], U8)
            madd = a.sb("madd", [112, SK])
            mtmp = [a.sb(f"mtmp{n}", [112, NP]) for n in range(MR)]
            maxkeep = a.sb("maxkeep", [112, 1])
            pad = a.sb("pad", [1, 2 * MR])
            madd16 = a.sb("madd16", [S, SK], BF16)
            qsel = a.sb("qsel", [S, QP], BF16)
        sps = [a.ps(f"sps{n}") for n in range(SR)]
        mps = [a.ps(f"mps{n}") for n in range(MR)]
        ops = [a.ps(f"ops{h}") for h in range(2)]
        tps = a.ps("tps")

        c_in, cleared, setup = a.sem("c_in"), a.sem("cleared"), a.sem("setup")
        k_in = [[a.sem(f"k_in{u}_{h}") for h in range(2)] for u in range(U)]
        v_in = [a.sem(f"v_in{u}") for u in range(U)]
        m_in = [[a.sem(f"m_in{u}_{h}") for h in range(2)] for u in range(U)]
        s_ps, p_sb, pv = a.sem("s_ps"), a.sem("p_sb"), a.sem("pv")
        m_ps, m_red, mneg_sb, mT_ps, mhi_sb, mlo_sb = (a.sem(n) for n in ("m_ps", "m_red", "mneg_sb", "mT_ps", "mhi_sb", "mlo_sb"))
        o_sb, oT_ps, rden_sb, att_sb = (a.sem(n) for n in ("o_sb", "oT_ps", "rden_sb", "att_sb"))
        att_out = [a.sem(f"att_out{h}") for h in range(2)]
        block = ctx.enter_context(nc.Block())
        KQ_DMAS = 3 + 6

        def load_kq(sp, n, i, u, h):
            prs = slice(2 * h, 2 * h + 2)
            for r, part in enumerate((0, 0, 1)):
                sp.dma_start(kst[u][32 * r:32 * r + 32, prs, :],
                             scr["k"][n, part, layer].rearrange("(a r) t -> r a t", r=32)[:, prs, :]
                             ).then_inc(k_in[u][h], 16)
            for r, part in enumerate((0, 1, 0)):
                for g in range(2):
                    sp.dma_start(qst[u][32 * r + 16 * g:32 * r + 16 * g + 16, prs, g * QG:(g + 1) * QG],
                                 scr["q"][part, n].rearrange("(a g r) c -> g r a c", g=2, r=HD)[g, :, prs, :]
                                 ).then_inc(k_in[u][h], 16)

        def held(eng, value):
            return value if isinstance(value, int) else eng.snap(value)

        def windows(eng, one):
            for u in range(U):
                one(u, 0, u, True, False)
            with eng.Fori(1, B // U - 1) as i:
                for u in range(U):
                    one(U * i + u, i, u, False, False)
            for u in range(U):
                one(B - U + u, B // U - 1, u, False, u == U - 1)

        @block.sync
        def _(sp):
            sp.dma_start(ident[:, :], io["ident"]).then_inc(c_in, 16)
            if masked:
                for r in range(2):
                    sp.dma_start(mask_u8[r * S:(r + 1) * S, :], io["mask"]).then_inc(c_in, 16)
            sp.wait_ge(cleared, 4)
            for u in range(U):
                for h in range(2):
                    load_kq(sp, u, 0, u, h)
                sp.dma_start(v[u][:, :], scr["v"][layer, u]).then_inc(v_in[u], 16)

            def maximum_out(wb, ub, h):
                for row, (ready, m) in enumerate(((mhi_sb, mhi), (mlo_sb, mlo))):
                    sp.wait_ge(ready, 2 * wb + h + 1)
                    sp.dma_start(qst[ub][96 + row:97 + row, 2 * h:2 * h + 2, :].rearrange("o a (t c) -> o (a t) c", c=112),
                                 m[h][:, :]).then_inc(m_in[ub][h], 16)

            def attention_out(w, h):
                sp.wait_ge(att_sb, 2 * w + h + 1)
                for j2 in range(2):
                    sp.dma_start(scr["att"][w, :, j2 * 256 + h * 128:j2 * 256 + (h + 1) * 128],
                                 att[h][j2 * S:(j2 + 1) * S, :, :, :].rearrange("p a b c -> p (a b c)")).then_inc(att_out[h], 16)

            def window(w, i, u, first, last):
                more = not (isinstance(w, int) and w >= B - U)
                maximum_out(w, u, 1)
                if not (first and u == 0):
                    attention_out(w - 1, 1)
                if more:
                    sp.wait_ge(s_ps, NU * w + NU // 2)
                    load_kq(sp, w + 2, i + 1, u, 0)
                if not last:
                    maximum_out(w + 1, 1 - u, 0)
                attention_out(w, 0)
                if more:
                    sp.wait_ge(s_ps, NU * w + NU)
                    load_kq(sp, w + 2, i + 1, u, 1)
                    sp.wait_ge(pv, 2 * NCH * (w + 1))
                    sp.dma_start(v[u][:, :], scr["v"][layer, w + 2]).then_inc(v_in[u], 16)

            maximum_out(0, 0, 0)
            windows(sp, window)
            attention_out(B - 1, 1)
            for h in range(2):
                sp.wait_ge(att_out[h], 32 * B)

        @block.tensor
        def _(pe):
            pe.wait_ge(c_in, 48 if masked else 16)
            if masked:
                pe.wait_ge(setup, 5)

            def maximum_unit(wb, m0, ib, ub, n):
                t, part = n // PT, n % PT
                h = t // 8
                if n % (8 * PT) == 0:
                    pe.wait_ge(k_in[ub][h], 16 * KQ_DMAS * (ib + 1))
                if not (isinstance(wb, int) and wb == 0 and n < MR):
                    pe.wait_ge(m_red, m0 + n + 1 - MR)
                tt = t % 8
                pr = 2 * h + tt // 4
                c = (tt % 4) * 112
                pe.matmul(mps[n % MR][0:112, 0:NP], qst[ub][0:96, pr, c:c + 112],
                          kst[ub][0:96, pr, part * NP:(part + 1) * NP], start=True, stop=True).then_inc(m_ps, 1)

            def maxima_transposed(wb, h):
                pe.wait_ge(mneg_sb, 2 * wb + h + 1)
                if not isinstance(wb, int) or 2 * wb + h > 2:
                    pe.wait_ge(att_sb, 2 * wb + h - 2)
                elif 2 * wb + h > 0:
                    pe.wait_ge(mlo_sb, 2 * wb + h)
                pe.transpose(tps[0:8, 0:112], mneg[h][:, :], ident[0:112, 0:112]).then_inc(mT_ps, 1)

            def output_transposed(w, h, after_output=False):
                pe.wait_ge(o_sb, 2 * w + h + 1)
                if after_output:
                    pe.wait_ge(att_sb, 2 * w + h)
                else:
                    pe.wait_ge(mlo_sb, 2 * w + h + 3)
                for jh in range(2):
                    mm = pe.transpose(tps[0:112, jh * 128:(jh + 1) * 128], osb[h][:, jh * 112:(jh + 1) * 112], ident[:, :])
                mm.then_inc(oT_ps, 1)

            def pv_step(w, p0, i, u, cs):
                h, k = cs // NCH, cs % NCH
                if k == 0:
                    if h == 0:
                        pe.wait_ge(v_in[u], 16 * (i + 1))
                    if not (isinstance(w, int) and w == 0):
                        pe.wait_ge(o_sb, 2 * w + h - 1)
                pe.wait_ge(p_sb, p0 + 2 * cs + 2)
                for c in range(4):
                    unit = 2 * cs + c // 2
                    g = 4 * h + c
                    mm = pe.matmul(ops[h][32 * c:32 * c + 32, 0:QG],
                                   v[u][:, (k * G + g) * VS:(k * G + g) * VS + 32],
                                   p[:, unit % PR, (c % 2) * QG:(c % 2 + 1) * QG],
                                   start=(k == 0), stop=(k == NCH - 1))
                mm.then_inc(pv, 1)

            def window(w, i, u, first, last):
                s0, m0, p0 = held(pe, NU * w), held(pe, NU * w + NU), held(pe, NU * w)
                for cs in range(2 * NCH):
                    h, k = cs // NCH, cs % NCH
                    if k == 0:
                        pe.wait_ge(m_in[u][h], 32 * (i + 1))
                    for pr in range(2):
                        n = 2 * cs + pr
                        if not (first and u == 0 and n < SR):
                            pe.wait_ge(p_sb, s0 + n + 1 - SR)
                        ch = slice(k * CH, (k + 1) * CH)
                        mm = pe.matmul(sps[n % SR][0:CH, 0:QP], kst[u][:, 2 * h + pr, ch], qst[u][:, 2 * h + pr, :],
                                       start=True, stop=not masked)
                        if masked:
                            mm = pe.matmul(sps[n % SR][0:CH, 0:QP], madd16[:, ch], qsel[:, :], start=False, stop=True)
                        mm.then_inc(s_ps, 1)
                        if not last:
                            maximum_unit(w + 1, m0, i if u == 0 else i + 1, 1 - u, n)
                    if cs > 0:
                        pv_step(w, p0, i, u, cs - 1)
                    elif not (first and u == 0):
                        pv_step(w - 1, p0 - NU, i - (1 - u), 1 - u, 2 * NCH - 1)
                    if cs == 2:
                        maxima_transposed(w, 1)
                    if cs == 4 and not (first and u == 0):
                        output_transposed(w - 1, 1)
                    if cs == 14 and not last:
                        maxima_transposed(w + 1, 0)
                    if cs == 16:
                        output_transposed(w, 0, after_output=last)

            for n in range(NU):
                maximum_unit(0, 0, 0, 0, n)
                if n == 30:
                    maxima_transposed(0, 0)
            windows(pe, window)
            pv_step(B - 1, NU * (B - 1), B // U - 1, U - 1, 2 * NCH - 1)
            output_transposed(B - 1, 1, after_output=True)

        @block.scalar
        def _(act):
            def output_copy(w, h):
                act.wait_ge(pv, 2 * NCH * w + NCH * (h + 1))
                if not (isinstance(w, int) and w == 0):
                    act.wait_ge(oT_ps, 2 * w + h - 1)
                nc.scalar.activation(osb[h][:, :], ops[h][:, 0:QG], ACT.Copy).then_inc(o_sb, 1)

            def window(w, i, u, first, last):
                s0, v0 = held(act, NU * w), held(act, 2 * NCH * w)
                for n in range(NU):
                    act.wait_ge(s_ps, s0 + n + 1)
                    if not (first and u == 0 and n < PR):
                        act.wait_ge(pv, v0 + (n - PR) // 2 + 1)
                    nc.scalar.activation(p[:, n % PR, :], sps[n % SR][0:CH, 0:QP], ACT.Exp).then_inc(p_sb, 1)
                    if n == 3 and not (first and u == 0):
                        output_copy(w - 1, 1)
                    if n == 2 * NCH + 3:
                        output_copy(w, 0)

            windows(act, window)
            output_copy(B - 1, 1)

        @block.vector
        def _(dve):
            for u in range(U):
                nc.vector.memset(kst[u][96:98, :, :], WSCALE).then_inc(cleared, 1)
                nc.vector.memset(qst[u][:, :, :], 0.0).then_inc(cleared, 1)
            dve.wait_ge(c_in, 48 if masked else 16)
            if masked:
                nc.vector.tensor_copy(madd[:, :], mask_u8[:, :]).then_inc(setup, 1)
                dve.wait_ge(setup, 1)
                nc.vector.reduce_max(maxkeep[:, :], madd[:, :], AX.X).then_inc(setup, 1)
                dve.wait_ge(setup, 2)
                nc.vector.tensor_scalar(madd[:, :], madd[:, :], maxkeep[:, 0:1], -NEG, ALU.subtract, ALU.mult).then_inc(setup, 1)
                dve.wait_ge(setup, 3)
                nc.vector.tensor_copy(madd16[:, :], madd[0:S, :]).then_inc(setup, 1)
                nc.vector.tensor_copy(qsel[:, :].rearrange("p (h q) -> p h q", q=S),
                                      ident[0:S, 0:S].unsqueeze(1).to_broadcast([S, 2 * J, S])).then_inc(setup, 1)

            def maximum(wb, m0, r0, n):
                t, part = n // PT, n % PT
                h, tt = t // 8, t % 8
                dve.wait_ge(m_ps, m0 + n + 1)
                dst = mxp[h][:, tt, part:part + 1]
                src = mps[n % MR][0:112, 0:NP]
                if masked:
                    nc.vector.memset(pad[:, n % MR:n % MR + 1], 0.0)
                    if not (isinstance(wb, int) and wb == 0 and n < MR):
                        dve.wait_ge(m_red, r0 + n + 1 - MR)
                    nc.vector.memset(pad[:, n % MR + MR:n % MR + MR + 1], 0.0)
                    nc.vector.tensor_tensor_reduce(out=mtmp[n % MR][:, :], in0=src, in1=madd[:, part * NP:(part + 1) * NP],
                                                   scale=1.0, scalar=2 * NEG, op0=ALU.add, op1=ALU.max,
                                                   accum_out=dst).then_inc(m_red, 1)
                else:
                    nc.vector.tensor_reduce(dst, src, AX.X, ALU.max).then_inc(m_red, 1)
                if n % (8 * PT) == 8 * PT - 1:
                    dve.wait_ge(m_red, r0 + n + 1)
                    if not (isinstance(wb, int) and wb == 0):
                        dve.wait_ge(mT_ps, 2 * wb + h - 1)
                    nc.vector.tensor_reduce(mneg[h][:, :], mxp[h][:, :, :], AX.X, ALU.max, negate=True).then_inc(mneg_sb, 1)

            def maximum_rows(wb, ib, ub, h):
                dve.wait_ge(mT_ps, 2 * wb + h + 1)
                if not (isinstance(wb, int) and wb == 0):
                    dve.wait_ge(m_in[1 - ub][h], 32 * (ib + ub))
                nc.vector.tensor_scalar(mhi[h][:, :], tps[0:8, 0:112], 1.0 / WSCALE, None, ALU.mult).then_inc(mhi_sb, 1)
                dve.wait_ge(mhi_sb, 2 * wb + h + 1)
                nc.vector.scalar_tensor_tensor(out=mlo[h][:, :], in0=tps[0:8, 0:112], scalar=1.0 / WSCALE, in1=mhi[h][:, :],
                                               op0=ALU.mult, op1=ALU.subtract).then_inc(mlo_sb, 1)

            def output_scaled(w, i, h):
                o = tps[0:112, 0:256].rearrange("p (j c v) -> p j c v", j=2, c=4)
                dve.wait_ge(oT_ps, 2 * w + h + 1)
                nc.vector.reciprocal(rden[h][:, :, :, :], o[:, :, :, HD:HD + 1]).then_inc(rden_sb, 1)
                dve.wait_ge(rden_sb, 2 * w + h + 1)
                dve.wait_ge(att_out[h], 32 * w)
                nc.vector.tensor_tensor(att[h][:, :, :, :], o[:, :, :, 0:HD], rden[h][:, :, :, :].to_broadcast([112, 2, 4, HD]),
                                        ALU.mult).then_inc(att_sb, 1)

            def window(w, i, u, first, last):
                m0, r0 = held(dve, NU * w + NU), held(dve, NU * w + NU)
                for n in range(NU):
                    if not last:
                        maximum(w + 1, m0, r0, n)
                    if n == 5:
                        maximum_rows(w, i, u, 1)
                    if n == 9 and not (first and u == 0):
                        output_scaled(w - 1, i, 1)
                    if n == 29 and not last:
                        maximum_rows(w + 1, i if u == 0 else i + 1, 1 - u, 0)
                    if n == 33:
                        output_scaled(w, i, 0)

            for n in range(NU):
                maximum(0, 0, 0, n)
                if n == 30:
                    maximum_rows(0, 0, 0, 0)
            windows(dve, window)
            output_scaled(B - 1, B // U - 1, 1)


def after_cross(nc, io, scr, layer, out):
    with ExitStack() as ctx:
        a = Arena(nc, ctx, f"ff{layer}")
        L0 = layer == 0
        wo = a.sb("wo", [128, KC, D])
        ident = a.sb("ident", [128, 128])
        eps = a.sb("eps", [128, 1])
        loads = [(wo[:, :, :], wcols(io[f"xa{layer}_wo"])), (ident[:, :], io["ident"])]
        if L0:
            NI = 8
            up = a.sb("up", [128, KC, 1024])
            down = a.sb("down", [128, NI, D])
            fc1 = a.sb("fc1", [128, KC, 256])
            expert = a.sb("expert", [128, 2, 256])
            fc2 = a.sb("fc2", [128, 2, D])
            gate = a.sb("gate", [128, KC, 8])
            gamma, beta = a.sb("gamma", [128, D]), a.sb("beta", [128, D])
            loads += [(up[:, :, :], wcols(io["up"])), (down[:, :, :], wcols(io["down"])),
                      (fc1[:, :, :], wcols(io["fc1"])), (expert[:, :, :], wcols(io["expert"])),
                      (fc2[:, :, :], wcols(io["fc2"])), (gate[:, :, :], wcols(io["gate"])),
                      (gamma[:, :], io["gamma"].partition_broadcast(128)), (beta[:, :], io["beta"].partition_broadcast(128))]
        else:
            NE, R = 4, 16
            wr = a.sb("wr", [128, KC, NE * R + NE])
            lb = a.sb("lb", [NE * R, D])
            lower = a.sb("lower", [128, NE, NE])
            loads += [(wr[:, :, :], wcols(io["lora_a"])), (lb[:, :], io["lora_b"]),
                      (lower[:, :, :], io["lower"].rearrange("p (a b) -> p a b", a=NE))]

        def two(name, shape, dt=F32):
            return [a.sb(f"{name}{u}", shape, dt) for u in range(U)]

        at, x = two("at", [128, D]), two("x", [128, D])
        aT, xT = two("aT", [128, KC, 128]), two("xT", [128, KC, 128])
        y, x1, y2, x2 = two("y", [128, D]), two("x1", [128, D]), two("y2", [128, D]), two("x2", [128, D])
        if L0:
            lat, moe = two("lat", [128, 2, 128]), two("moe", [128, 2, 128])
            hid, hsq = two("hid", [128, NI, 128]), two("hsq", [128, NI, 128])
            top, wsum = two("top", [128, 8]), two("wsum", [128, 1])
            t1, f = two("t1", [128, D]), two("f", [128, D])
        else:
            lg, top = two("lg", [128, 8]), two("top", [128, 8])
            gt, eq = two("gt", [128, NE, NE]), two("eq", [128, NE, NE])
            rank, ex, gs, gr = two("rank", [128, NE]), two("ex", [128, NE]), two("gs", [128, 1]), two("gr", [128, 1])
            mid = two("mid", [128, 128 // R, R])
            midT = two("midT", [NE * R, 128])
        bank = [[a.ps(f"bank{u}_{n}") for n in range(4)] for u in range(U)]
        w_in, setup = a.sem("w_in"), a.sem("setup")
        x_in = [a.sem(f"x_in{u}") for u in range(U)]
        x_out = [a.sem(f"x_out{u}") for u in range(U)]
        names = ["aT_ps", "aT_sb", "y_ps", "y_sb", "x1_sb", "x1T_ps", "x1T_sb", "y2_sb", "x2_sb", "chain_dve"]
        names += ["lat_ps", "lat_sb", "moe_ps", "moe_sb", "up_ps", "hid_sb", "hsq_sb", "logit_ps", "top_sb", "down_ps",
                  "routed_ps", "f_sb", "t1_sb"] if L0 else ["mid_ps", "lg_sb", "ex_sb", "mid_sb", "midT_ps", "midT_sb", "delta_ps"]
        s = {n: a.sem(n) for n in names}
        norm = Norm(a, eps)
        pad = a.sb("pad", [1, U])
        NN = 3 if L0 else 2
        block = ctx.enter_context(nc.Block())

        @block.sync
        def _(sp):
            for dst, src in loads:
                sp.dma_start(dst, src).then_inc(w_in, 16)
            sp.wait_ge(setup, 2 * U)
            n_out = 16 if L0 else 32
            with sp.Fori(0, TILES // U) as i:
                for u in range(U):
                    n = U * i + u
                    sp.wait_ge(x_out[u], n_out * i)
                    sp.dma_start(x[u][:, :], scr["x"][n]).then_inc(x_in[u], 16)
                    for b in range(2):
                        sp.dma_start(at[u][b * SP_:b * SP_ + S, :], scr["att"][2 * U * i + 2 * u + b]).then_inc(x_in[u], 16)
                for u in range(U):
                    n = U * i + u
                    sp.wait_ge(s["x2_sb"], n + 1)
                    if L0:
                        sp.dma_start(scr["x"][n], x2[u][:, :]).then_inc(x_out[u], 16)
                    else:
                        for b in range(2):
                            sp.dma_start(out[2 * U * i + 2 * u + b], x2[u][b * SP_:b * SP_ + S, :]).then_inc(x_out[u], 16)
            for u in range(U):
                sp.wait_ge(x_out[u], n_out * (TILES // U))

        @block.tensor
        def _(pe):
            pe.wait_ge(w_in, 16 * len(loads))

            def transposed(u, src, dst, done):
                for k in range(KC):
                    mm = pe.transpose(dst[:, k * 128:(k + 1) * 128], src[u][:, k * 128:(k + 1) * 128], ident[:, :])
                mm.then_inc(done, 1)

            with pe.Fori(0, TILES // U) as i:
                for u in range(U):
                    pe.wait_ge(x_in[u], 48 * i + 48)
                    transposed(u, at, bank[u][0], s["aT_ps"])
                for u in range(U):
                    pe.wait_ge(s["aT_sb"], U * i + u + 1)
                    for k in range(KC):
                        mm = pe.matmul(bank[u][1][:, :], aT[u][:, k, :], wo[:, k, :], start=(k == 0), stop=(k == KC - 1))
                    mm.then_inc(s["y_ps"], 1)
                for u in range(U):
                    pe.wait_ge(s["x1_sb"], U * i + u + 1)
                    transposed(u, x1, bank[u][2], s["x1T_ps"])
                if L0:
                    for u in range(U):
                        n = U * i + u
                        pe.wait_ge(s["x1T_sb"], n + 1)
                        for t in range(2):
                            for k in range(KC):
                                mm = pe.matmul(bank[u][3][:, t * 128:(t + 1) * 128], fc1[:, k, t * 128:(t + 1) * 128],
                                               xT[u][:, k, :], start=(k == 0), stop=(k == KC - 1))
                        mm.then_inc(s["lat_ps"], 1)
                        for t in range(NI):
                            for k in range(KC):
                                mm = pe.matmul(bank[u][1 + t // 4][:, (t % 4) * 128:(t % 4 + 1) * 128],
                                               up[:, k, t * 128:(t + 1) * 128], xT[u][:, k, :],
                                               start=(k == 0), stop=(k == KC - 1))
                        mm.then_inc(s["up_ps"], 1)
                    for u in range(U):
                        n = U * i + u
                        pe.wait_ge(s["lat_sb"], n + 1)
                        for k in range(KC):
                            mm = pe.matmul(bank[u][3][:, 0:8], xT[u][:, k, :], gate[:, k, :], start=(k == 0), stop=(k == KC - 1))
                        mm.then_inc(s["logit_ps"], 1)
                        for t in range(2):
                            for k in range(2):
                                mm = pe.matmul(bank[u][0][:, t * 128:(t + 1) * 128], expert[:, k, t * 128:(t + 1) * 128],
                                               lat[u][:, k, :], start=(k == 0), stop=(k == 1))
                        mm.then_inc(s["moe_ps"], 1)
                    for u in range(U):
                        n = U * i + u
                        pe.wait_ge(s["moe_sb"], n + 1)
                        pe.wait_ge(s["hsq_sb"], n + 1)
                        for k in range(NI):
                            mm = pe.matmul(bank[u][0][:, :], hsq[u][:, k, :], down[:, k, :], start=(k == 0), stop=(k == NI - 1))
                        mm.then_inc(s["down_ps"], 1)
                        pe.wait_ge(s["top_sb"], n + 1)
                        for k in range(2):
                            mm = pe.matmul(bank[u][3][:, :], moe[u][:, k, :], fc2[:, k, :], start=(k == 0), stop=(k == 1))
                        mm.then_inc(s["routed_ps"], 1)
                else:
                    for u in range(U):
                        n = U * i + u
                        pe.wait_ge(s["x1T_sb"], n + 1)
                        for k in range(KC):
                            mm = pe.matmul(bank[u][3][:, 0:NE * R + NE], xT[u][:, k, :], wr[:, k, :], start=(k == 0), stop=(k == KC - 1))
                        mm.then_inc(s["mid_ps"], 1)
                    for u in range(U):
                        n = U * i + u
                        pe.wait_ge(s["mid_sb"], 4 * n + 4)
                        pe.transpose(bank[u][0][:, 0:128], mid[u][:, :, :].rearrange("p a b -> p (a b)"), ident[:, :]).then_inc(s["midT_ps"], 1)
                    for u in range(U):
                        n = U * i + u
                        pe.wait_ge(s["midT_sb"], n + 1)
                        pe.matmul(bank[u][1][:, :], midT[u][:, :], lb[:, :], start=True, stop=True).then_inc(s["delta_ps"], 1)

        @block.vector
        def _(dve):
            for u in range(U):
                nc.vector.memset(at[u][:, :], 0.0).then_inc(setup, 1)
            nc.vector.memset(eps[:, :], 1e-5).then_inc(setup, 1)
            if L0:
                nc.vector.memset(t1[0][:, :], 0.0).then_inc(setup, 1)
            else:
                for u in range(U):
                    nc.vector.memset(mid[u][:, :, :], 0.0)
                    last = nc.vector.memset(lg[u][:, :], NEG)
                last.then_inc(setup, 1)
            dve.wait_ge(w_in, 16 * len(loads))
            dve.wait_ge(setup, 2 * U)
            chain = Chain(dve, s["chain_dve"], U * (2 * NN + (3 if L0 else 8)), pad)
            with dve.Fori(0, TILES // U) as i:
                chain.k = 0
                chain.start = chain.per_round * i
                nn = 0
                for u in range(U):
                    n = U * i + u
                    dve.wait_ge(s["aT_ps"], n + 1)
                    nc.vector.tensor_copy(aT[u][:, :, :], bank[u][0][:, :].rearrange("p (c t) -> p c t", c=KC)).then_inc(s["aT_sb"], 1)
                for u in range(U):
                    n = U * i + u
                    dve.wait_ge(s["y_ps"], n + 1)
                    nc.vector.tensor_tensor(y[u][:, :], bank[u][1][:, :], x[u][:, :], ALU.add).then_inc(s["y_sb"], 1)
                    dve.wait_ge(s["y_sb"], n + 1)
                    norm.statistics(nc, chain, u, y[u][:, :])
                for u in range(U):
                    norm.apply(nc, dve, chain, u, x1[u][:, :], y[u][:, :], NN * U * i + U * nn + u + 1).then_inc(s["x1_sb"], 1)
                nn += 1
                for u in range(U):
                    n = U * i + u
                    dve.wait_ge(s["x1T_ps"], n + 1)
                    nc.vector.tensor_copy(xT[u][:, :, :], bank[u][2][:, :].rearrange("p (c t) -> p c t", c=KC)).then_inc(s["x1T_sb"], 1)
                if L0:
                    for u in range(U):
                        n = U * i + u
                        dve.wait_ge(s["hid_sb"], n + 1)
                        nc.vector.tensor_tensor(hsq[u][:, :, :], hid[u][:, :, :], hid[u][:, :, :], ALU.mult).then_inc(s["hsq_sb"], 1)
                        dve.wait_ge(s["logit_ps"], n + 1)
                        chain.carry(u)
                        chain.link(nc.vector.max(top[u][:, :], bank[u][3][:, 0:8]))
                        nc.vector.tensor_tensor(wsum[u][:, :], top[u][:, 0:1], top[u][:, 1:2], ALU.add).then_inc(s["top_sb"], 1)
                    for u in range(U):
                        n = U * i + u
                        dve.wait_ge(s["routed_ps"], n + 1)
                        dve.wait_ge(s["top_sb"], n + 1)
                        nc.vector.tensor_scalar(t1[u][:, :], bank[u][3][:, :], wsum[u][:, 0:1], None, ALU.mult).then_inc(s["t1_sb"], 1)
                        dve.wait_ge(s["t1_sb"], n + 1)
                        chain.link(nc.vector.tensor_tensor(f[u][:, :], bank[u][0][:, :], t1[u][:, :], ALU.add))
                        norm.statistics(nc, chain, u, f[u][:, :])
                    for u in range(U):
                        n = U * i + u
                        norm.apply(nc, dve, chain, u, f[u][:, :], f[u][:, :], NN * U * i + U * nn + u + 1).then_inc(s["f_sb"], 1)
                        dve.wait_ge(s["f_sb"], 3 * n + 1)
                        nc.vector.tensor_tensor(f[u][:, :], f[u][:, :], gamma[:, :], ALU.mult).then_inc(s["f_sb"], 1)
                        dve.wait_ge(s["f_sb"], 3 * n + 2)
                        nc.vector.tensor_tensor(f[u][:, :], f[u][:, :], beta[:, :], ALU.add).then_inc(s["f_sb"], 1)
                        dve.wait_ge(s["f_sb"], 3 * n + 3)
                        chain.link(nc.vector.tensor_tensor(y2[u][:, :], f[u][:, :], x1[u][:, :], ALU.add))
                        norm.statistics(nc, chain, u, y2[u][:, :])
                    nn += 1
                else:
                    for u in range(U):
                        n = U * i + u
                        dve.wait_ge(s["mid_ps"], n + 1)
                        chain.link(nc.vector.tensor_copy(lg[u][:, 0:NE], bank[u][3][:, NE * R:NE * R + NE]))
                        chain.carry(u)
                        chain.link(nc.vector.max(top[u][:, :], lg[u][:, :]))
                        nc.vector.tensor_scalar(ex[u][:, :], lg[u][:, 0:NE], top[u][:, 0:1], None, ALU.subtract).then_inc(s["lg_sb"], 1)
                        mine = lg[u][:, 0:NE].unsqueeze(2).to_broadcast([128, NE, NE])
                        other = lg[u][:, 0:NE].unsqueeze(1).to_broadcast([128, NE, NE])
                        chain.link(nc.vector.tensor_tensor(gt[u][:, :, :], other, mine, ALU.is_gt))
                        chain.link(nc.vector.tensor_tensor(eq[u][:, :, :], other, mine, ALU.is_equal))
                        chain.link(nc.vector.tensor_tensor(eq[u][:, :, :], eq[u][:, :, :], lower[:, :, :], ALU.mult))
                        chain.link(nc.vector.tensor_tensor(gt[u][:, :, :], gt[u][:, :, :], eq[u][:, :, :], ALU.add))
                        chain.link(nc.vector.tensor_reduce(rank[u][:, :], gt[u][:, :, :], AX.X, ALU.add))
                    for u in range(U):
                        n = U * i + u
                        dve.wait_ge(s["ex_sb"], n + 1)
                        nc.vector.scalar_tensor_tensor(out=ex[u][:, :], in0=rank[u][:, :], scalar=1.5, in1=ex[u][:, :],
                                                       op0=ALU.is_lt, op1=ALU.mult, accum_out=gs[u][:, :]).then_inc(s["mid_sb"], 1)
                        dve.wait_ge(s["mid_sb"], 4 * n + 1)
                        nc.vector.reciprocal(gr[u][:, :], gs[u][:, :]).then_inc(s["mid_sb"], 1)
                        dve.wait_ge(s["mid_sb"], 4 * n + 2)
                        nc.vector.tensor_scalar(ex[u][:, :], ex[u][:, :], gr[u][:, 0:1], None, ALU.mult).then_inc(s["mid_sb"], 1)
                        dve.wait_ge(s["mid_sb"], 4 * n + 3)
                        nc.vector.tensor_tensor(mid[u][:, 0:NE, :], bank[u][3][:, 0:NE * R].rearrange("p (e r) -> p e r", e=NE),
                                                ex[u][:, :].unsqueeze(2).to_broadcast([128, NE, R]), ALU.mult).then_inc(s["mid_sb"], 1)
                    for u in range(U):
                        n = U * i + u
                        dve.wait_ge(s["midT_ps"], n + 1)
                        nc.vector.tensor_copy(midT[u][:, :], bank[u][0][0:NE * R, 0:128]).then_inc(s["midT_sb"], 1)
                    for u in range(U):
                        n = U * i + u
                        dve.wait_ge(s["delta_ps"], n + 1)
                        chain.link(nc.vector.scalar_tensor_tensor(out=y2[u][:, :], in0=bank[u][1][:, :], scalar=4.0, in1=x1[u][:, :],
                                                                  op0=ALU.mult, op1=ALU.add))
                        norm.statistics(nc, chain, u, y2[u][:, :])
                for u in range(U):
                    norm.apply(nc, dve, chain, u, x2[u][:, :], y2[u][:, :], NN * U * i + U * nn + u + 1).then_inc(s["x2_sb"], 1)
                assert chain.k == chain.per_round, (chain.k, chain.per_round)

        @block.scalar
        def _(act):
            act.wait_ge(setup, 2 * U)
            with act.Fori(0, TILES // U) as i:
                for u in range(U):
                    norm.root(nc, act, u, NN * U * i + u + 1)
                if L0:
                    for u in range(U):
                        n = U * i + u
                        act.wait_ge(s["lat_ps"], n + 1)
                        nc.scalar.activation(lat[u][:, :, :], bank[u][3][:, 0:256].rearrange("p (a t) -> p a t", a=2), ACT.Copy).then_inc(s["lat_sb"], 1)
                        act.wait_ge(s["up_ps"], n + 1)
                        for c in range(2):
                            last = nc.scalar.activation(hid[u][:, 4 * c:4 * c + 4, :], bank[u][1 + c][:, :].rearrange("p (a t) -> p a t", a=4), ACT.Relu)
                        last.then_inc(s["hid_sb"], 1)
                    for u in range(U):
                        n = U * i + u
                        act.wait_ge(s["moe_ps"], n + 1)
                        nc.scalar.activation(moe[u][:, :, :], bank[u][0][:, 0:256].rearrange("p (a t) -> p a t", a=2), ACT.Copy).then_inc(s["moe_sb"], 1)
                    for u in range(U):
                        norm.root(nc, act, u, NN * U * i + U + u + 1)
                else:
                    for u in range(U):
                        n = U * i + u
                        act.wait_ge(s["lg_sb"], n + 1)
                        nc.scalar.activation(ex[u][:, :], ex[u][:, :], ACT.Exp).then_inc(s["ex_sb"], 1)
                for u in range(U):
                    norm.root(nc, act, u, NN * U * i + (NN - 1) * U + u + 1)


def decoder_kernel(nc, io, out):
    scr = {
        "k": nc.dram_tensor("scr_k", [B, 2, 2, 128, SK], F16, kind="Internal").ap(),
        "v": nc.dram_tensor("scr_v", [2, B, CH, VW], F32, kind="Internal").ap(),
        "q": nc.dram_tensor("scr_q", [2, B, 128, QG], F16, kind="Internal").ap(),
        "att": nc.dram_tensor("scr_att", [B, S, D], F32, kind="Internal").ap(),
        "x": nc.dram_tensor("scr_x", [TILES, 128, D], F32, kind="Internal").ap(),
    }
    project_context(nc, io, scr)
    self_attention(nc, io, scr, 0, io["x"])
    cross_attention(nc, io, scr, 0)
    after_cross(nc, io, scr, 0, None)
    self_attention(nc, io, scr, 1, scr["x"])
    cross_attention(nc, io, scr, 1)
    after_cross(nc, io, scr, 1, out)


def layout(inputs, np):
    f = lambda n: np.asarray(inputs[n])
    g, j, d = np.meshgrid(np.arange(G), np.arange(J), np.arange(HD), indexing="ij")
    head = ((g * J + j) * HD + d)
    by_j = head.transpose(1, 0, 2).reshape(-1)
    rot_q = head[:, :, (np.arange(HD) + HD // 2) % HD].transpose(1, 0, 2).reshape(-1)
    kv = np.arange(128).reshape(G, HD)
    rot_k = kv[:, (np.arange(HD) + HD // 2) % HD].reshape(-1)
    stored = head.reshape(2, 4, 2, 2, HD).transpose(3, 0, 2, 1, 4).reshape(-1)
    x = f("x")
    xp = np.zeros((B, SP_, D), x.dtype)
    xp[:, :S] = x
    io = {"x": xp.reshape(TILES, 128, D), "ctxT": f("ctx_4096").transpose(0, 2, 1), "mask": f("mask_SxS2_bk0")}
    io["wkv"] = np.concatenate([f("L0_xattn_Wk"), f("L1_xattn_w_k").T, f("L0_xattn_Wv"), f("L1_xattn_w_v").T], axis=1)
    io["sa0_wq"], io["sa0_wk"] = f("L0_attn_Wq").T, f("L0_attn_Wk").T
    io["sa0_wv"], io["sa0_wo"] = f("L0_attn_Wv").T, f("L0_attn_Wo").T
    for n in ("bq", "bk", "bv", "bo"):
        b = f(f"L0_attn_{n}")
        io[f"sa0_{n}"] = b.reshape(KC, 128).T if n in ("bq", "bk") else b
    wq, wk = f("L1_attn_Wq"), f("L1_attn_Wk")
    io["sa1_wq"] = np.concatenate([wq[:, by_j], wq[:, rot_q]], axis=1)
    io["sa1_wk"] = np.concatenate([wk, wk[:, rot_k]], axis=1)
    io["sa1_wv"], io["sa1_wo"] = f("L1_attn_Wv"), f("L1_attn_Wo")[by_j, :]
    io["xa0_wq"], io["xa0_wo"] = f("L0_xattn_Wq")[:, by_j], f("L0_xattn_Wo")[stored, :]
    io["xa1_wq"], io["xa1_wo"] = f("L1_xattn_w_q").T[:, by_j], f("L1_xattn_w_out").T[stored, :]
    io["up"], io["down"], io["fc1"] = f("L0_ffn_up_w"), f("L0_ffn_down_w"), f("L0_ffn_fc1_w")
    io["expert"], io["fc2"], io["gate"] = f("L0_ffn_expert_w"), f("L0_ffn_fc2_w"), f("L0_ffn_gate_w")
    io["gamma"], io["beta"] = f("L0_ffn_ln_gamma"), f("L0_ffn_ln_beta")
    io["lora_a"] = np.concatenate([f("L1_ffn_A").reshape(-1, D), f("L1_ffn_router_w")], axis=0).T
    io["lora_b"] = f("L1_ffn_B").transpose(0, 2, 1).reshape(-1, D)
    io["ident"] = np.eye(128, dtype=np.float32)
    io["blockmask"] = np.repeat((np.arange(128)[:, None] // HD == np.arange(8)[None, :]).astype(np.float32), SP_, axis=1)
    q = np.arange(128)[:, None] % SP_
    k = np.arange(SP_)[None, :]
    io["causal"] = np.where((k <= q) & (k < S), 0.0, NEG).astype(np.float32)
    half = HD // 2
    freq = (1.0 / np.float32(10000.0) ** (np.arange(half, dtype=np.float32) / np.float32(half))).astype(np.float32)
    ang = np.arange(SP_, dtype=np.float32)[None, :] * freq[np.arange(128) % half][:, None]
    sign = np.where(np.arange(128) % HD < half, -1.0, 1.0).astype(np.float32)[:, None]
    cos, sin = np.cos(ang).astype(np.float32), (sign * np.sin(ang)).astype(np.float32)
    io["rope"] = np.concatenate([cos * np.float32(0.25), sin * np.float32(0.25), cos, sin], axis=1)
    io["lower"] = np.tile((np.arange(4)[None, :] < np.arange(4)[:, None]).astype(np.float32).reshape(1, -1), (128, 1))
    return {n: np.ascontiguousarray(v) for n, v in io.items()}


def kernel(**inputs):
    import numpy as _np
    import concourse.bacc as _bacc
    from concourse import mybir as _mybir
    from concourse.bass_utils import run_bass_kernel_spmd as _run

    nc = _bacc.Bacc("TRN2", target_bir_lowering=False, num_devices=1)
    io = layout(inputs, _np)
    arrays = {f"in_{n}": v for n, v in io.items()}
    aps = {n: nc.dram_tensor(f"in_{n}", list(v.shape), _mybir.dt.from_np(v.dtype), kind="ExternalInput").ap()
           for n, v in io.items()}
    out = nc.dram_tensor("out_x", [B, S, D], F32, kind="ExternalOutput").ap()
    decoder_kernel(nc, aps, out)
    r = _run(nc, [arrays], core_ids=[0])
    return r.results[0]["out_x"]
```

```python
from contextlib import ExitStack

import concourse.bass as bass
from concourse import mybir

F32 = mybir.dt.float32
F16 = mybir.dt.float16
BF16 = mybir.dt.bfloat16
U8 = mybir.dt.uint8
ALU = mybir.AluOpType
ACT = mybir.ActivationFunctionType
AX = mybir.AxisListType

B, S, D = 16, 56, 512
KC = D // 128
SK = 1500
CH, NCH = 125, 12
NP, PT = 500, 3
H, G, J, HD = 32, 8, 4, 16
SP_ = 64
TILES = B // 2
U = 2
QG = J * S
QP = 2 * QG
NEG = -1e30
BIG = 60000.0
WSCALE = 64.0
VS = HD + 1
VW = NCH * G * VS + 16


class Arena:

    def __init__(self, nc, ctx, tag):
        self.nc, self.ctx, self.tag, self.sems = nc, ctx, tag, []
        ctx.callback(self.give_back)

    def give_back(self):
        self.nc.clear_and_free_semaphores(self.sems)
        self.nc.all_engine_barrier()

    def sb(self, name, shape, dt=F32):
        return self.ctx.enter_context(self.nc.sbuf_tensor(f"{self.tag}_{name}", shape, dt))

    def ps(self, name, shape=(128, 512)):
        return self.ctx.enter_context(self.nc.psum_tensor(f"{self.tag}_{name}", list(shape), F32))

    def sem(self, name):
        self.sems.append(self.nc.alloc_semaphore(f"{self.tag}_{name}"))
        return self.sems[-1]


def ge(eng, sem, value):
    if not isinstance(value, int) or value > 0:
        eng.wait_ge(sem, value)


def is_last(part, i):
    return isinstance(i, int) and i == part.rounds - 1


def run_rounds(eng, name, parts, rounds):
    def one(r):
        heads = []
        for p in parts:
            if not isinstance(r, int) or 0 <= r - p.lag < p.rounds:
                steps = p.programs[name](eng, r - p.lag)
                heads.append([next(steps, None), steps])
        while any(h[0] is not None for h in heads):
            h = min((h for h in heads if h[0] is not None), key=lambda h: h[0])
            h[0] = next(h[1], None)

    edge = 1 + max(p.lag for p in parts)
    for r in range(edge):
        one(r)
    with eng.Fori(edge, rounds - edge) as r:
        one(r)
    for r in range(rounds - edge, rounds):
        one(r)


class Chain:

    def __init__(self, eng, sem, per_round, pad):
        self.eng, self.sem, self.per_round, self.pad = eng, sem, per_round, pad
        self.start, self.k = 0, 0

    def link(self, ins):
        self.k += 1
        ins.then_inc(self.sem, 1)
        self.eng.wait_ge(self.sem, self.start + self.k)

    def carry(self, u):
        self.eng.memset(self.pad[:, u:u + 1], 0.0)


def wcols(w):
    return w.rearrange("(c p) n -> p c n", p=128)


class ContextProjection:

    NK, NV = 2 * PT, NCH
    NB = 2
    lag, rounds = 0, B // 2
    SPLITS = (7, 10, 13, 16)

    def __init__(self, nc, a, io, scr):
        self.nc, self.io, self.scr = nc, io, scr
        self.ctx32 = a.sb("ctx32", [128, KC, SK])
        self.chi = [a.sb(f"chi{u}", [128, KC, SK], F16) for u in range(2)]
        self.clo = [a.sb(f"clo{u}", [128, KC, SK], F16) for u in range(2)]
        self.w32 = a.sb("w32", [128, KC, 512])
        self.whi = a.sb("whi", [128, KC, 512], F16)
        self.wlo = a.sb("wlo", [128, KC, 512], F16)
        self.khi = a.sb("khi", [128, 2, SK], F16)
        self.klo = a.sb("klo", [128, 2, SK], F16)
        self.vout = a.sb("vout", [CH, 2, VW])
        self.kps = [a.ps(f"kps{n}") for n in range(self.NB)]
        self.vps = [a.ps(f"vps{n}") for n in range(self.NB)]
        self.w_in, self.w_hi, self.w_lo = a.sem("w_in"), a.sem("w_hi"), a.sem("w_lo")
        self.ctx_in = [a.sem(f"ctx_in{k}") for k in range(KC)]
        self.hi_done, self.lo_done = a.sem("hi_done"), a.sem("lo_done")
        self.k_ps, self.k_hi, self.k_lo = a.sem("k_ps"), a.sem("k_hi"), a.sem("k_lo")
        self.v_ps, self.v_sb = a.sem("v_ps"), a.sem("v_sb")
        self.k_out, self.v_out, self.ones = a.sem("k_out"), a.sem("v_out"), a.sem("ones")
        self.programs = {"sync": self.sync, "tensor": self.tensor, "scalar": self.scalar,
                         "vector": self.vector, "gpsimd": self.gpsimd}

    def load_chunk(self, sp, n, k):
        sp.dma_start(self.ctx32[:, k, :], self.io["ctxT"][n, k * 128:(k + 1) * 128, :]).then_inc(self.ctx_in[k], 16)

    def setup_sync(self, sp):
        sp.dma_start(self.w32[:, :, :], wcols(self.io["wkv"])).then_inc(self.w_in, 16)
        for k in range(KC):
            self.load_chunk(sp, 0, k)
        for k in range(KC):
            sp.wait_ge(self.lo_done, k + 1)
            self.load_chunk(sp, 1, k)

    def sync(self, sp, i):
        for u in range(2):
            n = 2 * i + u
            yield 18 * u + self.NK + 2
            sp.wait_ge(self.k_lo, self.NK * n + self.NK)
            for part, k in enumerate((self.khi, self.klo)):
                sp.dma_start(self.scr["k"][n, part].rearrange("l p t -> p l t"), k[:, :, :]).then_inc(self.k_out, 16)
            if not is_last(self, i):
                for k, slot in enumerate(self.SPLITS):
                    yield 18 * u + slot + 1
                    sp.wait_ge(self.lo_done, KC * (n + 1) + k + 1)
                    self.load_chunk(sp, n + 2, k)
            yield 18 * u + 18.5
            sp.wait_ge(self.v_sb, self.NV * n + self.NV)
            for layer in range(2):
                sp.dma_start(self.scr["v"][layer, n], self.vout[:, layer, :]).then_inc(self.v_out, 16)

    def finish_sync(self, sp):
        sp.wait_ge(self.k_out, 32 * B)
        sp.wait_ge(self.v_out, 32 * B)

    def setup_tensor(self, pe):
        pe.wait_ge(self.w_hi, KC)
        pe.wait_ge(self.w_lo, KC)

    def tensor(self, pe, i):
        for u in range(2):
            n = 2 * i + u
            terms = ((self.whi, self.chi[u]), (self.wlo, self.chi[u]), (self.whi, self.clo[u]))
            for m in range(self.NK):
                yield 18 * u + m
                if m == 0:
                    pe.wait_ge(self.lo_done, KC * n + KC)
                layer, part = m // PT, m % PT
                ge(pe, self.k_lo, self.NK * n + m + 1 - self.NB)
                for t, (w, c) in enumerate(terms):
                    for k in range(KC):
                        mm = pe.matmul(self.kps[m % self.NB][:, 0:NP], w[:, k, layer * 128:layer * 128 + 128],
                                       c[:, k, part * NP:(part + 1) * NP],
                                       start=(t == 0 and k == 0), stop=(t == 2 and k == KC - 1))
                mm.then_inc(self.k_ps, 1)
            for m in range(self.NV):
                yield 18 * u + self.NK + m
                ge(pe, self.v_sb, self.NV * n + m + 1 - self.NB)
                for k in range(KC):
                    for t, (w, c) in enumerate(terms):
                        mm = pe.matmul(self.vps[m % self.NB][0:CH, 0:256], c[:, k, m * CH:(m + 1) * CH],
                                       w[:, k, 256:512], start=(t == 0 and k == 0), stop=(t == 2 and k == KC - 1))
                mm.then_inc(self.v_ps, 1)

    def split_hi(self, n, u, k):
        self.nc.scalar.activation(self.chi[u][:, k, :], self.ctx32[:, k, :], ACT.Copy).then_inc(self.hi_done, 1)

    def setup_scalar(self, act):
        act.wait_ge(self.w_in, 16)
        for k in range(KC):
            self.nc.scalar.activation(self.whi[:, k, :], self.w32[:, k, :], ACT.Copy, scale=WSCALE).then_inc(self.w_hi, 1)
        for k in range(KC):
            act.wait_ge(self.ctx_in[k], 16)
            self.split_hi(0, 0, k)
        act.wait_ge(self.ones, 1)

    def scalar(self, act, i):
        nc = self.nc
        for u in range(2):
            n = 2 * i + u
            for m in range(self.NK):
                yield 18 * u + m + 1
                layer, part = m // PT, m % PT
                if m == 0:
                    ge(act, self.k_out, 32 * n)
                act.wait_ge(self.k_ps, self.NK * n + m + 1)
                nc.scalar.activation(self.khi[:, layer, part * NP:(part + 1) * NP], self.kps[m % self.NB][:, 0:NP],
                                     ACT.Copy, scale=1.0 / WSCALE).then_inc(self.k_hi, 1)
            for m in range(self.NV):
                slot = self.NK + m + 1
                yield 18 * u + slot
                if m == 0:
                    ge(act, self.v_out, 32 * n)
                act.wait_ge(self.v_ps, self.NV * n + m + 1)
                nc.scalar.activation(
                    self.vout[:, :, m * G * VS:(m + 1) * G * VS].rearrange("p l (g v) -> p l g v", v=VS)[:, :, :, 0:HD],
                    self.vps[m % self.NB][0:CH, 0:256].rearrange("p (l g v) -> p l g v", l=2, v=HD),
                    ACT.Copy, scale=1.0 / WSCALE).then_inc(self.v_sb, 1)
                if slot in self.SPLITS and not (is_last(self, i) and u == 1):
                    k = self.SPLITS.index(slot)
                    act.wait_ge(self.ctx_in[k], 16 * (n + 2))
                    self.split_hi(n + 1, 1 - u, k)

    def split_lo(self, u, k):
        self.nc.vector.tensor_tensor(self.clo[u][:, k, :], self.ctx32[:, k, :], self.chi[u][:, k, :],
                                     ALU.subtract).then_inc(self.lo_done, 1)

    def setup_vector(self, dve):
        nc = self.nc
        nc.vector.memset(self.vout[:, :, :], 1.0).then_inc(self.ones, 1)
        for k in range(KC):
            dve.wait_ge(self.w_hi, k + 1)
            nc.vector.scalar_tensor_tensor(out=self.wlo[:, k, :], in0=self.w32[:, k, :], scalar=WSCALE,
                                           in1=self.whi[:, k, :], op0=ALU.mult, op1=ALU.subtract).then_inc(self.w_lo, 1)
        for k in range(KC):
            dve.wait_ge(self.hi_done, k + 1)
            self.split_lo(0, k)

    def vector(self, dve, i):
        for u in range(2):
            n = 2 * i + u
            for m in range(self.NK):
                yield 18 * u + m + 1
                layer, part = m // PT, m % PT
                cols = slice(part * NP, (part + 1) * NP)
                dve.wait_ge(self.k_hi, self.NK * n + m + 1)
                if m == 0:
                    ge(dve, self.k_out, 32 * n)
                self.nc.vector.scalar_tensor_tensor(out=self.klo[:, layer, cols], in0=self.kps[m % self.NB][:, 0:NP],
                                                    scalar=1.0 / WSCALE, in1=self.khi[:, layer, cols],
                                                    op0=ALU.mult, op1=ALU.subtract).then_inc(self.k_lo, 1)
            for k, slot in enumerate(self.SPLITS):
                yield 18 * u + slot + 0.5
                if not (is_last(self, i) and u == 1):
                    dve.wait_ge(self.hi_done, KC * (n + 1) + k + 1)
                    self.split_lo(1 - u, k)

    def gpsimd(self, pool, i):
        return iter(())


class Norm:

    def __init__(self, nc, a, eps, tiles):
        self.nc = nc
        self.stats = [a.sb(f"stats{u}", [128, 6]) for u in range(tiles)]
        self.mv = [a.sb(f"mv{u}", [128, 2]) for u in range(tiles)]
        self.std = [a.sb(f"std{u}", [128, 1]) for u in range(tiles)]
        self.rstd = [a.sb(f"rstd{u}", [128, 1]) for u in range(tiles)]
        self.eps = eps
        self.var_ready, self.std_ready = a.sem("var_ready"), a.sem("std_ready")

    def statistics(self, chain, u, src):
        chain.link(self.nc.vector.bn_stats(self.stats[u][:, :], src))
        chain.carry(u)
        self.nc.vector.bn_aggr(self.mv[u][:, :], self.stats[u][:, :]).then_inc(self.var_ready, 1)

    def root(self, act, u, count):
        act.wait_ge(self.var_ready, count)
        self.nc.scalar.activation(self.std[u][:, :], self.mv[u][:, 1:2], ACT.Sqrt, bias=self.eps[:, 0:1]).then_inc(self.std_ready, 1)

    def apply(self, dve, chain, u, dst, src, count):
        dve.wait_ge(self.std_ready, count)
        chain.link(self.nc.vector.reciprocal(self.rstd[u][:, :], self.std[u][:, :]))
        return self.nc.vector.tensor_scalar(dst, src, self.mv[u][:, 0:1], self.rstd[u][:, 0:1],
                                            ALU.subtract, ALU.mult)


class SelfAttention:

    def __init__(self, nc, a, io, scr, layer, lag, x_src=None, x_tile=None, x_ready=None):
        self.nc, self.scr, self.layer, self.x_src, self.lag = nc, scr, layer, x_src, lag
        self.rounds = TILES
        L0 = layer == 0
        NQ = D if L0 else 2 * D
        NKC = D if L0 else 2 * 128
        NVC = D if L0 else 128
        self.KT = KT = 4 if L0 else 1
        self.wq = a.sb("wq", [128, KC, NQ])
        self.wk = a.sb("wk", [128, KC, NKC])
        self.wv = a.sb("wv", [128, KC, NVC])
        self.wo = a.sb("wo", [128, KC, D])
        self.wxq = a.sb("wxq", [128, KC, D])
        self.ident = a.sb("ident", [128, 128])
        self.blockmask = a.sb("blockmask", [128, 8, SP_])
        self.causal = a.sb("causal", [128, SP_])
        self.eps = a.sb("eps", [128, 1])
        self.loads = [(self.ident[:, :], io["ident"]),
                      (self.wq[:, :, :], wcols(io[f"sa{layer}_wq"])), (self.wk[:, :, :], wcols(io[f"sa{layer}_wk"])),
                      (self.wv[:, :, :], wcols(io[f"sa{layer}_wv"])), (self.wo[:, :, :], wcols(io[f"sa{layer}_wo"])),
                      (self.wxq[:, :, :], wcols(io[f"xa{layer}_wq"])),
                      (self.blockmask[:, :, :], io["blockmask"].rearrange("p (h k) -> p h k", h=8)),
                      (self.causal[:, :], io["causal"])]
        if L0:
            self.bq, self.bk = a.sb("bq", [128, 4]), a.sb("bk", [128, 4])
            self.bv, self.bo = a.sb("bv", [1, D]), a.sb("bo", [1, D])
            self.ones = a.sb("ones", [1, 128])
            self.loads += [(self.bq[:, :], io["sa0_bq"]), (self.bk[:, :], io["sa0_bk"]),
                           (self.bv[:, :], io["sa0_bv"].rearrange("(a n) -> a n", a=1)),
                           (self.bo[:, :], io["sa0_bo"].rearrange("(a n) -> a n", a=1))]
        else:
            self.rope = a.sb("rope", [128, 4, SP_])
            self.mask_u8 = a.sb("mask_u8", [S, SK], U8)
            self.mask16 = a.sb("mask16", [S, SK], BF16)
            self.maxkeep = a.sb("maxkeep", [S, 1])
            self.keepq = a.sb("keepq", [S, 128])
            self.keep_bc = a.sb("keep_bc", [128, SP_])
            self.rot = a.sb("rot", [128, 512])
            self.loads += [(self.rope[:, :, :], io["rope"].rearrange("p (a q) -> p a q", a=4)),
                           (self.mask_u8[:, :], io["mask"])]
        self.x = x_tile if x_src is None else a.sb("x", [128, D])
        self.xT = a.sb("xT", [128, KC, 128])
        self.qT = a.sb("qT", [128, 4, 128])
        self.kT = a.sb("kT", [128, KT, 128])
        self.kbd = [a.sb(f"kbd{r}", [128, 2, 8, SP_]) for r in range(min(KT, 2))]
        hp = 16 if L0 else 4
        self.vbd = a.sb("vbd", [128, 2, hp, 2, HD])
        self.sc = a.sb("sc", [128, 4, 8, SP_])
        self.mx, self.sm, self.rs = (a.sb(n, [128, 4, 8]) for n in ("mx", "sm", "rs"))
        self.pT = a.sb("pT", [128, 4, 512])
        self.att = a.sb("att", [128, 512])
        self.attT = a.sb("attT", [128, KC, 128])
        self.y, self.x1 = a.sb("y", [128, D]), a.sb("x1", [128, D])
        self.q32 = a.sb("q32", [128, 512])
        self.qhi, self.qlo = a.sb("qhi", [128, 512], F16), a.sb("qlo", [128, 512], F16)
        self.pad = a.sb("pad", [1, 1])
        self.bank = [a.ps(f"bank{n}") for n in range(4)]
        self.w_in, self.setup, self.eps_ready = a.sem("w_in"), a.sem("setup"), a.sem("eps_ready")
        names = ["x_in", "x_out", "xT_ps", "xT_sb", "qk_ps", "q_sb", "k_sb", "v_ps", "v_sb", "kbd_sb", "s_ps", "s_sub",
                 "s_add", "p_sb", "pT_ps", "pT_sb", "att_ps", "att_sb", "attT_ps", "attT_sb", "y_ps", "y_sb",
                 "x1_sb", "x1T_ps", "x1T_sb", "xq_ps", "q32_sb", "qhi_sb", "qlo_sb", "chain_dve", "keep_ps", "keep_sb"]
        self.s = {n: a.sem(n) for n in names}
        self.x_ready, self.x_count = (self.s["x_in"], 16) if x_src is not None else (x_ready, 1)
        self.norm = Norm(nc, a, self.eps, 1)
        self.chain = None
        self.programs = {"sync": self.sync, "tensor": self.tensor, "scalar": self.scalar,
                         "vector": self.vector, "gpsimd": self.gpsimd}

    def loaded(self, eng):
        eng.wait_ge(self.w_in, 16 * len(self.loads))

    def setup_sync(self, sp):
        for dst, src in self.loads:
            sp.dma_start(dst, src).then_inc(self.w_in, 16)
        if self.x_src is not None:
            sp.dma_start(self.x[:, :], self.x_src[0]).then_inc(self.x_ready, 16)

    def sync(self, sp, i):
        s = self.s
        yield 26
        if self.x_src is not None and not is_last(self, i):
            sp.wait_ge(s["y_sb"], i + 1)
            sp.dma_start(self.x[:, :], self.x_src[i + 1]).then_inc(self.x_ready, 16)
        yield 28
        sp.wait_ge(s["x1_sb"], i + 1)
        sp.dma_start(self.scr["x"][self.layer, i], self.x1[:, :]).then_inc(s["x_out"], 16)
        yield 34
        for part, (ready, q) in enumerate(((s["qhi_sb"], self.qhi), (s["qlo_sb"], self.qlo))):
            sp.wait_ge(ready, i + 1)
            for b in range(2):
                sp.dma_start(self.scr["q"][part, 2 * i + b],
                             q[:, :].rearrange("p (j b q) -> p j b q", b=2, j=4)[:, :, b, 0:S]).then_inc(s["x_out"], 16)

    def finish_sync(self, sp):
        sp.wait_ge(self.s["x_out"], 80 * TILES)

    def setup_tensor(self, pe):
        pass

    def tensor(self, pe, i):
        s, L0, bank, ident = self.s, self.layer == 0, self.bank, self.ident

        def transposed(src, dst, done):
            for k in range(KC):
                mm = pe.transpose(dst[:, k * 128:(k + 1) * 128], src[:, k * 128:(k + 1) * 128], ident[:, :])
            mm.then_inc(done, 1)

        yield 1
        if isinstance(i, int) and i == 0:
            self.loaded(pe)
            if not L0:
                pe.wait_ge(self.setup, 4)
                pe.matmul(bank[0][:, 0:S], self.keepq[:, :], ident[0:S, 0:S], start=True, stop=True).then_inc(s["keep_ps"], 1)
                pe.wait_ge(s["keep_sb"], 1)
        pe.wait_ge(self.x_ready, self.x_count * i + self.x_count)
        transposed(self.x, bank[0], s["xT_ps"])
        yield 3
        pe.wait_ge(s["xT_sb"], i + 1)
        jobs = [(bank[1], self.wq, 4, 0), (bank[2], self.wk, 4, 0)] if L0 else \
               [(bank[1], self.wq, 4, 0), (bank[2], self.wq, 4, 4), (bank[3], self.wk, 2, 0)]
        for dst, w, tiles, first in jobs:
            for t in range(tiles):
                for k in range(KC):
                    mm = pe.matmul(dst[:, t * 128:(t + 1) * 128], w[:, k, (first + t) * 128:(first + t + 1) * 128],
                                   self.xT[:, k, :], start=(k == 0), stop=(k == KC - 1))
        mm.then_inc(s["qk_ps"], 1)
        yield 4
        for b in range(2):
            out = bank[3 if b == 0 else 0][:, 0:D] if L0 else bank[0][:, b * 128:(b + 1) * 128]
            for k in range(KC):
                for half in range(2):
                    mm = pe.matmul(out[half * SP_:(half + 1) * SP_, :], self.xT[:, k, b * SP_:(b + 1) * SP_],
                                   self.wv[:, k, :], start=(k == 0), stop=(k == KC - 1 and not L0))
            if L0:
                for half in range(2):
                    mm = pe.matmul(out[half * SP_:(half + 1) * SP_, :], self.ones[0:1, 0:SP_], self.bv[0:1, :],
                                   start=False, stop=True)
        mm.then_inc(s["v_ps"], 1)

        def scores(t):
            if t == 0:
                pe.wait_ge(s["q_sb"], i + 1)
                pe.wait_ge(s["k_sb"], i + 1)
            pe.wait_ge(s["kbd_sb"], self.KT * i + min(t, self.KT - 1) + 1)
            if t >= 2:
                pe.wait_ge(s["s_add"], 4 * i + t - 1)
            for b in range(2):
                mm = pe.matmul(bank[1 + t % 2][b * SP_:(b + 1) * SP_, :], self.qT[:, t, b * SP_:(b + 1) * SP_],
                               self.kbd[t % 2 if L0 else 0][:, b, :, :], start=True, stop=True)
            mm.then_inc(s["s_ps"], 1)

        def probs_transposed(t):
            pe.wait_ge(s["p_sb"], 4 * i + t + 1)
            if t == 0:
                pe.wait_ge(s["v_sb"], i + 1)
            if t >= 2:
                pe.wait_ge(s["pT_sb"], 4 * i + t - 1)
            for k in range(4):
                mm = pe.transpose(bank[3 if t % 2 == 0 else 0][:, k * 128:(k + 1) * 128],
                                  self.sc[:, t, 2 * k:2 * k + 2, :], ident[:, :])
            mm.then_inc(s["pT_ps"], 1)

        for t in range(6):
            yield 7 + 2 * t
            if t < 4:
                scores(t)
            if t >= 2:
                probs_transposed(t - 2)
        yield 19
        pe.wait_ge(s["s_add"], 4 * i + 4)
        pe.wait_ge(s["pT_sb"], 4 * i + 4)
        for t in range(4):
            for k in range(4):
                for b in range(2):
                    c = t * 128 + k * 32
                    mm = pe.matmul(bank[1][b * SP_:(b + 1) * SP_, c:c + 32],
                                   self.pT[:, t, k * 128 + b * SP_:k * 128 + (b + 1) * SP_],
                                   self.vbd[:, b, t * 4 + k if L0 else k, :, :], start=True, stop=True)
        mm.then_inc(s["att_ps"], 1)
        yield 21
        pe.wait_ge(s["att_sb"], i + 1)
        transposed(self.att, bank[2], s["attT_ps"])
        yield 23
        pe.wait_ge(s["attT_sb"], i + 1)
        for k in range(KC):
            mm = pe.matmul(bank[3][:, :], self.attT[:, k, :], self.wo[:, k, :], start=(k == 0), stop=(k == KC - 1 and not L0))
        if L0:
            mm = pe.matmul(bank[3][:, :], self.ones[0:1, :], self.bo[0:1, :], start=False, stop=True)
        mm.then_inc(s["y_ps"], 1)
        yield 28
        pe.wait_ge(s["x1_sb"], i + 1)
        transposed(self.x1, bank[0], s["x1T_ps"])
        yield 30
        pe.wait_ge(s["x1T_sb"], i + 1)
        for t in range(4):
            for k in range(KC):
                mm = pe.matmul(bank[1][:, t * 128:(t + 1) * 128], self.wxq[:, k, t * 128:(t + 1) * 128],
                               self.xT[:, k, :], start=(k == 0), stop=(k == KC - 1))
        mm.then_inc(s["xq_ps"], 1)

    def setup_vector(self, dve):
        nc = self.nc
        nc.vector.memset(self.vbd[:, :, :, :, :], 0.0).then_inc(self.setup, 1)
        nc.vector.memset(self.eps[:, :], 1e-5).then_inc(self.eps_ready, 1)
        if self.layer == 0:
            nc.vector.memset(self.ones[:, :], 1.0).then_inc(self.setup, 1)
        self.chain = Chain(dve, self.s["chain_dve"], (0 if self.layer == 0 else 5) + 4 * 2 + 1 + 2, self.pad)

    def prepare_mask(self, dve):
        nc = self.nc
        nc.vector.tensor_copy(self.mask16[:, :], self.mask_u8[:, :]).then_inc(self.setup, 1)
        dve.wait_ge(self.setup, 2)
        nc.vector.reduce_max(self.maxkeep[:, :], self.mask16[:, :], AX.X).then_inc(self.setup, 1)
        dve.wait_ge(self.setup, 3)
        nc.vector.tensor_copy(self.keepq[:, :], self.maxkeep[:, 0:1].to_broadcast([S, 128])).then_inc(self.setup, 1)
        nc.vector.memset(self.keep_bc[:, S:SP_], 1.0)
        dve.wait_ge(self.s["keep_ps"], 1)
        nc.vector.tensor_copy(self.keep_bc[:, 0:S], self.bank[0][:, 0:S]).then_inc(self.s["keep_sb"], 1)

    def vector(self, dve, i):
        nc, s, L0, bank, chain = self.nc, self.s, self.layer == 0, self.bank, self.chain
        chain.start, chain.k = chain.per_round * i, 0
        yield 0
        if isinstance(i, int) and i == 0:
            self.loaded(dve)
            if not L0:
                self.prepare_mask(dve)
                dve.wait_ge(s["keep_sb"], 1)
        yield 2
        dve.wait_ge(s["xT_ps"], i + 1)
        nc.vector.tensor_copy(self.xT[:, :, :], bank[0][:, :].rearrange("p (c t) -> p c t", c=KC)).then_inc(s["xT_sb"], 1)
        yield 5
        dve.wait_ge(s["qk_ps"], i + 1)
        qT = self.qT[:, :, :].rearrange("p a b -> p (a b)")
        if L0:
            for t in range(4):
                last = nc.vector.tensor_scalar(self.qT[:, t, :], bank[1][:, t * 128:(t + 1) * 128],
                                               self.bq[:, t:t + 1], 0.25, ALU.add, ALU.mult)
            last.then_inc(s["q_sb"], 1)
        else:
            def tab(r, reps):
                return self.rope[:, r, :].unsqueeze(1).to_broadcast([128, reps, SP_])

            def by(ap):
                return ap.rearrange("p (r q) -> p r q", q=SP_)
            rot, k = self.rot, self.kT[:, 0, :]
            chain.link(nc.vector.tensor_tensor(by(rot[:, 0:128]), by(bank[3][:, 128:256]), tab(3, 2), ALU.mult))
            chain.link(nc.vector.tensor_tensor(by(k), by(bank[3][:, 0:128]), tab(2, 2), ALU.mult))
            nc.vector.tensor_tensor(k, k, rot[:, 0:128], ALU.add).then_inc(s["k_sb"], 1)
            dve.wait_ge(s["k_sb"], i + 1)
            chain.link(nc.vector.tensor_tensor(by(rot[:, :]), by(bank[2][:, :]), tab(1, 8), ALU.mult))
            chain.link(nc.vector.tensor_tensor(by(qT), by(bank[1][:, :]), tab(0, 8), ALU.mult))
            nc.vector.tensor_tensor(qT, qT, rot[:, :], ALU.add).then_inc(s["q_sb"], 1)

        def mask_and_maximum(t):
            sc = self.sc[:, t, :, :]
            dve.wait_ge(s["s_ps"], 4 * i + t + 1)
            nc.vector.tensor_tensor(sc, bank[1 + t % 2][:, :].rearrange("p (h k) -> p h k", h=8),
                                    self.causal[:, :].unsqueeze(1).to_broadcast([128, 8, SP_]), ALU.add).then_inc(s["s_add"], 1)
            dve.wait_ge(s["s_add"], 4 * i + t + 1)
            chain.link(nc.vector.tensor_reduce(self.mx[:, t, :], sc, AX.X, ALU.max))
            nc.vector.tensor_tensor(sc, sc, self.mx[:, t, :].unsqueeze(2).to_broadcast([128, 8, SP_]),
                                    ALU.subtract).then_inc(s["s_sub"], 1)

        def sums(t):
            dve.wait_ge(s["p_sb"], 4 * i + t + 1)
            chain.link(nc.vector.tensor_reduce(self.sm[:, t, :], self.sc[:, t, :, :], AX.X, ALU.add))

        for t in range(5):
            yield 8 + 2 * t
            if t < 4:
                mask_and_maximum(t)
            if t >= 1:
                sums(t - 1)
        chain.link(nc.vector.reciprocal(self.rs[:, :, :], self.sm[:, :, :]))
        yield 20
        dve.wait_ge(s["att_ps"], i + 1)
        nc.vector.tensor_tensor(self.att[:, :].rearrange("p (h d) -> p h d", d=HD),
                                bank[1][:, :].rearrange("p (h d) -> p h d", d=HD),
                                self.rs[:, :, :].rearrange("p t h -> p (t h)").unsqueeze(2).to_broadcast([128, 32, HD]),
                                ALU.mult).then_inc(s["att_sb"], 1)
        yield 25
        dve.wait_ge(s["y_ps"], i + 1)
        nc.vector.tensor_tensor(self.y[:, :], bank[3][:, :], self.x[:, :], ALU.add).then_inc(s["y_sb"], 1)
        dve.wait_ge(s["y_sb"], i + 1)
        self.norm.statistics(chain, 0, self.y[:, :])
        yield 27
        ge(dve, s["x_out"], 80 * i)
        self.norm.apply(dve, chain, 0, self.x1[:, :], self.y[:, :], i + 1).then_inc(s["x1_sb"], 1)
        yield 29
        dve.wait_ge(s["x1T_ps"], i + 1)
        nc.vector.tensor_copy(self.xT[:, :, :], bank[0][:, :].rearrange("p (c t) -> p c t", c=KC)).then_inc(s["x1T_sb"], 1)
        yield 32
        dve.wait_ge(s["xq_ps"], i + 1)
        if L0:
            nc.vector.tensor_scalar(self.q32[:, :], bank[1][:, :], 0.25, None, ALU.mult).then_inc(s["q32_sb"], 1)
        else:
            chain.link(nc.vector.tensor_tensor(self.q32[:, :].rearrange("p (r q) -> p r q", q=SP_),
                                               bank[1][:, :].rearrange("p (r q) -> p r q", q=SP_),
                                               self.keep_bc[:, :].unsqueeze(1).to_broadcast([128, 8, SP_]), ALU.mult))
            nc.vector.tensor_scalar(self.q32[:, :], self.q32[:, :], 0.25, None, ALU.mult).then_inc(s["q32_sb"], 1)
        yield 34
        dve.wait_ge(s["qhi_sb"], i + 1)
        nc.vector.tensor_tensor(self.qlo[:, :], self.q32[:, :], self.qhi[:, :], ALU.subtract).then_inc(s["qlo_sb"], 1)
        assert chain.k == chain.per_round, (chain.k, chain.per_round)

    def setup_scalar(self, act):
        pass

    def scalar(self, act, i):
        nc, s, L0, bank = self.nc, self.s, self.layer == 0, self.bank
        yield 5
        if isinstance(i, int) and i == 0:
            self.loaded(act)
            act.wait_ge(self.setup, 2 if L0 else 4)
            act.wait_ge(self.eps_ready, 1)
        if L0:
            act.wait_ge(s["qk_ps"], i + 1)
            for t in range(4):
                last = nc.scalar.activation(self.kT[:, t, :], bank[2][:, t * 128:(t + 1) * 128],
                                            ACT.Identity, bias=self.bk[:, t:t + 1])
            last.then_inc(s["k_sb"], 1)
        yield 6
        act.wait_ge(s["v_ps"], i + 1)
        for b in range(2):
            src = bank[3 if b == 0 else 0][:, 0:D] if L0 else bank[0][:, b * 128:(b + 1) * 128]
            for half in range(2):
                rows = slice(64 * half, 64 * half + 64)
                last = nc.scalar.activation(self.vbd[rows, b, :, half, :],
                                            src[rows, :].rearrange("p (m s d) -> p m s d", s=2, d=HD)[:, :, half, :],
                                            ACT.Copy)
        last.then_inc(s["v_sb"], 1)
        for t in range(6):
            yield 9 + 2 * t
            if t < 4:
                act.wait_ge(s["s_sub"], 4 * i + t + 1)
                nc.scalar.activation(self.sc[:, t, :, :], self.sc[:, t, :, :], ACT.Exp).then_inc(s["p_sb"], 1)
            if t >= 2:
                yield 9 + 2 * t - 0.5 + 1
                act.wait_ge(s["pT_ps"], 4 * i + t - 1)
                nc.scalar.activation(self.pT[:, t - 2, :], bank[3 if t % 2 == 0 else 0][:, :], ACT.Copy).then_inc(s["pT_sb"], 1)
        yield 22
        act.wait_ge(s["attT_ps"], i + 1)
        nc.scalar.activation(self.attT[:, :, :], bank[2][:, :].rearrange("p (c t) -> p c t", c=KC), ACT.Copy).then_inc(s["attT_sb"], 1)
        yield 26
        self.norm.root(act, 0, i + 1)
        yield 33
        act.wait_ge(s["q32_sb"], i + 1)
        nc.scalar.activation(self.qhi[:, :], self.q32[:, :], ACT.Copy).then_inc(s["qhi_sb"], 1)

    def gpsimd(self, pool, i):
        nc, s = self.nc, self.s
        yield 6
        if isinstance(i, int) and i == 0:
            self.loaded(pool)
        pool.wait_ge(s["k_sb"], i + 1)
        for t in range(self.KT):
            if t >= 2:
                yield 8 + 2 * (t - 2)
                pool.wait_ge(s["s_ps"], 4 * i + t - 1)
            for b in range(2):
                last = nc.gpsimd.tensor_tensor(
                    self.kbd[t % 2][:, b, :, :], self.kT[:, t, b * SP_:(b + 1) * SP_].unsqueeze(1).to_broadcast([128, 8, SP_]),
                    self.blockmask[:, :, :], ALU.mult)
            last.then_inc(s["kbd_sb"], 1)




class AfterCross:

    NI = 8
    NE, R = 4, 16
    lag = 0

    def __init__(self, nc, a, io, scr, layer, T, out):
        self.nc, self.io, self.scr, self.layer, self.T, self.out = nc, io, scr, layer, T, out
        self.rounds, self.x2_used = TILES // T, None
        NI, NE, R = self.NI, self.NE, self.R
        self.wo = a.sb("wo", [128, KC, D])
        self.ident = a.sb("ident", [128, 128])
        self.eps = a.sb("eps", [128, 1])
        self.loads = [(self.ident[:, :], io["ident"]), (self.wo[:, :, :], wcols(io[f"xa{layer}_wo"]))]
        if layer == 0:
            self.up = a.sb("up", [128, KC, 1024])
            self.down = a.sb("down", [128, NI, D])
            self.fc1 = a.sb("fc1", [128, KC, 256])
            self.expert = a.sb("expert", [128, 2, 256])
            self.fc2 = a.sb("fc2", [128, 2, D])
            self.gate = a.sb("gate", [128, KC, 8])
            self.gamma, self.beta = a.sb("gamma", [128, D]), a.sb("beta", [128, D])
            self.loads += [(self.fc1[:, :, :], wcols(io["fc1"])), (self.up[:, :, :], wcols(io["up"])),
                           (self.gate[:, :, :], wcols(io["gate"])), (self.expert[:, :, :], wcols(io["expert"])),
                           (self.down[:, :, :], wcols(io["down"])), (self.fc2[:, :, :], wcols(io["fc2"])),
                           (self.gamma[:, :], io["gamma"].partition_broadcast(128)),
                           (self.beta[:, :], io["beta"].partition_broadcast(128))]
        else:
            self.wr = a.sb("wr", [128, KC, NE * R + NE])
            self.lb = a.sb("lb", [NE * R, D])
            self.lower = a.sb("lower", [128, NE, NE])
            self.loads += [(self.wr[:, :, :], wcols(io["lora_a"])), (self.lb[:, :], io["lora_b"]),
                           (self.lower[:, :, :], io["lower"].rearrange("p (a b) -> p a b", a=NE))]

        def each(name, shape, dt=F32):
            return [a.sb(f"{name}{u}", shape, dt) for u in range(T)]

        self.at, self.x = each("at", [128, D]), each("x", [128, D])
        self.aT, self.xT = each("aT", [128, KC, 128]), each("xT", [128, KC, 128])
        self.y, self.x1, self.y2, self.x2 = (each(n, [128, D]) for n in ("y", "x1", "y2", "x2"))
        if layer == 0:
            self.lat, self.moe = each("lat", [128, 2, 128]), each("moe", [128, 2, 128])
            self.hid, self.hsq = each("hid", [128, NI, 128]), each("hsq", [128, NI, 128])
            self.top, self.wsum = each("top", [128, 8]), each("wsum", [128, 1])
            self.t1, self.f = each("t1", [128, D]), each("f", [128, D])
        else:
            self.lg, self.top = each("lg", [128, 8]), each("top", [128, 8])
            self.gt, self.eq = each("gt", [128, NE, NE]), each("eq", [128, NE, NE])
            self.rank, self.ex = each("rank", [128, NE]), each("ex", [128, NE])
            self.gs, self.gr = each("gs", [128, 1]), each("gr", [128, 1])
            self.mid = each("mid", [128, 128 // R, R])
            self.midT = each("midT", [NE * R, 128])
        self.bank = [[a.ps(f"bank{u}_{n}") for n in range(4)] for u in range(T)]
        self.w_in, self.setup = [a.sem(f"w_in{n}") for n in range(len(self.loads))], a.sem("setup")
        self.n_setup = T + 1 + (1 if layer == 1 else 0)
        self.x_in = [a.sem(f"x_in{u}") for u in range(T)]
        self.x_out = [a.sem(f"x_out{u}") for u in range(T)]
        names = ["aT_ps", "aT_sb", "y_ps", "y_sb", "x1_sb", "x1T_ps", "x1T_sb", "x2_sb", "chain_dve"]
        names += ["lat_ps", "lat_sb", "moe_ps", "moe_sb", "up_ps", "hid_sb", "hsq_sb", "logit_ps", "top_sb", "down_ps",
                  "routed_ps", "f_sb", "t1_sb"] if layer == 0 else \
                 ["mid_ps", "lg_sb", "ex_sb", "mid_sb", "midT_ps", "midT_sb", "delta_ps"]
        self.s = {n: a.sem(n) for n in names}
        self.norm = Norm(nc, a, self.eps, T)
        self.pad = a.sb("pad", [1, T + 1])
        self.NN = 3 if layer == 0 else 2
        self.programs = {"sync": self.sync, "tensor": self.tensor, "scalar": self.scalar,
                         "vector": self.vector, "gpsimd": self.gpsimd}

    def count(self, i, norm, u):
        return self.NN * self.T * i + self.T * norm + u + 1

    def weights(self, eng, *which):
        for n in which:
            eng.wait_ge(self.w_in[n], 16)

    def load(self, sp, n, u):
        sp.dma_start(self.x[u][:, :], self.scr["x"][self.layer, n]).then_inc(self.x_in[u], 16)
        for b in range(2):
            sp.dma_start(self.at[u][b * SP_:b * SP_ + S, :], self.scr["att"][2 * n + b]).then_inc(self.x_in[u], 16)

    def setup_sync(self, sp):
        sp.dma_start(*self.loads[0]).then_inc(self.w_in[0], 16)
        sp.wait_ge(self.setup, self.T)
        for u in range(self.T):
            self.load(sp, u, u)
        for n in range(1, len(self.loads)):
            sp.dma_start(*self.loads[n]).then_inc(self.w_in[n], 16)

    def sync(self, sp, i):
        T, s = self.T, self.s
        yield 5.5
        if not is_last(self, i):
            for u in range(T):
                sp.wait_ge(s["y_sb"], T * i + u + 1)
                self.load(sp, T * i + T + u, u)
        yield 27.5
        if self.out is not None:
            for u in range(T):
                n = T * i + u
                sp.wait_ge(s["x2_sb"], n + 1)
                for b in range(2):
                    sp.dma_start(self.out[2 * T * i + 2 * u + b], self.x2[u][b * SP_:b * SP_ + S, :]).then_inc(self.x_out[u], 16)

    def finish_sync(self, sp):
        if self.out is not None:
            for u in range(self.T):
                sp.wait_ge(self.x_out[u], 32 * self.rounds)

    def setup_tensor(self, pe):
        pass

    def tensor(self, pe, i):
        T, s, bank, NI = self.T, self.s, self.bank, self.NI
        first = isinstance(i, int) and i == 0

        def transposed(src, dst, done):
            for k in range(KC):
                mm = pe.transpose(dst[:, k * 128:(k + 1) * 128], src[:, k * 128:(k + 1) * 128], self.ident[:, :])
            mm.then_inc(done, 1)

        def product(dst, moving, weights, n, done):
            for k in range(n):
                mm = pe.matmul(dst, moving(k), weights(k), start=(k == 0), stop=(k == n - 1))
            if done is not None:
                mm.then_inc(done, 1)

        yield 1.5
        if first:
            self.weights(pe, 0)
        for u in range(T):
            pe.wait_ge(self.x_in[u], 48 * i + 48)
            transposed(self.at[u], bank[u][0], s["aT_ps"])
        yield 3.5
        if first:
            self.weights(pe, 1)
        for u in range(T):
            pe.wait_ge(s["aT_sb"], T * i + u + 1)
            product(bank[u][1][:, :], lambda k: self.aT[u][:, k, :], lambda k: self.wo[:, k, :], KC, s["y_ps"])
        yield 7.5
        for u in range(T):
            pe.wait_ge(s["x1_sb"], T * i + u + 1)
            transposed(self.x1[u], bank[u][2], s["x1T_ps"])
        if self.layer == 0:
            for part in range(2):
                yield 9.5 + 2 * part
                if first:
                    self.weights(pe, *((2, 4) if part == 0 else (3,)))
                for u in range(T):
                    pe.wait_ge(s["x1T_sb"], T * i + u + 1)
                    if part == 0:
                        for t in range(2):
                            product(bank[u][3][:, t * 128:(t + 1) * 128], lambda k: self.fc1[:, k, t * 128:(t + 1) * 128],
                                    lambda k: self.xT[u][:, k, :], KC, s["lat_ps"] if t == 1 else None)
                    else:
                        for t in range(NI):
                            product(bank[u][1 + t // 4][:, (t % 4) * 128:(t % 4 + 1) * 128],
                                    lambda k: self.up[:, k, t * 128:(t + 1) * 128],
                                    lambda k: self.xT[u][:, k, :], KC, s["up_ps"] if t % 4 == 3 else None)
            yield 13.5
            if first:
                self.weights(pe, 5)
            for u in range(T):
                pe.wait_ge(s["lat_sb"], T * i + u + 1)
                product(bank[u][3][:, 0:8], lambda k: self.xT[u][:, k, :], lambda k: self.gate[:, k, :], KC, s["logit_ps"])
                for t in range(2):
                    product(bank[u][0][:, t * 128:(t + 1) * 128], lambda k: self.expert[:, k, t * 128:(t + 1) * 128],
                            lambda k: self.lat[u][:, k, :], 2, s["moe_ps"] if t == 1 else None)
            yield 17.5
            if first:
                self.weights(pe, 6, 7)
            for u in range(T):
                pe.wait_ge(s["moe_sb"], T * i + u + 1)
                pe.wait_ge(s["hsq_sb"], T * i + u + 1)
                product(bank[u][0][:, :], lambda k: self.hsq[u][:, k, :], lambda k: self.down[:, k, :], NI, s["down_ps"])
                pe.wait_ge(s["top_sb"], T * i + u + 1)
                product(bank[u][3][:, :], lambda k: self.moe[u][:, k, :], lambda k: self.fc2[:, k, :], 2, s["routed_ps"])
        else:
            MR = self.NE * self.R
            yield 9.5
            if first:
                self.weights(pe, 2)
            for u in range(T):
                pe.wait_ge(s["x1T_sb"], T * i + u + 1)
                product(bank[u][3][:, 0:MR + self.NE], lambda k: self.xT[u][:, k, :], lambda k: self.wr[:, k, :], KC, s["mid_ps"])
            yield 13.5
            for u in range(T):
                pe.wait_ge(s["mid_sb"], 4 * (T * i + u) + 4)
                pe.transpose(bank[u][0][:, 0:128], self.mid[u][:, :, :].rearrange("p a b -> p (a b)"),
                             self.ident[:, :]).then_inc(s["midT_ps"], 1)
            yield 15.5
            if first:
                self.weights(pe, 3)
            for u in range(T):
                pe.wait_ge(s["midT_sb"], T * i + u + 1)
                pe.matmul(bank[u][1][:, :], self.midT[u][:, :], self.lb[:, :], start=True, stop=True).then_inc(s["delta_ps"], 1)

    def setup_vector(self, dve):
        nc = self.nc
        for u in range(self.T):
            nc.vector.memset(self.at[u][:, :], 0.0).then_inc(self.setup, 1)
        nc.vector.memset(self.eps[:, :], 1e-5).then_inc(self.setup, 1)
        if self.layer == 1:
            for u in range(self.T):
                nc.vector.memset(self.mid[u][:, :, :], 0.0)
                last = nc.vector.memset(self.lg[u][:, :], NEG)
            last.then_inc(self.setup, 1)
        dve.wait_ge(self.setup, self.n_setup)
        self.chain = Chain(dve, self.s["chain_dve"], self.T * (2 * self.NN + (3 if self.layer == 0 else 8)), self.pad)

    def vector(self, dve, i):
        nc, T, s, bank, chain, norm = self.nc, self.T, self.s, self.bank, self.chain, self.norm
        NE, R = self.NE, self.R
        first = isinstance(i, int) and i == 0
        chain.start, chain.k = chain.per_round * i, 0
        yield 2.5
        for u in range(T):
            dve.wait_ge(s["aT_ps"], T * i + u + 1)
            nc.vector.tensor_copy(self.aT[u][:, :, :], bank[u][0][:, :].rearrange("p (c t) -> p c t", c=KC)).then_inc(s["aT_sb"], 1)
        yield 4.5
        for u in range(T):
            y = self.y[u]
            dve.wait_ge(s["y_ps"], T * i + u + 1)
            nc.vector.tensor_tensor(y[:, :], bank[u][1][:, :], self.x[u][:, :], ALU.add).then_inc(s["y_sb"], 1)
            dve.wait_ge(s["y_sb"], T * i + u + 1)
            norm.statistics(chain, u, y[:, :])
        yield 6.5
        for u in range(T):
            norm.apply(dve, chain, u, self.x1[u][:, :], self.y[u][:, :], self.count(i, 0, u)).then_inc(s["x1_sb"], 1)
        yield 8.5
        for u in range(T):
            dve.wait_ge(s["x1T_ps"], T * i + u + 1)
            nc.vector.tensor_copy(self.xT[u][:, :, :], bank[u][2][:, :].rearrange("p (c t) -> p c t", c=KC)).then_inc(s["x1T_sb"], 1)
        if self.layer == 0:
            yield 14.5
            for u in range(T):
                n, top = T * i + u, self.top[u]
                dve.wait_ge(s["logit_ps"], n + 1)
                chain.carry(u)
                chain.link(nc.vector.max(top[:, :], bank[u][3][:, 0:8]))
                nc.vector.tensor_tensor(self.wsum[u][:, :], top[:, 0:1], top[:, 1:2], ALU.add).then_inc(s["top_sb"], 1)
                dve.wait_ge(s["hid_sb"], n + 1)
                nc.vector.tensor_tensor(self.hsq[u][:, :, :], self.hid[u][:, :, :], self.hid[u][:, :, :], ALU.mult).then_inc(s["hsq_sb"], 1)
            yield 18.5
            if first:
                self.weights(dve, 8, 9)
            for u in range(T):
                n, f = T * i + u, self.f[u]
                dve.wait_ge(s["routed_ps"], n + 1)
                nc.vector.tensor_scalar(self.t1[u][:, :], bank[u][3][:, :], self.wsum[u][:, 0:1], None, ALU.mult).then_inc(s["t1_sb"], 1)
                dve.wait_ge(s["t1_sb"], n + 1)
                chain.link(nc.vector.tensor_tensor(f[:, :], bank[u][0][:, :], self.t1[u][:, :], ALU.add))
                norm.statistics(chain, u, f[:, :])
            yield 20.5
            for u in range(T):
                n, f = T * i + u, self.f[u]
                norm.apply(dve, chain, u, f[:, :], f[:, :], self.count(i, 1, u)).then_inc(s["f_sb"], 1)
                dve.wait_ge(s["f_sb"], 3 * n + 1)
                nc.vector.tensor_tensor(f[:, :], f[:, :], self.gamma[:, :], ALU.mult).then_inc(s["f_sb"], 1)
                dve.wait_ge(s["f_sb"], 3 * n + 2)
                nc.vector.tensor_tensor(f[:, :], f[:, :], self.beta[:, :], ALU.add).then_inc(s["f_sb"], 1)
                dve.wait_ge(s["f_sb"], 3 * n + 3)
                chain.link(nc.vector.tensor_tensor(self.y2[u][:, :], f[:, :], self.x1[u][:, :], ALU.add))
                norm.statistics(chain, u, self.y2[u][:, :])
        else:
            yield 10.5
            if first:
                self.weights(dve, 4)
            for u in range(T):
                lg, gt, eq = self.lg[u], self.gt[u], self.eq[u]
                dve.wait_ge(s["mid_ps"], T * i + u + 1)
                chain.link(nc.vector.tensor_copy(lg[:, 0:NE], bank[u][3][:, NE * R:NE * R + NE]))
                chain.carry(u)
                chain.link(nc.vector.max(self.top[u][:, :], lg[:, :]))
                nc.vector.tensor_scalar(self.ex[u][:, :], lg[:, 0:NE], self.top[u][:, 0:1], None, ALU.subtract).then_inc(s["lg_sb"], 1)
                mine = lg[:, 0:NE].unsqueeze(2).to_broadcast([128, NE, NE])
                other = lg[:, 0:NE].unsqueeze(1).to_broadcast([128, NE, NE])
                chain.link(nc.vector.tensor_tensor(gt[:, :, :], other, mine, ALU.is_gt))
                chain.link(nc.vector.tensor_tensor(eq[:, :, :], other, mine, ALU.is_equal))
                chain.link(nc.vector.tensor_tensor(eq[:, :, :], eq[:, :, :], self.lower[:, :, :], ALU.mult))
                chain.link(nc.vector.tensor_tensor(gt[:, :, :], gt[:, :, :], eq[:, :, :], ALU.add))
                chain.link(nc.vector.tensor_reduce(self.rank[u][:, :], gt[:, :, :], AX.X, ALU.add))
            yield 12.5
            for u in range(T):
                n, ex = T * i + u, self.ex[u]
                dve.wait_ge(s["ex_sb"], n + 1)
                nc.vector.scalar_tensor_tensor(out=ex[:, :], in0=self.rank[u][:, :], scalar=1.5, in1=ex[:, :],
                                               op0=ALU.is_lt, op1=ALU.mult, accum_out=self.gs[u][:, :]).then_inc(s["mid_sb"], 1)
                dve.wait_ge(s["mid_sb"], 4 * n + 1)
                nc.vector.reciprocal(self.gr[u][:, :], self.gs[u][:, :]).then_inc(s["mid_sb"], 1)
                dve.wait_ge(s["mid_sb"], 4 * n + 2)
                nc.vector.tensor_scalar(ex[:, :], ex[:, :], self.gr[u][:, 0:1], None, ALU.mult).then_inc(s["mid_sb"], 1)
                dve.wait_ge(s["mid_sb"], 4 * n + 3)
                nc.vector.tensor_tensor(self.mid[u][:, 0:NE, :], bank[u][3][:, 0:NE * R].rearrange("p (e r) -> p e r", e=NE),
                                        ex[:, :].unsqueeze(2).to_broadcast([128, NE, R]), ALU.mult).then_inc(s["mid_sb"], 1)
            yield 14.5
            for u in range(T):
                dve.wait_ge(s["midT_ps"], T * i + u + 1)
                nc.vector.tensor_copy(self.midT[u][:, :], bank[u][0][0:NE * R, 0:128]).then_inc(s["midT_sb"], 1)
            yield 20.5
            for u in range(T):
                dve.wait_ge(s["delta_ps"], T * i + u + 1)
                chain.link(nc.vector.scalar_tensor_tensor(out=self.y2[u][:, :], in0=bank[u][1][:, :], scalar=4.0, in1=self.x1[u][:, :],
                                                          op0=ALU.mult, op1=ALU.add))
                norm.statistics(chain, u, self.y2[u][:, :])
        yield 25.5
        for u in range(T):
            if self.out is None:
                ge(dve, self.x2_used, T * i + u)
            else:
                ge(dve, self.x_out[u], 32 * i)
            norm.apply(dve, chain, u, self.x2[u][:, :], self.y2[u][:, :], self.count(i, self.NN - 1, u)).then_inc(s["x2_sb"], 1)
        assert chain.k == chain.per_round, (chain.k, chain.per_round)

    def setup_scalar(self, act):
        act.wait_ge(self.setup, self.n_setup)

    def scalar(self, act, i):
        nc, T, s, bank = self.nc, self.T, self.s, self.bank
        yield 5.5
        for u in range(T):
            self.norm.root(act, u, self.count(i, 0, u))
        if self.layer == 0:
            yield 10.5
            for u in range(T):
                act.wait_ge(s["lat_ps"], T * i + u + 1)
                nc.scalar.activation(self.lat[u][:, :, :], bank[u][3][:, 0:256].rearrange("p (a t) -> p a t", a=2), ACT.Copy).then_inc(s["lat_sb"], 1)
            yield 12.5
            for u in range(T):
                n = T * i + u
                for c in range(2):
                    act.wait_ge(s["up_ps"], 2 * n + c + 1)
                    last = nc.scalar.activation(self.hid[u][:, 4 * c:4 * c + 4, :], bank[u][1 + c][:, :].rearrange("p (a t) -> p a t", a=4), ACT.Relu)
                last.then_inc(s["hid_sb"], 1)
            yield 14.5
            for u in range(T):
                act.wait_ge(s["moe_ps"], T * i + u + 1)
                nc.scalar.activation(self.moe[u][:, :, :], bank[u][0][:, 0:256].rearrange("p (a t) -> p a t", a=2), ACT.Copy).then_inc(s["moe_sb"], 1)
            yield 19.5
            for u in range(T):
                self.norm.root(act, u, self.count(i, 1, u))
        else:
            yield 11.5
            for u in range(T):
                act.wait_ge(s["lg_sb"], T * i + u + 1)
                nc.scalar.activation(self.ex[u][:, :], self.ex[u][:, :], ACT.Exp).then_inc(s["ex_sb"], 1)
        yield 21.5
        for u in range(T):
            self.norm.root(act, u, self.count(i, self.NN - 1, u))

    def gpsimd(self, pool, i):
        return iter(())


def woven_phase(nc, ctx, parts, rounds):
    block = ctx.enter_context(nc.Block())

    @block.sync
    def _(sp):
        for p in parts:
            p.setup_sync(sp)
        run_rounds(sp, "sync", parts, rounds)
        for p in parts:
            p.finish_sync(sp)

    @block.tensor
    def _(pe):
        for p in parts:
            p.setup_tensor(pe)
        run_rounds(pe, "tensor", parts, rounds)

    @block.scalar
    def _(act):
        for p in parts:
            p.setup_scalar(act)
        run_rounds(act, "scalar", parts, rounds)

    @block.vector
    def _(dve):
        for p in parts:
            p.setup_vector(dve)
        run_rounds(dve, "vector", parts, rounds)

    @block.gpsimd
    def _(pool):
        run_rounds(pool, "gpsimd", parts, rounds)


def context_and_self_attention(nc, io, scr):
    with ExitStack() as ctx:
        parts = [ContextProjection(nc, Arena(nc, ctx, "kv"), io, scr),
                 SelfAttention(nc, Arena(nc, ctx, "sa0"), io, scr, 0, 0, x_src=io["x"])]
        woven_phase(nc, ctx, parts, TILES)


def after_cross_and_self_attention(nc, io, scr):
    with ExitStack() as ctx:
        ff = AfterCross(nc, Arena(nc, ctx, "ff0"), io, scr, 0, 1, None)
        sa = SelfAttention(nc, Arena(nc, ctx, "sa1"), io, scr, 1, 1, x_tile=ff.x2[0], x_ready=ff.s["x2_sb"])
        ff.x2_used = sa.s["y_sb"]
        woven_phase(nc, ctx, [ff, sa], TILES + 1)


def last_after_cross(nc, io, scr, out):
    with ExitStack() as ctx:
        ff = AfterCross(nc, Arena(nc, ctx, "ff1"), io, scr, 1, 2, out)
        woven_phase(nc, ctx, [ff], ff.rounds)



def cross_attention(nc, io, scr, layer):
    NU = 2 * 2 * NCH
    with ExitStack() as ctx:
        a = Arena(nc, ctx, f"xa{layer}")
        masked = layer == 1
        GS = 1 if masked else 2
        NS, SW = G // GS, GS * QG
        TR = GS * HD
        ZR = 3 * TR + (S if masked else 0)
        KR = ZR + 2
        kst = [a.sb(f"kst{u}", [KR, NS, SK], F16) for u in range(U)]
        qst = [a.sb(f"qst{u}", [KR, NS, SW], F16) for u in range(U)]
        v = [a.sb(f"v{u}", [CH, VW]) for u in range(U)]
        PR, SR, MR = 6, 3, 2
        p = a.sb("p", [CH, PR, QP])
        mxp = [a.sb(f"mxp{h}", [112, 8, PT]) for h in range(2)]
        mneg = [a.sb(f"mneg{h}", [112, 8]) for h in range(2)]
        mhi = [a.sb(f"mhi{h}", [8, 112], F16) for h in range(2)]
        mlo = [a.sb(f"mlo{h}", [8, 112], F16) for h in range(2)]
        osb = [a.sb(f"osb{h}", [128, QG]) for h in range(2)]
        rden = [a.sb(f"rden{h}", [112, 2, 4, 1]) for h in range(2)]
        att = [a.sb(f"att{h}", [112, 2, 4, HD]) for h in range(2)]
        ident = a.sb("ident", [128, 128])
        if masked:
            mask_u8 = a.sb("mask_u8", [S, SK], U8)
            keep = a.sb("keep", [S, SK])
            maxkeep = a.sb("maxkeep", [S, 1])
            kmask = a.sb("kmask", [S, SK], F16)
            qsel = a.sb("qsel", [S, QG], F16)
            mask_rows = a.sem("mask_rows")
        sps = [a.ps(f"sps{n}") for n in range(SR)]
        mps = [a.ps(f"mps{n}") for n in range(MR)]
        ops = [a.ps(f"ops{h}") for h in range(2)]
        tps = a.ps("tps")

        c_in, cleared, setup = a.sem("c_in"), a.sem("cleared"), a.sem("setup")
        k_in = [[a.sem(f"k_in{u}_{h}") for h in range(2)] for u in range(U)]
        v_in = [a.sem(f"v_in{u}") for u in range(U)]
        m_in = [[a.sem(f"m_in{u}_{h}") for h in range(2)] for u in range(U)]
        s_ps, p_sb, pv = a.sem("s_ps"), a.sem("p_sb"), a.sem("pv")
        m_ps, m_red, mneg_sb, mT_ps, mhi_sb, mlo_sb = (a.sem(n) for n in ("m_ps", "m_red", "mneg_sb", "mT_ps", "mhi_sb", "mlo_sb"))
        o_sb, oT_ps, rden_sb, att_sb = (a.sem(n) for n in ("o_sb", "oT_ps", "rden_sb", "att_sb"))
        att_out = [a.sem(f"att_out{h}") for h in range(2)]
        block = ctx.enter_context(nc.Block())
        KQ_DMAS = 3 + 3 * GS

        def load_kq(sp, n, i, u, h):
            stacks = slice(h * NS // 2, (h + 1) * NS // 2)
            for r, part in enumerate((0, 0, 1)):
                sp.dma_start(kst[u][TR * r:TR * r + TR, stacks, :],
                             scr["k"][n, part, layer].rearrange("(a r) t -> r a t", r=TR)[:, stacks, :]
                             ).then_inc(k_in[u][h], 16)
            for r, part in enumerate((0, 1, 0)):
                for g in range(GS):
                    rows = slice(TR * r + HD * g, TR * r + HD * g + HD)
                    sp.dma_start(qst[u][rows, stacks, g * QG:(g + 1) * QG],
                                 scr["q"][part, n].rearrange("(a g r) c -> g r a c", g=GS, r=HD)[g, :, stacks, :]
                                 ).then_inc(k_in[u][h], 16)

        def held(eng, value):
            return value if isinstance(value, int) else eng.snap(value)

        def windows(eng, one):
            for u in range(U):
                one(u, 0, u, True, False)
            with eng.Fori(1, B // U - 1) as i:
                for u in range(U):
                    one(U * i + u, i, u, False, False)
            for u in range(U):
                one(B - U + u, B // U - 1, u, False, u == U - 1)

        @block.sync
        def _(sp):
            sp.dma_start(ident[:, :], io["ident"]).then_inc(c_in, 16)
            if masked:
                sp.dma_start(mask_u8[:, :], io["mask"]).then_inc(c_in, 16)
            sp.wait_ge(cleared, U * GS)
            for u in range(U):
                for h in range(2):
                    load_kq(sp, u, 0, u, h)
                sp.dma_start(v[u][:, :], scr["v"][layer, u]).then_inc(v_in[u], 16)
            if masked:
                sp.wait_ge(setup, 4)
                for u in range(U):
                    for dst, src, width in ((kst[u], kmask, SK), (qst[u], qsel, QG)):
                        sp.dma_start(dst[3 * TR:ZR, :, :], src[:, :].unsqueeze(1).to_broadcast([S, NS, width])).then_inc(mask_rows, 16)

            def maximum_out(wb, ub, h):
                for row, (ready, m) in enumerate(((mhi_sb, mhi), (mlo_sb, mlo))):
                    sp.wait_ge(ready, 2 * wb + h + 1)
                    sp.dma_start(qst[ub][ZR + row:ZR + row + 1, h * NS // 2:(h + 1) * NS // 2, :].rearrange("o a (t c) -> o (a t) c", c=112),
                                 m[h][:, :]).then_inc(m_in[ub][h], 16)

            def attention_out(w, h):
                sp.wait_ge(att_sb, 2 * w + h + 1)
                for j2 in range(2):
                    sp.dma_start(scr["att"][w, :, j2 * 256 + h * 128:j2 * 256 + (h + 1) * 128],
                                 att[h][j2 * S:(j2 + 1) * S, :, :, :].rearrange("p a b c -> p (a b c)")).then_inc(att_out[h], 16)

            def window(w, i, u, first, last):
                more = not (isinstance(w, int) and w >= B - U)
                maximum_out(w, u, 1)
                if not (first and u == 0):
                    attention_out(w - 1, 1)
                if more:
                    sp.wait_ge(s_ps, NU * w + NU // 2)
                    load_kq(sp, w + 2, i + 1, u, 0)
                if not last:
                    maximum_out(w + 1, 1 - u, 0)
                attention_out(w, 0)
                if more:
                    sp.wait_ge(s_ps, NU * w + NU)
                    load_kq(sp, w + 2, i + 1, u, 1)
                    sp.wait_ge(pv, 2 * NCH * (w + 1))
                    sp.dma_start(v[u][:, :], scr["v"][layer, w + 2]).then_inc(v_in[u], 16)

            maximum_out(0, 0, 0)
            windows(sp, window)
            attention_out(B - 1, 1)
            for h in range(2):
                sp.wait_ge(att_out[h], 32 * B)

        @block.tensor
        def _(pe):
            pe.wait_ge(c_in, 32 if masked else 16)
            pe.wait_ge(cleared, U * GS)
            if masked:
                pe.wait_ge(mask_rows, 64)

            def maximum_unit(wb, m0, ib, ub, n):
                t, part = n // PT, n % PT
                h = t // 8
                if n % (8 * PT) == 0:
                    pe.wait_ge(k_in[ub][h], 16 * KQ_DMAS * (ib + 1))
                if not (isinstance(wb, int) and wb == 0 and n < MR):
                    pe.wait_ge(m_red, m0 + n + 1 - MR)
                tt = t % 8
                stack, c = h * NS // 2 + tt * 112 // SW, tt * 112 % SW
                pe.matmul(mps[n % MR][0:112, 0:NP], qst[ub][0:ZR, stack, c:c + 112],
                          kst[ub][0:ZR, stack, part * NP:(part + 1) * NP], start=True, stop=True).then_inc(m_ps, 1)

            def maxima_transposed(wb, h):
                pe.wait_ge(mneg_sb, 2 * wb + h + 1)
                if not isinstance(wb, int) or 2 * wb + h > 2:
                    pe.wait_ge(att_sb, 2 * wb + h - 2)
                elif 2 * wb + h > 0:
                    pe.wait_ge(mlo_sb, 2 * wb + h)
                pe.transpose(tps[0:8, 0:112], mneg[h][:, :], ident[0:112, 0:112]).then_inc(mT_ps, 1)

            def output_transposed(w, h, after_output=False):
                pe.wait_ge(o_sb, 2 * w + h + 1)
                if after_output:
                    pe.wait_ge(att_sb, 2 * w + h)
                else:
                    pe.wait_ge(mlo_sb, 2 * w + h + 3)
                for jh in range(2):
                    mm = pe.transpose(tps[0:112, jh * 128:(jh + 1) * 128], osb[h][:, jh * 112:(jh + 1) * 112], ident[:, :])
                mm.then_inc(oT_ps, 1)

            def pv_step(w, p0, i, u, cs):
                h, k = cs // NCH, cs % NCH
                if k == 0:
                    if h == 0:
                        pe.wait_ge(v_in[u], 16 * (i + 1))
                    if not (isinstance(w, int) and w == 0):
                        pe.wait_ge(o_sb, 2 * w + h - 1)
                pe.wait_ge(p_sb, p0 + 2 * cs + 2)
                for c in range(4):
                    unit = 2 * cs + c // 2
                    g = 4 * h + c
                    mm = pe.matmul(ops[h][32 * c:32 * c + 32, 0:QG],
                                   v[u][:, (k * G + g) * VS:(k * G + g) * VS + 32],
                                   p[:, unit % PR, (c % 2) * QG:(c % 2 + 1) * QG],
                                   start=(k == 0), stop=(k == NCH - 1))
                mm.then_inc(pv, 1)

            def window(w, i, u, first, last):
                s0, m0, p0 = held(pe, NU * w), held(pe, NU * w + NU), held(pe, NU * w)
                for cs in range(2 * NCH):
                    h, k = cs // NCH, cs % NCH
                    if k == 0:
                        pe.wait_ge(m_in[u][h], 32 * (i + 1))
                    for pr in range(2):
                        n = 2 * cs + pr
                        if not (first and u == 0 and n < SR):
                            pe.wait_ge(p_sb, s0 + n + 1 - SR)
                        ch = slice(k * CH, (k + 1) * CH)
                        for c in range(2 // GS):
                            stack = (2 * h + pr) * 2 // GS + c
                            mm = pe.matmul(sps[n % SR][0:CH, c * SW:(c + 1) * SW], kst[u][:, stack, ch], qst[u][:, stack, :],
                                           start=True, stop=True)
                        mm.then_inc(s_ps, 1)
                        if not last:
                            maximum_unit(w + 1, m0, i if u == 0 else i + 1, 1 - u, n)
                    if cs > 0:
                        pv_step(w, p0, i, u, cs - 1)
                    elif not (first and u == 0):
                        pv_step(w - 1, p0 - NU, i - (1 - u), 1 - u, 2 * NCH - 1)
                    if cs == 2:
                        maxima_transposed(w, 1)
                    if cs == 4 and not (first and u == 0):
                        output_transposed(w - 1, 1)
                    if cs == 14 and not last:
                        maxima_transposed(w + 1, 0)
                    if cs == 16:
                        output_transposed(w, 0, after_output=last)

            for n in range(NU):
                maximum_unit(0, 0, 0, 0, n)
                if n == 30:
                    maxima_transposed(0, 0)
            windows(pe, window)
            pv_step(B - 1, NU * (B - 1), B // U - 1, U - 1, 2 * NCH - 1)
            output_transposed(B - 1, 1, after_output=True)

        @block.scalar
        def _(act):
            def output_copy(w, h):
                act.wait_ge(pv, 2 * NCH * w + NCH * (h + 1))
                if not (isinstance(w, int) and w == 0):
                    act.wait_ge(oT_ps, 2 * w + h - 1)
                nc.scalar.activation(osb[h][:, :], ops[h][:, 0:QG], ACT.Copy).then_inc(o_sb, 1)

            def window(w, i, u, first, last):
                s0, v0 = held(act, NU * w), held(act, 2 * NCH * w)
                for n in range(NU):
                    act.wait_ge(s_ps, s0 + n + 1)
                    if not (first and u == 0 and n < PR):
                        act.wait_ge(pv, v0 + (n - PR) // 2 + 1)
                    nc.scalar.activation(p[:, n % PR, :], sps[n % SR][0:CH, 0:QP], ACT.Exp).then_inc(p_sb, 1)
                    if n == 3 and not (first and u == 0):
                        output_copy(w - 1, 1)
                    if n == 2 * NCH + 3:
                        output_copy(w, 0)

            windows(act, window)
            output_copy(B - 1, 1)

        @block.vector
        def _(dve):
            for u in range(U):
                nc.vector.memset(kst[u][96:KR, :, :], WSCALE).then_inc(cleared, 1)
                if not masked:
                    nc.vector.memset(qst[u][:, :, :], 0.0).then_inc(cleared, 1)
            dve.wait_ge(c_in, 32 if masked else 16)
            if masked:
                nc.vector.tensor_copy(keep[:, :], mask_u8[:, :]).then_inc(setup, 1)
                dve.wait_ge(setup, 1)
                nc.vector.reduce_max(maxkeep[:, :], keep[:, :], AX.X).then_inc(setup, 1)
                dve.wait_ge(setup, 2)
                nc.vector.tensor_scalar(kmask[:, :], keep[:, :], maxkeep[:, 0:1], BIG, ALU.subtract, ALU.mult).then_inc(setup, 1)
                nc.vector.tensor_scalar(qsel[:, :].rearrange("p (h q) -> p h q", q=S),
                                        ident[0:S, 0:S].unsqueeze(1).to_broadcast([S, J, S]), BIG, None, ALU.mult).then_inc(setup, 1)

            def maximum(wb, m0, r0, n):
                t, part = n // PT, n % PT
                h, tt = t // 8, t % 8
                dve.wait_ge(m_ps, m0 + n + 1)
                dst = mxp[h][:, tt, part:part + 1]
                src = mps[n % MR][0:112, 0:NP]
                nc.vector.tensor_reduce(dst, src, AX.X, ALU.max).then_inc(m_red, 1)
                if n % (8 * PT) == 8 * PT - 1:
                    dve.wait_ge(m_red, r0 + n + 1)
                    if not (isinstance(wb, int) and wb == 0):
                        dve.wait_ge(mT_ps, 2 * wb + h - 1)
                    nc.vector.tensor_reduce(mneg[h][:, :], mxp[h][:, :, :], AX.X, ALU.max, negate=True).then_inc(mneg_sb, 1)

            def maximum_rows(wb, ib, ub, h):
                dve.wait_ge(mT_ps, 2 * wb + h + 1)
                if not (isinstance(wb, int) and wb == 0):
                    ge(dve, m_in[1 - ub][h], 32 * (ib + ub))
                nc.vector.tensor_scalar(mhi[h][:, :], tps[0:8, 0:112], 1.0 / WSCALE, None, ALU.mult).then_inc(mhi_sb, 1)
                dve.wait_ge(mhi_sb, 2 * wb + h + 1)
                nc.vector.scalar_tensor_tensor(out=mlo[h][:, :], in0=tps[0:8, 0:112], scalar=1.0 / WSCALE, in1=mhi[h][:, :],
                                               op0=ALU.mult, op1=ALU.subtract).then_inc(mlo_sb, 1)

            def output_scaled(w, i, h):
                o = tps[0:112, 0:256].rearrange("p (j c v) -> p j c v", j=2, c=4)
                dve.wait_ge(oT_ps, 2 * w + h + 1)
                nc.vector.reciprocal(rden[h][:, :, :, :], o[:, :, :, HD:HD + 1]).then_inc(rden_sb, 1)
                dve.wait_ge(rden_sb, 2 * w + h + 1)
                ge(dve, att_out[h], 32 * w)
                nc.vector.tensor_tensor(att[h][:, :, :, :], o[:, :, :, 0:HD], rden[h][:, :, :, :].to_broadcast([112, 2, 4, HD]),
                                        ALU.mult).then_inc(att_sb, 1)

            def window(w, i, u, first, last):
                m0, r0 = held(dve, NU * w + NU), held(dve, NU * w + NU)
                for n in range(NU):
                    if not last:
                        maximum(w + 1, m0, r0, n)
                    if n == 5:
                        maximum_rows(w, i, u, 1)
                    if n == 9 and not (first and u == 0):
                        output_scaled(w - 1, i, 1)
                    if n == 29 and not last:
                        maximum_rows(w + 1, i if u == 0 else i + 1, 1 - u, 0)
                    if n == 33:
                        output_scaled(w, i, 0)

            for n in range(NU):
                maximum(0, 0, 0, n)
                if n == 30:
                    maximum_rows(0, 0, 0, 0)
            windows(dve, window)
            output_scaled(B - 1, B // U - 1, 1)


def decoder_kernel(nc, io, out):
    scr = {
        "k": nc.dram_tensor("scr_k", [B, 2, 2, 128, SK], F16, kind="Internal").ap(),
        "v": nc.dram_tensor("scr_v", [2, B, CH, VW], F32, kind="Internal").ap(),
        "q": nc.dram_tensor("scr_q", [2, B, 128, QG], F16, kind="Internal").ap(),
        "att": nc.dram_tensor("scr_att", [B, S, D], F32, kind="Internal").ap(),
        "x": nc.dram_tensor("scr_x", [2, TILES, 128, D], F32, kind="Internal").ap(),
    }
    context_and_self_attention(nc, io, scr)
    cross_attention(nc, io, scr, 0)
    after_cross_and_self_attention(nc, io, scr)
    cross_attention(nc, io, scr, 1)
    last_after_cross(nc, io, scr, out)


def layout(inputs, np):
    f = lambda n: np.asarray(inputs[n])
    g, j, d = np.meshgrid(np.arange(G), np.arange(J), np.arange(HD), indexing="ij")
    head = ((g * J + j) * HD + d)
    by_j = head.transpose(1, 0, 2).reshape(-1)
    rot_q = head[:, :, (np.arange(HD) + HD // 2) % HD].transpose(1, 0, 2).reshape(-1)
    kv = np.arange(128).reshape(G, HD)
    rot_k = kv[:, (np.arange(HD) + HD // 2) % HD].reshape(-1)
    stored = head.reshape(2, 4, 2, 2, HD).transpose(3, 0, 2, 1, 4).reshape(-1)
    x = f("x")
    xp = np.zeros((B, SP_, D), x.dtype)
    xp[:, :S] = x
    io = {"x": xp.reshape(TILES, 128, D), "ctxT": f("ctx_4096").transpose(0, 2, 1), "mask": f("mask_SxS2_bk0")}
    io["wkv"] = np.concatenate([f("L0_xattn_Wk"), f("L1_xattn_w_k").T, f("L0_xattn_Wv"), f("L1_xattn_w_v").T], axis=1)
    io["sa0_wq"], io["sa0_wk"] = f("L0_attn_Wq").T, f("L0_attn_Wk").T
    io["sa0_wv"], io["sa0_wo"] = f("L0_attn_Wv").T, f("L0_attn_Wo").T
    for n in ("bq", "bk", "bv", "bo"):
        b = f(f"L0_attn_{n}")
        io[f"sa0_{n}"] = b.reshape(KC, 128).T if n in ("bq", "bk") else b
    wq, wk = f("L1_attn_Wq"), f("L1_attn_Wk")
    io["sa1_wq"] = np.concatenate([wq[:, by_j], wq[:, rot_q]], axis=1)
    io["sa1_wk"] = np.concatenate([wk, wk[:, rot_k]], axis=1)
    io["sa1_wv"], io["sa1_wo"] = f("L1_attn_Wv"), f("L1_attn_Wo")[by_j, :]
    io["xa0_wq"], io["xa0_wo"] = f("L0_xattn_Wq")[:, by_j], f("L0_xattn_Wo")[stored, :]
    io["xa1_wq"], io["xa1_wo"] = f("L1_xattn_w_q").T[:, by_j], f("L1_xattn_w_out").T[stored, :]
    io["up"], io["down"], io["fc1"] = f("L0_ffn_up_w"), f("L0_ffn_down_w"), f("L0_ffn_fc1_w")
    io["expert"], io["fc2"], io["gate"] = f("L0_ffn_expert_w"), f("L0_ffn_fc2_w"), f("L0_ffn_gate_w")
    io["gamma"], io["beta"] = f("L0_ffn_ln_gamma"), f("L0_ffn_ln_beta")
    io["lora_a"] = np.concatenate([f("L1_ffn_A").reshape(-1, D), f("L1_ffn_router_w")], axis=0).T
    io["lora_b"] = f("L1_ffn_B").transpose(0, 2, 1).reshape(-1, D)
    io["ident"] = np.eye(128, dtype=np.float32)
    io["blockmask"] = np.repeat((np.arange(128)[:, None] // HD == np.arange(8)[None, :]).astype(np.float32), SP_, axis=1)
    q = np.arange(128)[:, None] % SP_
    k = np.arange(SP_)[None, :]
    io["causal"] = np.where((k <= q) & (k < S), 0.0, NEG).astype(np.float32)
    half = HD // 2
    freq = (1.0 / np.float32(10000.0) ** (np.arange(half, dtype=np.float32) / np.float32(half))).astype(np.float32)
    ang = np.arange(SP_, dtype=np.float32)[None, :] * freq[np.arange(128) % half][:, None]
    sign = np.where(np.arange(128) % HD < half, -1.0, 1.0).astype(np.float32)[:, None]
    cos, sin = np.cos(ang).astype(np.float32), (sign * np.sin(ang)).astype(np.float32)
    io["rope"] = np.concatenate([cos * np.float32(0.25), sin * np.float32(0.25), cos, sin], axis=1)
    io["lower"] = np.tile((np.arange(4)[None, :] < np.arange(4)[:, None]).astype(np.float32).reshape(1, -1), (128, 1))
    return {n: np.ascontiguousarray(v) for n, v in io.items()}


def kernel(**inputs):
    import numpy as _np
    import concourse.bacc as _bacc
    from concourse import mybir as _mybir
    from concourse.bass_utils import run_bass_kernel_spmd as _run

    nc = _bacc.Bacc("TRN2", target_bir_lowering=False, num_devices=1)
    io = layout(inputs, _np)
    arrays = {f"in_{n}": v for n, v in io.items()}
    aps = {n: nc.dram_tensor(f"in_{n}", list(v.shape), _mybir.dt.from_np(v.dtype), kind="ExternalInput").ap()
           for n, v in io.items()}
    out = nc.dram_tensor("out_x", [B, S, D], F32, kind="ExternalOutput").ap()
    decoder_kernel(nc, aps, out)
    r = _run(nc, [arrays], core_ids=[0])
    return r.results[0]["out_x"]
```

```python
from contextlib import ExitStack
from itertools import chain as join

import concourse.bass as bass
from concourse import mybir

F32 = mybir.dt.float32
F16 = mybir.dt.float16
BF16 = mybir.dt.bfloat16
U8 = mybir.dt.uint8
ALU = mybir.AluOpType
ACT = mybir.ActivationFunctionType
AX = mybir.AxisListType

B, S, D = 16, 56, 512
KC = D // 128
SK = 1500
CH, NCH = 125, 12
NP, PT = 500, 3
H, G, J, HD = 32, 8, 4, 16
SP_ = 64
TILES = B // 2
U = 2
QG = J * S
QP = 2 * QG
NEG = -1e30
BIG = 60000.0
WSCALE = 64.0
VS = HD + 1
VW = NCH * G * VS + 16


class Arena:

    def __init__(self, nc, ctx, tag):
        self.nc, self.ctx, self.tag, self.sems = nc, ctx, tag, []
        ctx.callback(self.give_back)

    def give_back(self):
        self.nc.clear_and_free_semaphores(self.sems)
        self.nc.all_engine_barrier()

    def sb(self, name, shape, dt=F32):
        return self.ctx.enter_context(self.nc.sbuf_tensor(f"{self.tag}_{name}", shape, dt))

    def ps(self, name, shape=(128, 512)):
        return self.ctx.enter_context(self.nc.psum_tensor(f"{self.tag}_{name}", list(shape), F32))

    def sem(self, name):
        self.sems.append(self.nc.alloc_semaphore(f"{self.tag}_{name}"))
        return self.sems[-1]


def ge(eng, sem, value):
    if not isinstance(value, int) or value > 0:
        eng.wait_ge(sem, value)


class Part:

    def __init__(self, programs, lag, rounds):
        self.programs, self.lag, self.rounds = programs, lag, rounds


def is_last(part, i):
    return isinstance(i, int) and i == part.rounds - 1


def run_rounds(eng, name, parts, rounds):
    def one(r):
        heads = []
        for p in parts:
            if not isinstance(r, int) or 0 <= r - p.lag < p.rounds:
                steps = p.programs[name](eng, r - p.lag)
                heads.append([next(steps, None), steps])
        while any(h[0] is not None for h in heads):
            h = min((h for h in heads if h[0] is not None), key=lambda h: h[0])
            h[0] = next(h[1], None)

    edge = 1 + max(p.lag for p in parts)
    for r in range(edge):
        one(r)
    if edge < rounds - edge:
        with eng.Fori(edge, rounds - edge) as r:
            one(r)
    for r in range(rounds - edge, rounds):
        one(r)


class Chain:

    def __init__(self, eng, sem, per_round, pad):
        self.eng, self.sem, self.per_round, self.pad = eng, sem, per_round, pad
        self.start, self.k = 0, 0

    def begin(self, i):
        self.start, self.k = self.per_round * i, 0

    def link(self, ins):
        self.k += 1
        ins.then_inc(self.sem, 1)
        self.eng.wait_ge(self.sem, self.start + self.k)

    def carry(self, u):
        self.eng.memset(self.pad[:, u:u + 1], 0.0)


def wcols(w):
    return w.rearrange("(c p) n -> p c n", p=128)


class ContextProjection:

    NK, NV = 2 * PT, NCH
    NB = 2
    lag, rounds = 0, B // 2
    SPLITS = (7, 10, 13, 16)

    def __init__(self, nc, a, io, scr):
        self.nc, self.io, self.scr = nc, io, scr
        self.ctx32 = a.sb("ctx32", [128, KC, SK])
        self.chi = [a.sb(f"chi{u}", [128, KC, SK], F16) for u in range(2)]
        self.clo = [a.sb(f"clo{u}", [128, KC, SK], F16) for u in range(2)]
        self.w32 = a.sb("w32", [128, KC, 512])
        self.whi = a.sb("whi", [128, KC, 512], F16)
        self.wlo = a.sb("wlo", [128, KC, 512], F16)
        self.khi = a.sb("khi", [128, 2, SK], F16)
        self.klo = a.sb("klo", [128, 2, SK], F16)
        self.vout = a.sb("vout", [CH, 2, VW])
        self.kps = [a.ps(f"kps{n}") for n in range(self.NB)]
        self.vps = [a.ps(f"vps{n}") for n in range(self.NB)]
        self.w_in, self.w_hi, self.w_lo = a.sem("w_in"), a.sem("w_hi"), a.sem("w_lo")
        self.ctx_in = [a.sem(f"ctx_in{k}") for k in range(KC)]
        self.hi_done, self.lo_done = a.sem("hi_done"), a.sem("lo_done")
        self.k_ps, self.k_hi, self.k_lo = a.sem("k_ps"), a.sem("k_hi"), a.sem("k_lo")
        self.v_ps, self.v_sb = a.sem("v_ps"), a.sem("v_sb")
        self.k_out, self.v_out, self.ones = a.sem("k_out"), a.sem("v_out"), a.sem("ones")
        self.programs = {"sync": self.sync, "tensor": self.tensor, "scalar": self.scalar,
                         "vector": self.vector, "gpsimd": self.gpsimd}

    def load_chunk(self, sp, n, k):
        sp.dma_start(self.ctx32[:, k, :], self.io["ctxT"][n, k * 128:(k + 1) * 128, :]).then_inc(self.ctx_in[k], 16)

    def setup_sync(self, sp):
        sp.dma_start(self.w32[:, :, :], wcols(self.io["wkv"])).then_inc(self.w_in, 16)
        for k in range(KC):
            self.load_chunk(sp, 0, k)

    def sync(self, sp, i):
        if isinstance(i, int) and i == 0:
            yield 0
            for k in range(KC):
                sp.wait_ge(self.lo_done, k + 1)
                self.load_chunk(sp, 1, k)
        for u in range(2):
            n = 2 * i + u
            yield 18 * u + self.NK + 2
            sp.wait_ge(self.k_lo, self.NK * n + self.NK)
            for part, k in enumerate((self.khi, self.klo)):
                sp.dma_start(self.scr["k"][n, part].rearrange("l p t -> p l t"), k[:, :, :]).then_inc(self.k_out, 16)
            if not is_last(self, i):
                for k, slot in enumerate(self.SPLITS):
                    yield 18 * u + slot + 1
                    sp.wait_ge(self.lo_done, KC * (n + 1) + k + 1)
                    self.load_chunk(sp, n + 2, k)
            yield 18 * u + 18.5
            sp.wait_ge(self.v_sb, self.NV * n + self.NV)
            for layer in range(2):
                sp.dma_start(self.scr["v"][layer, n], self.vout[:, layer, :]).then_inc(self.v_out, 16)

    def finish_sync(self, sp):
        sp.wait_ge(self.k_out, 32 * B)
        sp.wait_ge(self.v_out, 32 * B)

    def setup_tensor(self, pe):
        pe.wait_ge(self.w_hi, KC)
        pe.wait_ge(self.w_lo, KC)

    def tensor(self, pe, i):
        for u in range(2):
            n = 2 * i + u
            terms = ((self.whi, self.chi[u]), (self.wlo, self.chi[u]), (self.whi, self.clo[u]))
            for m in range(self.NK):
                yield 18 * u + m
                if m == 0:
                    pe.wait_ge(self.lo_done, KC * n + KC)
                layer, part = m // PT, m % PT
                ge(pe, self.k_lo, self.NK * n + m + 1 - self.NB)
                for t, (w, c) in enumerate(terms):
                    for k in range(KC):
                        mm = pe.matmul(self.kps[m % self.NB][:, 0:NP], w[:, k, layer * 128:layer * 128 + 128],
                                       c[:, k, part * NP:(part + 1) * NP],
                                       start=(t == 0 and k == 0), stop=(t == 2 and k == KC - 1))
                mm.then_inc(self.k_ps, 1)
            for m in range(self.NV):
                yield 18 * u + self.NK + m
                ge(pe, self.v_sb, self.NV * n + m + 1 - self.NB)
                for k in range(KC):
                    for t, (w, c) in enumerate(terms):
                        mm = pe.matmul(self.vps[m % self.NB][0:CH, 0:256], c[:, k, m * CH:(m + 1) * CH],
                                       w[:, k, 256:512], start=(t == 0 and k == 0), stop=(t == 2 and k == KC - 1))
                mm.then_inc(self.v_ps, 1)

    def split_hi(self, n, u, k):
        self.nc.scalar.activation(self.chi[u][:, k, :], self.ctx32[:, k, :], ACT.Copy).then_inc(self.hi_done, 1)

    def setup_scalar(self, act):
        act.wait_ge(self.w_in, 16)
        for k in range(KC):
            self.nc.scalar.activation(self.whi[:, k, :], self.w32[:, k, :], ACT.Copy, scale=WSCALE).then_inc(self.w_hi, 1)
        for k in range(KC):
            act.wait_ge(self.ctx_in[k], 16)
            self.split_hi(0, 0, k)
        act.wait_ge(self.ones, 1)

    def scalar(self, act, i):
        nc = self.nc
        for u in range(2):
            n = 2 * i + u
            for m in range(self.NK):
                yield 18 * u + m + 1
                layer, part = m // PT, m % PT
                if m == 0:
                    ge(act, self.k_out, 32 * n)
                act.wait_ge(self.k_ps, self.NK * n + m + 1)
                nc.scalar.activation(self.khi[:, layer, part * NP:(part + 1) * NP], self.kps[m % self.NB][:, 0:NP],
                                     ACT.Copy, scale=1.0 / WSCALE).then_inc(self.k_hi, 1)
            for m in range(self.NV):
                slot = self.NK + m + 1
                yield 18 * u + slot
                if m == 0:
                    ge(act, self.v_out, 32 * n)
                act.wait_ge(self.v_ps, self.NV * n + m + 1)
                nc.scalar.activation(
                    self.vout[:, :, m * G * VS:(m + 1) * G * VS].rearrange("p l (g v) -> p l g v", v=VS)[:, :, :, 0:HD],
                    self.vps[m % self.NB][0:CH, 0:256].rearrange("p (l g v) -> p l g v", l=2, v=HD),
                    ACT.Copy, scale=1.0 / WSCALE).then_inc(self.v_sb, 1)
                if slot in self.SPLITS and not (is_last(self, i) and u == 1):
                    k = self.SPLITS.index(slot)
                    act.wait_ge(self.ctx_in[k], 16 * (n + 2))
                    self.split_hi(n + 1, 1 - u, k)

    def split_lo(self, u, k):
        self.nc.vector.tensor_tensor(self.clo[u][:, k, :], self.ctx32[:, k, :], self.chi[u][:, k, :],
                                     ALU.subtract).then_inc(self.lo_done, 1)

    def setup_vector(self, dve):
        nc = self.nc
        nc.vector.memset(self.vout[:, :, :], 1.0).then_inc(self.ones, 1)
        for k in range(KC):
            dve.wait_ge(self.w_hi, k + 1)
            nc.vector.scalar_tensor_tensor(out=self.wlo[:, k, :], in0=self.w32[:, k, :], scalar=WSCALE,
                                           in1=self.whi[:, k, :], op0=ALU.mult, op1=ALU.subtract).then_inc(self.w_lo, 1)
        for k in range(KC):
            dve.wait_ge(self.hi_done, k + 1)
            self.split_lo(0, k)

    def vector(self, dve, i):
        for u in range(2):
            n = 2 * i + u
            for m in range(self.NK):
                yield 18 * u + m + 1
                layer, part = m // PT, m % PT
                cols = slice(part * NP, (part + 1) * NP)
                dve.wait_ge(self.k_hi, self.NK * n + m + 1)
                if m == 0:
                    ge(dve, self.k_out, 32 * n)
                self.nc.vector.scalar_tensor_tensor(out=self.klo[:, layer, cols], in0=self.kps[m % self.NB][:, 0:NP],
                                                    scalar=1.0 / WSCALE, in1=self.khi[:, layer, cols],
                                                    op0=ALU.mult, op1=ALU.subtract).then_inc(self.k_lo, 1)
            for k, slot in enumerate(self.SPLITS):
                yield 18 * u + slot + 0.5
                if not (is_last(self, i) and u == 1):
                    dve.wait_ge(self.hi_done, KC * (n + 1) + k + 1)
                    self.split_lo(1 - u, k)

    def gpsimd(self, pool, i):
        return iter(())


class Norm:

    def __init__(self, nc, a, eps, tiles):
        self.nc = nc
        self.stats = [a.sb(f"stats{u}", [128, 6]) for u in range(tiles)]
        self.mv = [a.sb(f"mv{u}", [128, 2]) for u in range(tiles)]
        self.std = [a.sb(f"std{u}", [128, 1]) for u in range(tiles)]
        self.rstd = [a.sb(f"rstd{u}", [128, 1]) for u in range(tiles)]
        self.eps = eps
        self.var_ready, self.std_ready = a.sem("var_ready"), a.sem("std_ready")

    def statistics(self, chain, u, src):
        chain.link(self.nc.vector.bn_stats(self.stats[u][:, :], src))
        chain.carry(u)
        self.nc.vector.bn_aggr(self.mv[u][:, :], self.stats[u][:, :]).then_inc(self.var_ready, 1)

    def root(self, act, u, count):
        act.wait_ge(self.var_ready, count)
        self.nc.scalar.activation(self.std[u][:, :], self.mv[u][:, 1:2], ACT.Sqrt, bias=self.eps[:, 0:1]).then_inc(self.std_ready, 1)

    def deviation(self, dve, chain, u, dst, src, gamma, count):
        dve.wait_ge(self.std_ready, count)
        chain.link(self.nc.vector.reciprocal(self.rstd[u][:, :], self.std[u][:, :]))
        chain.link(self.nc.vector.scalar_tensor_tensor(out=dst, in0=src, scalar=self.mv[u][:, 0:1], in1=gamma,
                                                       op0=ALU.subtract, op1=ALU.mult))

    def apply(self, dve, chain, u, dst, src, count):
        dve.wait_ge(self.std_ready, count)
        chain.link(self.nc.vector.reciprocal(self.rstd[u][:, :], self.std[u][:, :]))
        return self.nc.vector.tensor_scalar(dst, src, self.mv[u][:, 0:1], self.rstd[u][:, 0:1],
                                            ALU.subtract, ALU.mult)


class SelfAttention:

    def __init__(self, nc, a, io, scr, layer, lag, x_src=None, x_tile=None, x_ready=None):
        self.nc, self.scr, self.layer, self.x_src, self.lag = nc, scr, layer, x_src, lag
        self.rounds = TILES
        self.front_at, self.back_at = (0, 20) if layer == 0 else (1, 2)
        L0 = layer == 0
        NQ = D if L0 else 2 * D
        NKC = D if L0 else 2 * 128
        NVC = D if L0 else 128
        self.KT = KT = 4 if L0 else 1
        self.wq = a.sb("wq", [128, KC, NQ])
        self.wk = a.sb("wk", [128, KC, NKC])
        self.wv = a.sb("wv", [128, KC, NVC])
        self.wo = a.sb("wo", [128, KC, D])
        self.wxq = a.sb("wxq", [128, KC, D])
        self.ident = a.sb("ident", [128, 128])
        self.blockmask = a.sb("blockmask", [128, 8, SP_])
        self.causal = a.sb("causal", [128, SP_])
        self.eps = a.sb("eps", [128, 1])
        w = lambda n: wcols(io[f"sa{layer}_{n}"])
        self.loads = {"ident": (self.ident[:, :], io["ident"])}
        if L0:
            self.bq, self.bk = a.sb("bq", [128, 4]), a.sb("bk", [128, 4])
            self.bv, self.bo = a.sb("bv", [1, D]), a.sb("bo", [1, D])
            self.ones = a.sb("ones", [1, 128])
            row = lambda n: io[n].rearrange("(a n) -> a n", a=1)
            self.loads |= {"wq": (self.wq[:, :, :], w("wq")), "wk": (self.wk[:, :, :], w("wk")),
                           "bq": (self.bq[:, :], io["sa0_bq"]), "bk": (self.bk[:, :], io["sa0_bk"]),
                           "bv": (self.bv[:, :], row("sa0_bv")), "bo": (self.bo[:, :], row("sa0_bo"))}
        else:
            self.rope = a.sb("rope", [128, 4, SP_])
            self.mask_u8 = a.sb("mask_u8", [S, SK], U8)
            self.mask16 = a.sb("mask16", [S, SK], BF16)
            self.maxkeep = a.sb("maxkeep", [S, 1])
            self.keepq = a.sb("keepq", [S, 128])
            self.keep_bc = a.sb("keep_bc", [128, SP_])
            self.rot = a.sb("rot", [128, 512])
            self.loads |= {"mask": (self.mask_u8[:, :], io["mask"]),
                           "wq": (self.wq[:, :, :], w("wq")), "wk": (self.wk[:, :, :], w("wk")),
                           "rope": (self.rope[:, :, :], io["rope"].rearrange("p (a q) -> p a q", a=4))}
        self.loads |= {"wv": (self.wv[:, :, :], w("wv")),
                       "blockmask": (self.blockmask[:, :, :], io["blockmask"].rearrange("p (h k) -> p h k", h=8)),
                       "causal": (self.causal[:, :], io["causal"]),
                       "wo": (self.wo[:, :, :], w("wo")), "wxq": (self.wxq[:, :, :], wcols(io[f"xa{layer}_wq"]))}
        self.x = x_tile if x_src is None else a.sb("x", [128, D])
        self.xr = self.x if layer == 0 else a.sb("xr", [128, D])
        self.xT = a.sb("xT", [128, KC, 128])
        self.x1T = self.xT if layer == 0 else a.sb("x1T", [128, KC, 128])
        self.xT_swapped = a.sb("xT_swapped", [128, KC, 128])
        self.qT = a.sb("qT", [128, 4, 128])
        self.kT = a.sb("kT", [128, KT, 128])
        self.kbd = [a.sb(f"kbd{r}", [128, 2, 8, SP_]) for r in range(min(KT, 2))]
        hp = 16 if L0 else 4
        self.vbd = a.sb("vbd", [128, 2, hp, 2, HD])
        self.sc = a.sb("sc", [128, 4, 8, SP_])
        self.mx, self.sm, self.rs = (a.sb(n, [128, 4, 8]) for n in ("mx", "sm", "rs"))
        self.pT = a.sb("pT", [128, 4, 512])
        self.att = a.sb("att", [128, 512])
        self.attT = a.sb("attT", [128, KC, 128])
        self.y, self.x1 = a.sb("y", [128, D]), a.sb("x1", [128, D])
        self.q32 = self.y if layer == 0 else a.sb("q32", [128, 512])
        self.qhi, self.qlo = a.sb("qhi", [128, 512], F16), a.sb("qlo", [128, 512], F16)
        self.pad = a.sb("pad", [1, 1])
        self.bank = bank = [a.ps(f"bank{n}") for n in range(4 if L0 else 5)]
        self.pT_bank = [bank[3], bank[0]] if L0 else [bank[0], bank[0]]
        self.attT_bank, self.y_bank = (bank[2], bank[3]) if L0 else (bank[3], bank[4])
        self.x1T_bank, self.xq_bank = (bank[0], bank[1]) if L0 else (bank[3], bank[4])
        self.v_bank = [bank[3][:, 0:D], bank[0][:, 0:D]] if L0 else [bank[0][:, 256:384], bank[0][:, 384:512]]
        self.w_in = {n: a.sem(f"{n}_in") for n in self.loads}
        self.setup, self.eps_ready = a.sem("setup"), a.sem("eps_ready")
        names = ["x_in", "x_out", "xT_ps", "xT_sb", "qk_ps", "q_sb", "k_sb", "v_ps", "v_sb", "kbd_sb", "s_ps", "s_sub",
                 "s_add", "p_sb", "pT_ps", "pT_sb", "att_ps", "att_sb", "attT_ps", "attT_sb", "y_ps", "y_sb",
                 "x1_sb", "x1T_ps", "x1T_sb", "xq_ps", "q32_sb", "qhi_sb", "qlo_sb", "chain_front",
                 "chain_back", "xr_sb", "xs_sb", "keep_ps", "keep_sb"]
        self.s = {n: a.sem(n) for n in names}
        self.x_ready, self.x_count = (self.s["x_in"], 16) if x_src is not None else (x_ready, 1)
        self.norm = Norm(nc, a, self.eps, 1)
        front = {"sync": self.no_steps, "tensor": self.tensor_front, "scalar": self.scalar_front,
                 "vector": self.vector_front, "gpsimd": self.gpsimd_front}
        back = {"sync": self.sync_back, "tensor": self.tensor_back, "scalar": self.scalar_back,
                "vector": self.vector_back, "gpsimd": self.no_steps}
        if L0:
            self.programs = {n: lambda eng, i, n=n: join(front[n](eng, i), back[n](eng, i)) for n in front}
        else:
            self.programs, self.back = front, Part(back, lag + 1, self.rounds)

    def no_steps(self, eng, i):
        return iter(())

    def loaded(self, eng, i, *names):
        if isinstance(i, int) and i == 0:
            for n in names:
                eng.wait_ge(self.w_in[n], 16)

    def setup_sync(self, sp):
        if self.x_src is not None:
            sp.dma_start(self.x[:, :], self.x_src[0]).then_inc(self.x_ready, 16)
        for n, (dst, src) in self.loads.items():
            sp.dma_start(dst, src).then_inc(self.w_in[n], 16)

    def sync_back(self, sp, i):
        s, at = self.s, self.back_at
        yield at + 6
        if self.x_src is not None and not is_last(self, i):
            sp.wait_ge(s["y_sb"], i + 1)
            sp.dma_start(self.x[:, :], self.x_src[i + 1]).then_inc(self.x_ready, 16)
        yield at + 8
        sp.wait_ge(s["x1_sb"], i + 1)
        sp.dma_start(self.scr["x"][self.layer, i], self.x1[:, :]).then_inc(s["x_out"], 16)
        yield at + 14
        for part, (ready, q) in enumerate(((s["qhi_sb"], self.qhi), (s["qlo_sb"], self.qlo))):
            sp.wait_ge(ready, i + 1)
            for b in range(2):
                sp.dma_start(self.scr["q"][part, 2 * i + b],
                             q[:, :].rearrange("p (j b q) -> p j b q", b=2, j=4)[:, :, b, 0:S]).then_inc(s["x_out"], 16)

    def finish_sync(self, sp):
        sp.wait_ge(self.s["x_out"], 80 * TILES)

    def setup_tensor(self, pe):
        pass

    def transposed(self, pe, src, dst, done):
        for k in range(KC):
            mm = pe.transpose(dst[:, k * 128:(k + 1) * 128], src[:, k * 128:(k + 1) * 128], self.ident[:, :])
        mm.then_inc(done, 1)

    def tensor_front(self, pe, i):
        s, L0, bank, ident, at = self.s, self.layer == 0, self.bank, self.ident, self.front_at
        yield at + 1
        self.loaded(pe, i, "ident")
        if isinstance(i, int) and i == 0:
            if L0:
                pe.wait_ge(self.setup, 2)
            else:
                pe.wait_ge(self.setup, 4)
                pe.matmul(bank[0][:, 0:S], self.keepq[:, :], ident[0:S, 0:S], start=True, stop=True).then_inc(s["keep_ps"], 1)
                pe.wait_ge(s["keep_sb"], 1)
        pe.wait_ge(self.x_ready, self.x_count * i + self.x_count)
        self.transposed(pe, self.x, bank[0], s["xT_ps"])
        yield at + 3
        self.loaded(pe, i, "wq", "wk")
        pe.wait_ge(s["xT_sb"], i + 1)
        jobs = [(bank[1], self.wq, 4, 0), (bank[2], self.wk, 4, 0)] if L0 else \
               [(bank[1], self.wq, 4, 0), (bank[2], self.wq, 4, 4), (bank[0], self.wk, 2, 0)]
        for dst, w, tiles, first in jobs:
            for t in range(tiles):
                for k in range(KC):
                    mm = pe.matmul(dst[:, t * 128:(t + 1) * 128], w[:, k, (first + t) * 128:(first + t + 1) * 128],
                                   self.xT[:, k, :], start=(k == 0), stop=(k == KC - 1))
        mm.then_inc(s["qk_ps"], 1)
        yield at + 4
        self.loaded(pe, i, "wv", *(("bv",) if L0 else ()))
        pe.wait_ge(s["xs_sb"], i + 1)
        for out, tokens in zip(self.v_bank, (self.xT, self.xT_swapped)):
            for k in range(KC):
                mm = pe.matmul(out, tokens[:, k, :], self.wv[:, k, :], start=(k == 0), stop=(k == KC - 1 and not L0))
            if L0:
                mm = pe.matmul(out, self.ones[0:1, :], self.bv[0:1, :], start=False, stop=True)
        mm.then_inc(s["v_ps"], 1)

        def scores(t):
            if t == 0:
                pe.wait_ge(s["q_sb"], i + 1)
                pe.wait_ge(s["k_sb"], i + 1)
            pe.wait_ge(s["kbd_sb"], self.KT * i + min(t, self.KT - 1) + 1)
            if t >= 2:
                pe.wait_ge(s["s_add"], 4 * i + t - 1)
            for b in range(2):
                mm = pe.matmul(bank[1 + t % 2][b * SP_:(b + 1) * SP_, :], self.qT[:, t, b * SP_:(b + 1) * SP_],
                               self.kbd[t % 2 if L0 else 0][:, b, :, :], start=True, stop=True)
            mm.then_inc(s["s_ps"], 1)

        def probs_transposed(t):
            pe.wait_ge(s["p_sb"], 4 * i + t + 1)
            if t == 0:
                pe.wait_ge(s["v_sb"], i + 1)
            if t >= (2 if L0 else 1):
                pe.wait_ge(s["pT_sb"], 4 * i + t - (1 if L0 else 0))
            for k in range(4):
                mm = pe.transpose(self.pT_bank[t % 2][:, k * 128:(k + 1) * 128],
                                  self.sc[:, t, 2 * k:2 * k + 2, :], ident[:, :])
            mm.then_inc(s["pT_ps"], 1)

        for t in range(6):
            yield at + 7 + 2 * t
            if t < 4:
                scores(t)
            if t >= 2:
                probs_transposed(t - 2)
        yield at + 19
        pe.wait_ge(s["s_add"], 4 * i + 4)
        pe.wait_ge(s["pT_sb"], 4 * i + 4)
        for t in range(4):
            for k in range(4):
                for b in range(2):
                    c = t * 128 + k * 32
                    mm = pe.matmul(bank[1][b * SP_:(b + 1) * SP_, c:c + 32],
                                   self.pT[:, t, k * 128 + b * SP_:k * 128 + (b + 1) * SP_],
                                   self.vbd[:, b, t * 4 + k if L0 else k, :, :], start=True, stop=True)
        mm.then_inc(s["att_ps"], 1)

    def tensor_back(self, pe, i):
        s, L0, at = self.s, self.layer == 0, self.back_at
        yield at + 1
        pe.wait_ge(s["att_sb"], i + 1)
        if not L0:
            ge(pe, s["x1T_sb"], i)
        self.transposed(pe, self.att, self.attT_bank, s["attT_ps"])
        yield at + 3
        self.loaded(pe, i, "wo", *(("bo",) if L0 else ()))
        pe.wait_ge(s["attT_sb"], i + 1)
        if not L0:
            ge(pe, s["q32_sb"], i)
        for k in range(KC):
            mm = pe.matmul(self.y_bank[:, :], self.attT[:, k, :], self.wo[:, k, :], start=(k == 0), stop=(k == KC - 1 and not L0))
        if L0:
            mm = pe.matmul(self.y_bank[:, :], self.ones[0:1, :], self.bo[0:1, :], start=False, stop=True)
        mm.then_inc(s["y_ps"], 1)
        yield at + 8
        pe.wait_ge(s["x1_sb"], i + 1)
        self.transposed(pe, self.x1, self.x1T_bank, s["x1T_ps"])
        yield at + 10
        self.loaded(pe, i, "wxq")
        pe.wait_ge(s["x1T_sb"], i + 1)
        for t in range(4):
            for k in range(KC):
                mm = pe.matmul(self.xq_bank[:, t * 128:(t + 1) * 128], self.wxq[:, k, t * 128:(t + 1) * 128],
                               self.x1T[:, k, :], start=(k == 0), stop=(k == KC - 1))
        mm.then_inc(s["xq_ps"], 1)

    def setup_vector(self, dve):
        nc = self.nc
        nc.vector.memset(self.vbd[:, :, :, :, :], 0.0).then_inc(self.setup, 1)
        nc.vector.memset(self.eps[:, :], 1e-5).then_inc(self.eps_ready, 1)
        if self.layer == 0:
            nc.vector.memset(self.ones[:, :], 1.0).then_inc(self.setup, 1)
        self.chain_front = Chain(dve, self.s["chain_front"], (0 if self.layer == 0 else 4) + 4 * 2 + 1, self.pad)
        self.chain_back = Chain(dve, self.s["chain_back"], 2, self.pad)

    def prepare_mask(self, dve):
        nc = self.nc
        nc.vector.tensor_copy(self.mask16[:, :], self.mask_u8[:, :]).then_inc(self.setup, 1)
        dve.wait_ge(self.setup, 2)
        nc.vector.reduce_max(self.maxkeep[:, :], self.mask16[:, :], AX.X).then_inc(self.setup, 1)
        dve.wait_ge(self.setup, 3)
        nc.vector.tensor_copy(self.keepq[:, :], self.maxkeep[:, 0:1].to_broadcast([S, 128])).then_inc(self.setup, 1)
        nc.vector.memset(self.keep_bc[:, S:SP_], 1.0)
        dve.wait_ge(self.s["keep_ps"], 1)
        nc.vector.tensor_copy(self.keep_bc[:, 0:S], self.bank[0][:, 0:S]).then_inc(self.s["keep_sb"], 1)

    def vector_front(self, dve, i):
        nc, s, L0, bank, chain, at = self.nc, self.s, self.layer == 0, self.bank, self.chain_front, self.front_at
        chain.begin(i)
        yield at
        if isinstance(i, int) and i == 0 and not L0:
            self.loaded(dve, i, "mask")
            self.prepare_mask(dve)
            dve.wait_ge(s["keep_sb"], 1)
        yield at + 2
        dve.wait_ge(s["xT_ps"], i + 1)
        nc.vector.tensor_copy(self.xT[:, :, :], bank[0][:, :].rearrange("p (c t) -> p c t", c=KC)).then_inc(s["xT_sb"], 1)
        yield at + 5
        self.loaded(dve, i, "bq" if L0 else "rope", "causal")
        dve.wait_ge(s["qk_ps"], i + 1)
        qT = self.qT[:, :, :].rearrange("p a b -> p (a b)")
        if L0:
            for t in range(4):
                last = nc.vector.tensor_scalar(self.qT[:, t, :], bank[1][:, t * 128:(t + 1) * 128],
                                               self.bq[:, t:t + 1], 0.25, ALU.add, ALU.mult)
            last.then_inc(s["q_sb"], 1)
        else:
            def tab(r, reps):
                return self.rope[:, r, :].unsqueeze(1).to_broadcast([128, reps, SP_])

            def by(ap):
                return ap.rearrange("p (r q) -> p r q", q=SP_)
            rot, k = self.rot, self.kT[:, 0, :]
            chain.link(nc.vector.tensor_tensor(by(rot[:, :]), by(bank[2][:, :]), tab(1, 8), ALU.mult))
            chain.link(nc.vector.tensor_tensor(by(qT), by(bank[1][:, :]), tab(0, 8), ALU.mult))
            nc.vector.tensor_tensor(qT, qT, rot[:, :], ALU.add).then_inc(s["q_sb"], 1)
            dve.wait_ge(s["q_sb"], i + 1)
            dve.wait_ge(s["v_ps"], i + 1)
            chain.link(nc.vector.tensor_tensor(by(rot[:, 0:128]), by(bank[0][:, 128:256]), tab(3, 2), ALU.mult))
            chain.link(nc.vector.tensor_tensor(by(k), by(bank[0][:, 0:128]), tab(2, 2), ALU.mult))
            nc.vector.tensor_tensor(k, k, rot[:, 0:128], ALU.add).then_inc(s["k_sb"], 1)

        def mask_and_maximum(t):
            sc = self.sc[:, t, :, :]
            dve.wait_ge(s["s_ps"], 4 * i + t + 1)
            nc.vector.tensor_tensor(sc, bank[1 + t % 2][:, :].rearrange("p (h k) -> p h k", h=8),
                                    self.causal[:, :].unsqueeze(1).to_broadcast([128, 8, SP_]), ALU.add).then_inc(s["s_add"], 1)
            dve.wait_ge(s["s_add"], 4 * i + t + 1)
            chain.link(nc.vector.tensor_reduce(self.mx[:, t, :], sc, AX.X, ALU.max))
            nc.vector.tensor_tensor(sc, sc, self.mx[:, t, :].unsqueeze(2).to_broadcast([128, 8, SP_]),
                                    ALU.subtract).then_inc(s["s_sub"], 1)

        def sums(t):
            dve.wait_ge(s["p_sb"], 4 * i + t + 1)
            chain.link(nc.vector.tensor_reduce(self.sm[:, t, :], self.sc[:, t, :, :], AX.X, ALU.add))

        for t in range(5):
            yield at + 8 + 2 * t
            if t < 4:
                mask_and_maximum(t)
            if t >= 1:
                sums(t - 1)
        chain.link(nc.vector.reciprocal(self.rs[:, :, :], self.sm[:, :, :]))
        yield at + 20
        dve.wait_ge(s["att_ps"], i + 1)
        nc.vector.tensor_tensor(self.att[:, :].rearrange("p (h d) -> p h d", d=HD),
                                bank[1][:, :].rearrange("p (h d) -> p h d", d=HD),
                                self.rs[:, :, :].rearrange("p t h -> p (t h)").unsqueeze(2).to_broadcast([128, 32, HD]),
                                ALU.mult).then_inc(s["att_sb"], 1)
        assert chain.k == chain.per_round, (chain.k, chain.per_round)

    def vector_back(self, dve, i):
        nc, s, L0, chain, at = self.nc, self.s, self.layer == 0, self.chain_back, self.back_at
        chain.begin(i)
        yield at + 5
        dve.wait_ge(s["y_ps"], i + 1)
        if not L0:
            dve.wait_ge(s["xr_sb"], i + 1)
        nc.vector.tensor_tensor(self.y[:, :], self.y_bank[:, :], self.xr[:, :], ALU.add).then_inc(s["y_sb"], 1)
        dve.wait_ge(s["y_sb"], i + 1)
        self.norm.statistics(chain, 0, self.y[:, :])
        yield at + 7
        ge(dve, s["x_out"], 80 * i)
        self.norm.apply(dve, chain, 0, self.x1[:, :], self.y[:, :], i + 1).then_inc(s["x1_sb"], 1)
        yield at + 9
        dve.wait_ge(s["x1T_ps"], i + 1)
        nc.vector.tensor_copy(self.x1T[:, :, :], self.x1T_bank[:, :].rearrange("p (c t) -> p c t", c=KC)).then_inc(s["x1T_sb"], 1)
        yield at + 12
        dve.wait_ge(s["xq_ps"], i + 1)
        if L0:
            nc.vector.tensor_scalar(self.q32[:, :], self.xq_bank[:, :], 0.25, None, ALU.mult).then_inc(s["q32_sb"], 1)
        else:
            nc.vector.scalar_tensor_tensor(out=self.q32[:, :].rearrange("p (r q) -> p r q", q=SP_),
                                           in0=self.xq_bank[:, :].rearrange("p (r q) -> p r q", q=SP_), scalar=0.25,
                                           in1=self.keep_bc[:, :].unsqueeze(1).to_broadcast([128, 8, SP_]),
                                           op0=ALU.mult, op1=ALU.mult).then_inc(s["q32_sb"], 1)
        yield at + 14
        dve.wait_ge(s["qhi_sb"], i + 1)
        nc.vector.tensor_tensor(self.qlo[:, :], self.q32[:, :], self.qhi[:, :], ALU.subtract).then_inc(s["qlo_sb"], 1)
        assert chain.k == chain.per_round, (chain.k, chain.per_round)

    def setup_scalar(self, act):
        pass

    def scalar_front(self, act, i):
        nc, s, L0, bank, at = self.nc, self.s, self.layer == 0, self.bank, self.front_at
        yield at + 2.5
        act.wait_ge(s["xT_sb"], i + 1)
        for b in range(2):
            last = nc.scalar.activation(self.xT_swapped[:, :, b * SP_:(b + 1) * SP_],
                                        self.xT[:, :, (1 - b) * SP_:(2 - b) * SP_], ACT.Copy)
        last.then_inc(s["xs_sb"], 1)
        yield at + 5
        if isinstance(i, int) and i == 0:
            act.wait_ge(self.setup, 2 if L0 else 4)
            act.wait_ge(self.eps_ready, 1)
        if L0:
            self.loaded(act, i, "bk")
            act.wait_ge(s["qk_ps"], i + 1)
            for t in range(4):
                last = nc.scalar.activation(self.kT[:, t, :], bank[2][:, t * 128:(t + 1) * 128],
                                            ACT.Identity, bias=self.bk[:, t:t + 1])
            last.then_inc(s["k_sb"], 1)
        yield at + 6
        act.wait_ge(s["v_ps"], i + 1)
        if not L0:
            act.wait_ge(s["k_sb"], i + 1)
        for b in range(2):
            for half in range(2):
                src = self.v_bank[b ^ half]
                rows = slice(64 * half, 64 * half + 64)
                last = nc.scalar.activation(self.vbd[rows, b, :, half, :],
                                            src[rows, :].rearrange("p (m s d) -> p m s d", s=2, d=HD)[:, :, half, :],
                                            ACT.Copy)
        last.then_inc(s["v_sb"], 1)
        if not L0:
            act.wait_ge(self.x_ready, i + 1)
            ge(act, s["y_sb"], i)
            nc.scalar.activation(self.xr[:, :], self.x[:, :], ACT.Copy).then_inc(s["xr_sb"], 1)
        for t in range(6):
            if t >= 2:
                yield at + 8.2 + 2 * t
                act.wait_ge(s["pT_ps"], 4 * i + t - 1)
                nc.scalar.activation(self.pT[:, t - 2, :], self.pT_bank[t % 2][:, :], ACT.Copy).then_inc(s["pT_sb"], 1)
            if t < 4:
                yield at + 9 + 2 * t
                act.wait_ge(s["s_sub"], 4 * i + t + 1)
                nc.scalar.activation(self.sc[:, t, :, :], self.sc[:, t, :, :], ACT.Exp).then_inc(s["p_sb"], 1)

    def scalar_back(self, act, i):
        nc, s, at = self.nc, self.s, self.back_at
        yield at + 2
        act.wait_ge(s["attT_ps"], i + 1)
        nc.scalar.activation(self.attT[:, :, :], self.attT_bank[:, :].rearrange("p (c t) -> p c t", c=KC), ACT.Copy).then_inc(s["attT_sb"], 1)
        yield at + 6
        self.norm.root(act, 0, i + 1)
        yield at + 13
        act.wait_ge(s["q32_sb"], i + 1)
        nc.scalar.activation(self.qhi[:, :], self.q32[:, :], ACT.Copy).then_inc(s["qhi_sb"], 1)

    def gpsimd_front(self, pool, i):
        nc, s, at = self.nc, self.s, self.front_at
        yield at + 6
        self.loaded(pool, i, "blockmask")
        pool.wait_ge(s["k_sb"], i + 1)
        for t in range(self.KT):
            if t >= 2:
                yield at + 8 + 2 * (t - 2)
                pool.wait_ge(s["s_ps"], 4 * i + t - 1)
            for b in range(2):
                last = nc.gpsimd.tensor_tensor(
                    self.kbd[t % 2][:, b, :, :], self.kT[:, t, b * SP_:(b + 1) * SP_].unsqueeze(1).to_broadcast([128, 8, SP_]),
                    self.blockmask[:, :, :], ALU.mult)
            last.then_inc(s["kbd_sb"], 1)




class AfterCross:

    NI = 8
    NE, R = 4, 16
    lag = 0

    def __init__(self, nc, a, io, scr, layer, T, out):
        self.nc, self.io, self.scr, self.layer, self.T, self.out = nc, io, scr, layer, T, out
        self.rounds, self.x2_used = TILES // T, None
        self.x1T_bank = 2 if layer == 0 else 0
        NI, NE, R = self.NI, self.NE, self.R
        self.wo = a.sb("wo", [128, KC, D])
        self.ident = a.sb("ident", [128, 128])
        self.eps = a.sb("eps", [128, 1])
        self.loads = [(self.ident[:, :], io["ident"]), (self.wo[:, :, :], wcols(io[f"xa{layer}_wo"]))]
        if layer == 0:
            self.up = a.sb("up", [128, KC, 1024])
            self.down = a.sb("down", [128, NI, D])
            self.fc1 = a.sb("fc1", [128, KC, 256])
            self.expert = a.sb("expert", [128, 2, 256])
            self.fc2 = a.sb("fc2", [128, 2, D])
            self.gate = a.sb("gate", [128, KC, 8])
            self.gamma, self.beta = a.sb("gamma", [128, D]), a.sb("beta", [128, D])
            self.loads += [(self.fc1[:, :, :], wcols(io["fc1"])), (self.up[:, :, :], wcols(io["up"])),
                           (self.gate[:, :, :], wcols(io["gate"])), (self.expert[:, :, :], wcols(io["expert"])),
                           (self.down[:, :, :], wcols(io["down"])), (self.fc2[:, :, :], wcols(io["fc2"])),
                           (self.gamma[:, :], io["gamma"].partition_broadcast(128)),
                           (self.beta[:, :], io["beta"].partition_broadcast(128))]
        else:
            self.wr = a.sb("wr", [128, KC, NE * R + NE])
            self.lb = a.sb("lb", [NE * R, D])
            self.lower = a.sb("lower", [128, NE, NE])
            self.loads += [(self.wr[:, :, :], wcols(io["lora_a"])), (self.lb[:, :], io["lora_b"]),
                           (self.lower[:, :, :], io["lower"].rearrange("p (a b) -> p a b", a=NE))]

        def each(name, shape, dt=F32):
            return [a.sb(f"{name}{u}", shape, dt) for u in range(T)]

        self.at, self.x = each("at", [128, D]), each("x", [128, D])
        self.aT, self.xT = each("aT", [128, KC, 128]), each("xT", [128, KC, 128])
        self.y, self.x1, self.y2, self.x2 = (each(n, [128, D]) for n in ("y", "x1", "y2", "x2"))
        if layer == 0:
            self.lat, self.moe = each("lat", [128, 2, 128]), each("moe", [128, 2, 128])
            self.hid, self.hsq = each("hid", [128, NI, 128]), each("hsq", [128, NI, 128])
            self.top, self.wsum = each("top", [128, 8]), each("wsum", [128, 1])
            self.xb, self.t1, self.f = (each(n, [128, D]) for n in ("xb", "t1", "f"))
        else:
            self.lg, self.top = each("lg", [128, 8]), each("top", [128, 8])
            self.gt, self.eq = each("gt", [128, NE, NE]), each("eq", [128, NE, NE])
            self.rank, self.ex = each("rank", [128, NE]), each("ex", [128, NE])
            self.gs, self.gr = each("gs", [128, 1]), each("gr", [128, 1])
            self.mid = each("mid", [128, 128 // R, R])
            self.midT = each("midT", [NE * R, 128])
        self.bank = [[a.ps(f"bank{u}_{n}") for n in range(3 if layer == 0 else 2)] for u in range(T)]
        self.w_in, self.setup = [a.sem(f"w_in{n}") for n in range(len(self.loads))], a.sem("setup")
        self.n_setup = T + 1 + (1 if layer == 1 else 0)
        self.x_in = [a.sem(f"x_in{u}") for u in range(T)]
        self.x_out = [a.sem(f"x_out{u}") for u in range(T)]
        names = ["aT_ps", "aT_sb", "y_ps", "y_sb", "x1_sb", "x1T_ps", "x1T_sb", "x2_sb", "chain_dve"]
        names += ["lat_ps", "lat_sb", "moe_ps", "moe_sb", "up_ps", "hid_sb", "hsq_sb", "top_sb", "down_ps",
                  "routed_ps", "f_sb", "t1_sb", "xb_sb"] if layer == 0 else \
                 ["mid_ps", "lg_sb", "ex_sb", "mid_sb", "midT_ps", "midT_sb", "delta_ps"]
        self.s = {n: a.sem(n) for n in names}
        self.norm = Norm(nc, a, self.eps, T)
        self.pad = a.sb("pad", [1, T + 1])
        self.NN = 3 if layer == 0 else 2
        self.programs = {"sync": self.sync, "tensor": self.tensor, "scalar": self.scalar,
                         "vector": self.vector, "gpsimd": self.gpsimd}

    def count(self, i, norm, u):
        return self.NN * self.T * i + self.T * norm + u + 1

    def weights(self, eng, *which):
        for n in which:
            eng.wait_ge(self.w_in[n], 16)

    def load(self, sp, n, u):
        sp.dma_start(self.x[u][:, :], self.scr["x"][self.layer, n]).then_inc(self.x_in[u], 16)
        for b in range(2):
            sp.dma_start(self.at[u][b * SP_:b * SP_ + S, :], self.scr["att"][2 * n + b]).then_inc(self.x_in[u], 16)

    def setup_sync(self, sp):
        sp.dma_start(*self.loads[0]).then_inc(self.w_in[0], 16)
        sp.wait_ge(self.setup, self.T)
        for u in range(self.T):
            self.load(sp, u, u)
        for n in range(1, len(self.loads)):
            sp.dma_start(*self.loads[n]).then_inc(self.w_in[n], 16)

    def sync(self, sp, i):
        T, s = self.T, self.s
        yield 5.5
        if not is_last(self, i):
            for u in range(T):
                sp.wait_ge(s["y_sb"], T * i + u + 1)
                self.load(sp, T * i + T + u, u)
        yield 27.5
        if self.out is not None:
            for u in range(T):
                n = T * i + u
                sp.wait_ge(s["x2_sb"], n + 1)
                for b in range(2):
                    sp.dma_start(self.out[2 * T * i + 2 * u + b], self.x2[u][b * SP_:b * SP_ + S, :]).then_inc(self.x_out[u], 16)

    def finish_sync(self, sp):
        if self.out is not None:
            for u in range(self.T):
                sp.wait_ge(self.x_out[u], 32 * self.rounds)

    def setup_tensor(self, pe):
        pass

    def tensor(self, pe, i):
        T, s, bank, NI = self.T, self.s, self.bank, self.NI
        first = isinstance(i, int) and i == 0

        def transposed(src, dst, done):
            for k in range(KC):
                mm = pe.transpose(dst[:, k * 128:(k + 1) * 128], src[:, k * 128:(k + 1) * 128], self.ident[:, :])
            mm.then_inc(done, 1)

        def product(dst, moving, weights, n, done):
            for k in range(n):
                mm = pe.matmul(dst, moving(k), weights(k), start=(k == 0), stop=(k == n - 1))
            if done is not None:
                mm.then_inc(done, 1)

        yield 1.5
        if first:
            self.weights(pe, 0)
        for u in range(T):
            pe.wait_ge(self.x_in[u], 48 * i + 48)
            if self.layer == 0:
                ge(pe, s["f_sb"], T * i + u)
            transposed(self.at[u], bank[u][0], s["aT_ps"])
        yield 3.5
        if first:
            self.weights(pe, 1)
        for u in range(T):
            pe.wait_ge(s["aT_sb"], T * i + u + 1)
            product(bank[u][1][:, :], lambda k: self.aT[u][:, k, :], lambda k: self.wo[:, k, :], KC, s["y_ps"])
        yield 7.5
        for u in range(T):
            pe.wait_ge(s["x1_sb"], T * i + u + 1)
            transposed(self.x1[u], bank[u][self.x1T_bank], s["x1T_ps"])
        if self.layer == 0:
            for part in range(2):
                yield 9.5 + 2 * part
                if first:
                    self.weights(pe, *((2, 4) if part == 0 else (3,)))
                for u in range(T):
                    pe.wait_ge(s["x1T_sb"], T * i + u + 1)
                    if part == 0:
                        for t in range(2):
                            product(bank[u][0][:, t * 128:(t + 1) * 128], lambda k: self.fc1[:, k, t * 128:(t + 1) * 128],
                                    lambda k: self.xT[u][:, k, :], KC, s["lat_ps"] if t == 1 else None)
                    else:
                        for t in range(NI):
                            product(bank[u][1 + t // 4][:, (t % 4) * 128:(t % 4 + 1) * 128],
                                    lambda k: self.up[:, k, t * 128:(t + 1) * 128],
                                    lambda k: self.xT[u][:, k, :], KC, s["up_ps"] if t % 4 == 3 else None)
            yield 13.5
            if first:
                self.weights(pe, 5)
            for u in range(T):
                pe.wait_ge(s["lat_sb"], T * i + u + 1)
                product(bank[u][0][:, 0:8], lambda k: self.xT[u][:, k, :], lambda k: self.gate[:, k, :], KC, None)
                for t in range(2):
                    product(bank[u][0][:, 256 + t * 128:256 + (t + 1) * 128], lambda k: self.expert[:, k, t * 128:(t + 1) * 128],
                            lambda k: self.lat[u][:, k, :], 2, s["moe_ps"] if t == 1 else None)
            yield 17.5
            if first:
                self.weights(pe, 6, 7)
            for u in range(T):
                pe.wait_ge(s["moe_sb"], T * i + u + 1)
                pe.wait_ge(s["hsq_sb"], T * i + u + 1)
                product(bank[u][1][:, :], lambda k: self.hsq[u][:, k, :], lambda k: self.down[:, k, :], NI, s["down_ps"])
                pe.wait_ge(s["top_sb"], T * i + u + 1)
                product(bank[u][0][:, :], lambda k: self.moe[u][:, k, :], lambda k: self.fc2[:, k, :], 2, s["routed_ps"])
        else:
            MR = self.NE * self.R
            yield 9.5
            if first:
                self.weights(pe, 2)
            for u in range(T):
                pe.wait_ge(s["x1T_sb"], T * i + u + 1)
                product(bank[u][0][:, 0:MR + self.NE], lambda k: self.xT[u][:, k, :], lambda k: self.wr[:, k, :], KC, s["mid_ps"])
            yield 13.5
            for u in range(T):
                pe.wait_ge(s["mid_sb"], 4 * (T * i + u) + 4)
                pe.transpose(bank[u][1][:, 0:128], self.mid[u][:, :, :].rearrange("p a b -> p (a b)"),
                             self.ident[:, :]).then_inc(s["midT_ps"], 1)
            yield 15.5
            if first:
                self.weights(pe, 3)
            for u in range(T):
                pe.wait_ge(s["midT_sb"], T * i + u + 1)
                pe.matmul(bank[u][1][:, :], self.midT[u][:, :], self.lb[:, :], start=True, stop=True).then_inc(s["delta_ps"], 1)

    def setup_vector(self, dve):
        nc = self.nc
        for u in range(self.T):
            nc.vector.memset(self.at[u][:, :], 0.0).then_inc(self.setup, 1)
        nc.vector.memset(self.eps[:, :], 1e-5).then_inc(self.setup, 1)
        if self.layer == 1:
            for u in range(self.T):
                nc.vector.memset(self.mid[u][:, :, :], 0.0)
                last = nc.vector.memset(self.lg[u][:, :], NEG)
            last.then_inc(self.setup, 1)
        dve.wait_ge(self.setup, self.n_setup)
        self.chain = Chain(dve, self.s["chain_dve"], self.T * (2 * self.NN + (3 if self.layer == 0 else 8)), self.pad)

    def vector(self, dve, i):
        nc, T, s, bank, chain, norm = self.nc, self.T, self.s, self.bank, self.chain, self.norm
        NE, R = self.NE, self.R
        first = isinstance(i, int) and i == 0
        chain.begin(i)
        yield 2.5
        for u in range(T):
            dve.wait_ge(s["aT_ps"], T * i + u + 1)
            nc.vector.tensor_copy(self.aT[u][:, :, :], bank[u][0][:, :].rearrange("p (c t) -> p c t", c=KC)).then_inc(s["aT_sb"], 1)
        yield 4.5
        for u in range(T):
            y = self.y[u]
            dve.wait_ge(s["y_ps"], T * i + u + 1)
            nc.vector.tensor_tensor(y[:, :], bank[u][1][:, :], self.x[u][:, :], ALU.add).then_inc(s["y_sb"], 1)
            dve.wait_ge(s["y_sb"], T * i + u + 1)
            norm.statistics(chain, u, y[:, :])
        yield 6.5
        for u in range(T):
            norm.apply(dve, chain, u, self.x1[u][:, :], self.y[u][:, :], self.count(i, 0, u)).then_inc(s["x1_sb"], 1)
        yield 8.5
        for u in range(T):
            dve.wait_ge(s["x1T_ps"], T * i + u + 1)
            nc.vector.tensor_copy(self.xT[u][:, :, :], bank[u][self.x1T_bank][:, :].rearrange("p (c t) -> p c t", c=KC)).then_inc(s["x1T_sb"], 1)
        if self.layer == 0:
            yield 10.5
            if first:
                self.weights(dve, 8, 9)
            for u in range(T):
                nc.vector.tensor_tensor(self.xb[u][:, :], self.x1[u][:, :], self.beta[:, :], ALU.add).then_inc(s["xb_sb"], 1)
            yield 14.5
            for u in range(T):
                n, top = T * i + u, self.top[u]
                dve.wait_ge(s["moe_ps"], n + 1)
                chain.carry(u)
                chain.link(nc.vector.max(top[:, :], bank[u][0][:, 0:8]))
                nc.vector.tensor_tensor(self.wsum[u][:, :], top[:, 0:1], top[:, 1:2], ALU.add).then_inc(s["top_sb"], 1)
                dve.wait_ge(s["hid_sb"], n + 1)
                nc.vector.tensor_tensor(self.hsq[u][:, :, :], self.hid[u][:, :, :], self.hid[u][:, :, :], ALU.mult).then_inc(s["hsq_sb"], 1)
            yield 18.5
            for u in range(T):
                n, f = T * i + u, self.f[u]
                dve.wait_ge(s["routed_ps"], n + 1)
                dve.wait_ge(s["t1_sb"], n + 1)
                nc.vector.scalar_tensor_tensor(out=f[:, :], in0=bank[u][0][:, :], scalar=self.wsum[u][:, 0:1],
                                               in1=self.t1[u][:, :], op0=ALU.mult, op1=ALU.add).then_inc(s["f_sb"], 1)
                dve.wait_ge(s["f_sb"], n + 1)
                norm.statistics(chain, u, f[:, :])
            yield 20.5
            for u in range(T):
                n, f = T * i + u, self.f[u]
                dve.wait_ge(s["xb_sb"], n + 1)
                norm.deviation(dve, chain, u, f[:, :], f[:, :], self.gamma[:, :], self.count(i, 1, u))
                chain.link(nc.vector.scalar_tensor_tensor(out=self.y2[u][:, :], in0=f[:, :], scalar=norm.rstd[u][:, 0:1],
                                                          in1=self.xb[u][:, :], op0=ALU.mult, op1=ALU.add))
                norm.statistics(chain, u, self.y2[u][:, :])
        else:
            yield 10.5
            if first:
                self.weights(dve, 4)
            for u in range(T):
                lg, gt, eq = self.lg[u], self.gt[u], self.eq[u]
                dve.wait_ge(s["mid_ps"], T * i + u + 1)
                chain.link(nc.vector.tensor_copy(lg[:, 0:NE], bank[u][0][:, NE * R:NE * R + NE]))
                chain.carry(u)
                chain.link(nc.vector.max(self.top[u][:, :], lg[:, :]))
                nc.vector.tensor_scalar(self.ex[u][:, :], lg[:, 0:NE], self.top[u][:, 0:1], None, ALU.subtract).then_inc(s["lg_sb"], 1)
                mine = lg[:, 0:NE].unsqueeze(2).to_broadcast([128, NE, NE])
                other = lg[:, 0:NE].unsqueeze(1).to_broadcast([128, NE, NE])
                chain.link(nc.vector.tensor_tensor(gt[:, :, :], other, mine, ALU.is_gt))
                chain.link(nc.vector.tensor_tensor(eq[:, :, :], other, mine, ALU.is_equal))
                chain.link(nc.vector.tensor_tensor(eq[:, :, :], eq[:, :, :], self.lower[:, :, :], ALU.mult))
                chain.link(nc.vector.tensor_tensor(gt[:, :, :], gt[:, :, :], eq[:, :, :], ALU.add))
                chain.link(nc.vector.tensor_reduce(self.rank[u][:, :], gt[:, :, :], AX.X, ALU.add))
            yield 12.5
            for u in range(T):
                n, ex = T * i + u, self.ex[u]
                dve.wait_ge(s["ex_sb"], n + 1)
                nc.vector.scalar_tensor_tensor(out=ex[:, :], in0=self.rank[u][:, :], scalar=1.5, in1=ex[:, :],
                                               op0=ALU.is_lt, op1=ALU.mult, accum_out=self.gs[u][:, :]).then_inc(s["mid_sb"], 1)
                dve.wait_ge(s["mid_sb"], 4 * n + 1)
                nc.vector.reciprocal(self.gr[u][:, :], self.gs[u][:, :]).then_inc(s["mid_sb"], 1)
                dve.wait_ge(s["mid_sb"], 4 * n + 2)
                nc.vector.tensor_scalar(ex[:, :], ex[:, :], self.gr[u][:, 0:1], None, ALU.mult).then_inc(s["mid_sb"], 1)
                dve.wait_ge(s["mid_sb"], 4 * n + 3)
                nc.vector.tensor_tensor(self.mid[u][:, 0:NE, :], bank[u][0][:, 0:NE * R].rearrange("p (e r) -> p e r", e=NE),
                                        ex[:, :].unsqueeze(2).to_broadcast([128, NE, R]), ALU.mult).then_inc(s["mid_sb"], 1)
            yield 14.5
            for u in range(T):
                dve.wait_ge(s["midT_ps"], T * i + u + 1)
                nc.vector.tensor_copy(self.midT[u][:, :], bank[u][1][0:NE * R, 0:128]).then_inc(s["midT_sb"], 1)
            yield 20.5
            for u in range(T):
                dve.wait_ge(s["delta_ps"], T * i + u + 1)
                chain.link(nc.vector.scalar_tensor_tensor(out=self.y2[u][:, :], in0=bank[u][1][:, :], scalar=4.0, in1=self.x1[u][:, :],
                                                          op0=ALU.mult, op1=ALU.add))
                norm.statistics(chain, u, self.y2[u][:, :])
        yield 25.5
        for u in range(T):
            if self.out is None:
                ge(dve, self.x2_used, T * i + u)
            else:
                ge(dve, self.x_out[u], 32 * i)
            norm.apply(dve, chain, u, self.x2[u][:, :], self.y2[u][:, :], self.count(i, self.NN - 1, u)).then_inc(s["x2_sb"], 1)
        assert chain.k == chain.per_round, (chain.k, chain.per_round)

    def setup_scalar(self, act):
        act.wait_ge(self.setup, self.n_setup)

    def scalar(self, act, i):
        nc, T, s, bank = self.nc, self.T, self.s, self.bank
        yield 5.5
        for u in range(T):
            self.norm.root(act, u, self.count(i, 0, u))
        if self.layer == 0:
            yield 10.5
            for u in range(T):
                act.wait_ge(s["lat_ps"], T * i + u + 1)
                nc.scalar.activation(self.lat[u][:, :, :], bank[u][0][:, 0:256].rearrange("p (a t) -> p a t", a=2), ACT.Copy).then_inc(s["lat_sb"], 1)
            yield 12.5
            for u in range(T):
                n = T * i + u
                for c in range(2):
                    act.wait_ge(s["up_ps"], 2 * n + c + 1)
                    last = nc.scalar.activation(self.hid[u][:, 4 * c:4 * c + 4, :], bank[u][1 + c][:, :].rearrange("p (a t) -> p a t", a=4), ACT.Relu)
                last.then_inc(s["hid_sb"], 1)
            yield 14.7
            for u in range(T):
                act.wait_ge(s["top_sb"], T * i + u + 1)
                nc.scalar.activation(self.moe[u][:, :, :], bank[u][0][:, 256:512].rearrange("p (a t) -> p a t", a=2), ACT.Copy).then_inc(s["moe_sb"], 1)
            yield 18.2
            for u in range(T):
                act.wait_ge(s["down_ps"], T * i + u + 1)
                nc.scalar.activation(self.t1[u][:, :], bank[u][1][:, :], ACT.Copy).then_inc(s["t1_sb"], 1)
            yield 19.5
            for u in range(T):
                self.norm.root(act, u, self.count(i, 1, u))
        else:
            yield 11.5
            for u in range(T):
                act.wait_ge(s["lg_sb"], T * i + u + 1)
                nc.scalar.activation(self.ex[u][:, :], self.ex[u][:, :], ACT.Exp).then_inc(s["ex_sb"], 1)
        yield 21.5
        for u in range(T):
            self.norm.root(act, u, self.count(i, self.NN - 1, u))

    def gpsimd(self, pool, i):
        return iter(())


def woven_phase(nc, ctx, parts, rounds):
    block = ctx.enter_context(nc.Block())
    whole = [p for p in parts if not isinstance(p, Part)]

    @block.sync
    def _(sp):
        for p in whole:
            p.setup_sync(sp)
        run_rounds(sp, "sync", parts, rounds)
        for p in whole:
            p.finish_sync(sp)

    @block.tensor
    def _(pe):
        for p in whole:
            p.setup_tensor(pe)
        run_rounds(pe, "tensor", parts, rounds)

    @block.scalar
    def _(act):
        for p in whole:
            p.setup_scalar(act)
        run_rounds(act, "scalar", parts, rounds)

    @block.vector
    def _(dve):
        for p in whole:
            p.setup_vector(dve)
        run_rounds(dve, "vector", parts, rounds)

    @block.gpsimd
    def _(pool):
        run_rounds(pool, "gpsimd", parts, rounds)


def context_and_self_attention(nc, io, scr):
    with ExitStack() as ctx:
        parts = [ContextProjection(nc, Arena(nc, ctx, "kv"), io, scr),
                 SelfAttention(nc, Arena(nc, ctx, "sa0"), io, scr, 0, 0, x_src=io["x"])]
        woven_phase(nc, ctx, parts, TILES)


def after_cross_and_self_attention(nc, io, scr):
    with ExitStack() as ctx:
        ff = AfterCross(nc, Arena(nc, ctx, "ff0"), io, scr, 0, 1, None)
        sa = SelfAttention(nc, Arena(nc, ctx, "sa1"), io, scr, 1, 1, x_tile=ff.x2[0], x_ready=ff.s["x2_sb"])
        ff.x2_used = sa.s["xr_sb"]
        woven_phase(nc, ctx, [ff, sa, sa.back], TILES + 2)


def last_after_cross(nc, io, scr, out):
    with ExitStack() as ctx:
        ff = AfterCross(nc, Arena(nc, ctx, "ff1"), io, scr, 1, 4, out)
        woven_phase(nc, ctx, [ff], ff.rounds)



def cross_attention(nc, io, scr, layer):
    NU = 2 * 2 * NCH
    MT = 4 * QG // 128
    NM = 2 * MT * PT
    with ExitStack() as ctx:
        a = Arena(nc, ctx, f"xa{layer}")
        masked = layer == 1
        GS = 1 if masked else 2
        NS, SW = G // GS, GS * QG
        TR = GS * HD
        ZR = 3 * TR + (S if masked else 0)
        KR = ZR + 2
        kst = [a.sb(f"kst{u}", [KR, NS, SK], F16) for u in range(U)]
        qst = [a.sb(f"qst{u}", [KR, NS, SW], F16) for u in range(U)]
        v = [a.sb(f"v{u}", [CH, VW]) for u in range(U)]
        PR, SR, MR = 6, 3, 3
        p = a.sb("p", [CH, PR, QP])
        mxp = [a.sb(f"mxp{h}", [128, MT, PT]) for h in range(2)]
        mneg = [a.sb(f"mneg{h}", [128, MT]) for h in range(2)]
        mhi = [a.sb(f"mhi{h}", [MT, 128], F16) for h in range(2)]
        mlo = [a.sb(f"mlo{h}", [MT, 128], F16) for h in range(2)]
        osb = [a.sb(f"osb{h}", [128, QG]) for h in range(2)]
        rden = [a.sb(f"rden{h}", [112, 2, 4, 1]) for h in range(2)]
        att = [a.sb(f"att{h}", [112, 2, 4, HD]) for h in range(2)]
        ident = a.sb("ident", [128, 128])
        const = a.sb("const", [2, SK], F16)
        if masked:
            mask_u8 = a.sb("mask_u8", [S, SK], U8)
            keep = a.sb("keep", [S, SK])
            maxkeep = a.sb("maxkeep", [S, 1])
            kmask = a.sb("kmask", [S, SK], F16)
            qsel = a.sb("qsel", [S, QG], F16)
            mask_rows = [a.sem(f"mask_rows{u}") for u in range(U)]
        sps = [a.ps(f"sps{n}") for n in range(SR)]
        mps = [a.ps(f"mps{n}") for n in range(MR)]
        ops, TC = [a.ps(f"ops{h}") for h in range(2)], 256

        c_in, cleared, const_rows, setup = a.sem("c_in"), a.sem("cleared"), a.sem("const_rows"), a.sem("setup")
        k_in = [[a.sem(f"k_in{u}_{h}") for h in range(2)] for u in range(U)]
        v_in = [a.sem(f"v_in{u}") for u in range(U)]
        m_in = [[a.sem(f"m_in{u}_{h}") for h in range(2)] for u in range(U)]
        s_ps, p_sb, pv = a.sem("s_ps"), a.sem("p_sb"), a.sem("pv")
        m_ps, m_red, mneg_sb, mT_ps, mhi_sb, mlo_sb = (a.sem(n) for n in ("m_ps", "m_red", "mneg_sb", "mT_ps", "mhi_sb", "mlo_sb"))
        o_sb, oT_ps, rden_sb, att_sb = (a.sem(n) for n in ("o_sb", "oT_ps", "rden_sb", "att_sb"))
        att_out = [a.sem(f"att_out{h}") for h in range(2)]
        block = ctx.enter_context(nc.Block())
        KQ_DMAS = 3 + 3 * GS

        def load_kq(sp, n, i, u, h):
            stacks = slice(h * NS // 2, (h + 1) * NS // 2)
            for r, part in enumerate((0, 0, 1)):
                sp.dma_start(kst[u][TR * r:TR * r + TR, stacks, :],
                             scr["k"][n, part, layer].rearrange("(a r) t -> r a t", r=TR)[:, stacks, :]
                             ).then_inc(k_in[u][h], 16)
            for r, part in enumerate((0, 1, 0)):
                for g in range(GS):
                    rows = slice(TR * r + HD * g, TR * r + HD * g + HD)
                    sp.dma_start(qst[u][rows, stacks, g * QG:(g + 1) * QG],
                                 scr["q"][part, n].rearrange("(a g r) c -> g r a c", g=GS, r=HD)[g, :, stacks, :]
                                 ).then_inc(k_in[u][h], 16)

        def held(eng, value):
            return value if isinstance(value, int) else eng.snap(value)

        def windows(eng, one):
            for u in range(U):
                one(u, 0, u, True, False)
            with eng.Fori(1, B // U - 1) as i:
                for u in range(U):
                    one(U * i + u, i, u, False, False)
            for u in range(U):
                one(B - U + u, B // U - 1, u, False, u == U - 1)

        @block.sync
        def _(sp):
            sp.dma_start(ident[:, :], io["ident"]).then_inc(c_in, 16)
            if masked:
                sp.dma_start(mask_u8[:, :], io["mask"]).then_inc(c_in, 16)
            for u in range(U):
                if not masked:
                    sp.wait_ge(cleared, u + 2)
                for h in range(2):
                    load_kq(sp, u, 0, u, h)
                sp.wait_ge(cleared, 1)
                sp.dma_start(kst[u][ZR:KR, :, :], const[:, :].unsqueeze(1).to_broadcast([2, NS, SK])).then_inc(const_rows, 16)
                if masked:
                    sp.wait_ge(setup, 4)
                    for dst, src, width in ((kst[u], kmask, SK), (qst[u], qsel, QG)):
                        sp.dma_start(dst[3 * TR:ZR, :, :], src[:, :].unsqueeze(1).to_broadcast([S, NS, width])).then_inc(mask_rows[u], 16)
                sp.dma_start(v[u][:, :], scr["v"][layer, u]).then_inc(v_in[u], 16)

            def maximum_out(wb, ub, h):
                for row, (ready, m) in enumerate(((mhi_sb, mhi), (mlo_sb, mlo))):
                    sp.wait_ge(ready, 2 * wb + h + 1)
                    sp.dma_start(qst[ub][ZR + row:ZR + row + 1, h * NS // 2:(h + 1) * NS // 2, :].rearrange("o a c -> o (a c)").rearrange("o (t c) -> o t c", c=128),
                                 m[h][:, :]).then_inc(m_in[ub][h], 16)

            def attention_out(w, h):
                sp.wait_ge(att_sb, 2 * w + h + 1)
                for j2 in range(2):
                    sp.dma_start(scr["att"][w, :, j2 * 256 + h * 128:j2 * 256 + (h + 1) * 128],
                                 att[h][j2 * S:(j2 + 1) * S, :, :, :].rearrange("p a b c -> p (a b c)")).then_inc(att_out[h], 16)

            def window(w, i, u, first, last):
                more = not (isinstance(w, int) and w >= B - U)
                maximum_out(w, u, 1)
                if not (first and u == 0):
                    attention_out(w - 1, 1)
                if more:
                    sp.wait_ge(s_ps, NU * w + NU // 2)
                    load_kq(sp, w + 2, i + 1, u, 0)
                if not last:
                    maximum_out(w + 1, 1 - u, 0)
                attention_out(w, 0)
                if more:
                    sp.wait_ge(s_ps, NU * w + NU)
                    load_kq(sp, w + 2, i + 1, u, 1)
                    sp.wait_ge(pv, 2 * NCH * (w + 1))
                    sp.dma_start(v[u][:, :], scr["v"][layer, w + 2]).then_inc(v_in[u], 16)

            maximum_out(0, 0, 0)
            windows(sp, window)
            attention_out(B - 1, 1)
            for h in range(2):
                sp.wait_ge(att_out[h], 32 * B)

        @block.tensor
        def _(pe):
            pe.wait_ge(c_in, 32 if masked else 16)
            if masked:
                pe.wait_ge(mask_rows[0], 32)

            def pieces(t):
                row = 0
                while row < 128:
                    col = 128 * t + row
                    rows = min(128 if row == 0 else 64 if row == 64 else 32, SW - col % SW)
                    rows = 128 if rows == 128 else 64 if rows >= 64 else 32
                    yield row, rows, col // SW, col % SW
                    row += rows

            def maximum_unit(wb, m0, ib, ub, m):
                h, t, part = m // (MT * PT), m // PT % MT, m % PT
                if m % (MT * PT) == 0:
                    pe.wait_ge(k_in[ub][h], 16 * KQ_DMAS * (ib + 1))
                if not (isinstance(wb, int) and wb == 0 and m < MR):
                    pe.wait_ge(m_red, m0 + m + 1 - MR)
                for row, rows, stack, c in pieces(t):
                    mm = pe.matmul(mps[m % MR][row:row + rows, 0:NP], qst[ub][0:ZR, h * NS // 2 + stack, c:c + rows],
                                   kst[ub][0:ZR, h * NS // 2 + stack, part * NP:(part + 1) * NP], start=True, stop=True)
                mm.then_inc(m_ps, 1)

            def maxima_transposed(wb, h):
                pe.wait_ge(mneg_sb, 2 * wb + h + 1)
                if not isinstance(wb, int) or 2 * wb + h > 1:
                    pe.wait_ge(o_sb, 2 * wb + h - 1)
                pe.transpose(ops[h][0:MT, TC:TC + 128], mneg[h][:, :], ident[:, :]).then_inc(mT_ps, 1)

            def output_transposed(w, h, last=False):
                pe.wait_ge(o_sb, 2 * w + h + 1)
                if not last:
                    pe.wait_ge(mlo_sb, 2 * w + h + 3)
                for jh in range(2):
                    mm = pe.transpose(ops[h][0:112, TC + jh * 128:TC + (jh + 1) * 128], osb[h][:, jh * 112:(jh + 1) * 112], ident[:, :])
                mm.then_inc(oT_ps, 1)

            def pv_step(w, p0, i, u, cs):
                h, k = cs // NCH, cs % NCH
                if k == 0:
                    if h == 0:
                        pe.wait_ge(v_in[u], 16 * (i + 1))
                    if isinstance(w, int) and w == 0:
                        pe.wait_ge(mlo_sb, h + 1)
                    else:
                        pe.wait_ge(att_sb, 2 * w + h - 1)
                pe.wait_ge(p_sb, p0 + 2 * cs + 2)
                for c in range(4):
                    unit = 2 * cs + c // 2
                    g = 4 * h + c
                    mm = pe.matmul(ops[h][32 * c:32 * c + 32, 0:QG],
                                   v[u][:, (k * G + g) * VS:(k * G + g) * VS + 32],
                                   p[:, unit % PR, (c % 2) * QG:(c % 2 + 1) * QG],
                                   start=(k == 0), stop=(k == NCH - 1))
                mm.then_inc(pv, 1)

            def window(w, i, u, first, last):
                s0, m0, p0 = held(pe, NU * w), held(pe, NM * w + NM), held(pe, NU * w)
                for cs in range(2 * NCH):
                    h, k = cs // NCH, cs % NCH
                    if k == 0:
                        pe.wait_ge(m_in[u][h], 32 * (i + 1))
                    for pr in range(2):
                        n = 2 * cs + pr
                        if not (first and u == 0 and n < SR):
                            pe.wait_ge(p_sb, s0 + n + 1 - SR)
                        ch = slice(k * CH, (k + 1) * CH)
                        for c in range(2 // GS):
                            stack = (2 * h + pr) * 2 // GS + c
                            mm = pe.matmul(sps[n % SR][0:CH, c * SW:(c + 1) * SW], kst[u][:, stack, ch], qst[u][:, stack, :],
                                           start=True, stop=True)
                        mm.then_inc(s_ps, 1)
                        if not last and n % 8 != 7:
                            maximum_unit(w + 1, m0, i if u == 0 else i + 1, 1 - u, n - n // 8)
                    if cs > 0:
                        pv_step(w, p0, i, u, cs - 1)
                    elif not (first and u == 0):
                        pv_step(w - 1, p0 - NU, i - (1 - u), 1 - u, 2 * NCH - 1)
                    if cs == 2:
                        maxima_transposed(w, 1)
                    if cs == 4 and not (first and u == 0):
                        output_transposed(w - 1, 1)
                    if cs == 14 and not last:
                        maxima_transposed(w + 1, 0)
                    if cs == 16:
                        output_transposed(w, 0, last)

            for m in range(NM):
                maximum_unit(0, 0, 0, 0, m)
                if m == NM // 2 + 6:
                    maxima_transposed(0, 0)
            pe.wait_ge(const_rows, 16 * U)
            if masked:
                pe.wait_ge(mask_rows[1], 32)
            windows(pe, window)
            pv_step(B - 1, NU * (B - 1), B // U - 1, U - 1, 2 * NCH - 1)
            output_transposed(B - 1, 1, last=True)

        @block.scalar
        def _(act):
            def output_copy(w, h):
                act.wait_ge(pv, 2 * NCH * w + NCH * (h + 1))
                if not (isinstance(w, int) and w == 0):
                    act.wait_ge(oT_ps, 2 * w + h - 1)
                nc.scalar.activation(osb[h][:, :], ops[h][:, 0:QG], ACT.Copy).then_inc(o_sb, 1)

            def window(w, i, u, first, last):
                s0, v0 = held(act, NU * w), held(act, 2 * NCH * w)
                for n in range(NU):
                    act.wait_ge(s_ps, s0 + n + 1)
                    if not (first and u == 0 and n < PR):
                        act.wait_ge(pv, v0 + (n - PR) // 2 + 1)
                    nc.scalar.activation(p[:, n % PR, :], sps[n % SR][0:CH, 0:QP], ACT.Exp).then_inc(p_sb, 1)
                    if n == 3 and not (first and u == 0):
                        output_copy(w - 1, 1)
                    if n == 2 * NCH + 3:
                        output_copy(w, 0)

            windows(act, window)
            output_copy(B - 1, 1)

        @block.vector
        def _(dve):
            nc.vector.memset(const[:, :], WSCALE).then_inc(cleared, 1)
            for u in range(U):
                if not masked:
                    nc.vector.memset(qst[u][:, :, :], 0.0).then_inc(cleared, 1)
            dve.wait_ge(c_in, 32 if masked else 16)
            if masked:
                nc.vector.tensor_copy(keep[:, :], mask_u8[:, :]).then_inc(setup, 1)
                dve.wait_ge(setup, 1)
                nc.vector.reduce_max(maxkeep[:, :], keep[:, :], AX.X).then_inc(setup, 1)
                dve.wait_ge(setup, 2)
                nc.vector.tensor_scalar(kmask[:, :], keep[:, :], maxkeep[:, 0:1], BIG, ALU.subtract, ALU.mult).then_inc(setup, 1)
                nc.vector.tensor_scalar(qsel[:, :].rearrange("p (h q) -> p h q", q=S),
                                        ident[0:S, 0:S].unsqueeze(1).to_broadcast([S, J, S]), BIG, None, ALU.mult).then_inc(setup, 1)

            def maximum(wb, m0, m):
                h, t, part = m // (MT * PT), m // PT % MT, m % PT
                dve.wait_ge(m_ps, m0 + m + 1)
                nc.vector.tensor_reduce(mxp[h][:, t, part:part + 1], mps[m % MR][:, 0:NP], AX.X, ALU.max).then_inc(m_red, 1)
                if m % (MT * PT) == MT * PT - 1:
                    dve.wait_ge(m_red, m0 + m + 1)
                    if not (isinstance(wb, int) and wb == 0):
                        dve.wait_ge(mT_ps, 2 * wb + h - 1)
                    nc.vector.tensor_reduce(mneg[h][:, :], mxp[h][:, :, :], AX.X, ALU.max, negate=True).then_inc(mneg_sb, 1)

            def maximum_rows(wb, ib, ub, h):
                dve.wait_ge(mT_ps, 2 * wb + h + 1)
                if not (isinstance(wb, int) and wb == 0):
                    ge(dve, m_in[1 - ub][h], 32 * (ib + ub))
                nc.vector.tensor_scalar(mhi[h][:, :], ops[h][0:MT, TC:TC + 128], 1.0 / WSCALE, None, ALU.mult).then_inc(mhi_sb, 1)
                dve.wait_ge(mhi_sb, 2 * wb + h + 1)
                nc.vector.scalar_tensor_tensor(out=mlo[h][:, :], in0=ops[h][0:MT, TC:TC + 128], scalar=1.0 / WSCALE, in1=mhi[h][:, :],
                                               op0=ALU.mult, op1=ALU.subtract).then_inc(mlo_sb, 1)

            def output_scaled(w, i, h):
                o = ops[h][0:112, TC:TC + 256].rearrange("p (j c v) -> p j c v", j=2, c=4)
                dve.wait_ge(oT_ps, 2 * w + h + 1)
                nc.vector.reciprocal(rden[h][:, :, :, :], o[:, :, :, HD:HD + 1]).then_inc(rden_sb, 1)
                dve.wait_ge(rden_sb, 2 * w + h + 1)
                ge(dve, att_out[h], 32 * w)
                nc.vector.tensor_tensor(att[h][:, :, :, :], o[:, :, :, 0:HD], rden[h][:, :, :, :].to_broadcast([112, 2, 4, HD]),
                                        ALU.mult).then_inc(att_sb, 1)

            def window(w, i, u, first, last):
                m0 = held(dve, NM * w + NM)
                for n in range(NU):
                    if not last and n % 8 != 7:
                        maximum(w + 1, m0, n - n // 8)
                    if n == 5:
                        maximum_rows(w, i, u, 1)
                    if n == 9 and not (first and u == 0):
                        output_scaled(w - 1, i, 1)
                    if n == 29 and not last:
                        maximum_rows(w + 1, i if u == 0 else i + 1, 1 - u, 0)
                    if n == 33:
                        output_scaled(w, i, 0)

            for m in range(NM):
                maximum(0, 0, m)
                if m == NM // 2 + 6:
                    maximum_rows(0, 0, 0, 0)
            windows(dve, window)
            output_scaled(B - 1, B // U - 1, 1)


def decoder_kernel(nc, io, out):
    scr = {
        "k": nc.dram_tensor("scr_k", [B, 2, 2, 128, SK], F16, kind="Internal").ap(),
        "v": nc.dram_tensor("scr_v", [2, B, CH, VW], F32, kind="Internal").ap(),
        "q": nc.dram_tensor("scr_q", [2, B, 128, QG], F16, kind="Internal").ap(),
        "att": nc.dram_tensor("scr_att", [B, S, D], F32, kind="Internal").ap(),
        "x": nc.dram_tensor("scr_x", [2, TILES, 128, D], F32, kind="Internal").ap(),
    }
    context_and_self_attention(nc, io, scr)
    cross_attention(nc, io, scr, 0)
    after_cross_and_self_attention(nc, io, scr)
    cross_attention(nc, io, scr, 1)
    last_after_cross(nc, io, scr, out)


def layout(inputs, np):
    f = lambda n: np.asarray(inputs[n])
    g, j, d = np.meshgrid(np.arange(G), np.arange(J), np.arange(HD), indexing="ij")
    head = ((g * J + j) * HD + d)
    by_j = head.transpose(1, 0, 2).reshape(-1)
    rot_q = head[:, :, (np.arange(HD) + HD // 2) % HD].transpose(1, 0, 2).reshape(-1)
    kv = np.arange(128).reshape(G, HD)
    rot_k = kv[:, (np.arange(HD) + HD // 2) % HD].reshape(-1)
    stored = head.reshape(2, 4, 2, 2, HD).transpose(3, 0, 2, 1, 4).reshape(-1)
    x = f("x")
    xp = np.zeros((B, SP_, D), x.dtype)
    xp[:, :S] = x
    io = {"x": xp.reshape(TILES, 128, D), "ctxT": f("ctx_4096").transpose(0, 2, 1), "mask": f("mask_SxS2_bk0")}
    io["wkv"] = np.concatenate([f("L0_xattn_Wk"), f("L1_xattn_w_k").T, f("L0_xattn_Wv"), f("L1_xattn_w_v").T], axis=1)
    io["sa0_wq"], io["sa0_wk"] = f("L0_attn_Wq").T, f("L0_attn_Wk").T
    io["sa0_wv"], io["sa0_wo"] = f("L0_attn_Wv").T, f("L0_attn_Wo").T
    for n in ("bq", "bk", "bv", "bo"):
        b = f(f"L0_attn_{n}")
        io[f"sa0_{n}"] = b.reshape(KC, 128).T if n in ("bq", "bk") else b
    wq, wk = f("L1_attn_Wq"), f("L1_attn_Wk")
    io["sa1_wq"] = np.concatenate([wq[:, by_j], wq[:, rot_q]], axis=1)
    io["sa1_wk"] = np.concatenate([wk, wk[:, rot_k]], axis=1)
    io["sa1_wv"], io["sa1_wo"] = f("L1_attn_Wv"), f("L1_attn_Wo")[by_j, :]
    io["xa0_wq"], io["xa0_wo"] = f("L0_xattn_Wq")[:, by_j], f("L0_xattn_Wo")[stored, :]
    io["xa1_wq"], io["xa1_wo"] = f("L1_xattn_w_q").T[:, by_j], f("L1_xattn_w_out").T[stored, :]
    io["up"], io["down"], io["fc1"] = f("L0_ffn_up_w"), f("L0_ffn_down_w"), f("L0_ffn_fc1_w")
    io["expert"], io["fc2"], io["gate"] = f("L0_ffn_expert_w"), f("L0_ffn_fc2_w"), f("L0_ffn_gate_w")
    io["gamma"], io["beta"] = f("L0_ffn_ln_gamma"), f("L0_ffn_ln_beta")
    io["lora_a"] = np.concatenate([f("L1_ffn_A").reshape(-1, D), f("L1_ffn_router_w")], axis=0).T
    io["lora_b"] = f("L1_ffn_B").transpose(0, 2, 1).reshape(-1, D)
    io["ident"] = np.eye(128, dtype=np.float32)
    io["blockmask"] = np.repeat((np.arange(128)[:, None] // HD == np.arange(8)[None, :]).astype(np.float32), SP_, axis=1)
    q = np.arange(128)[:, None] % SP_
    k = np.arange(SP_)[None, :]
    io["causal"] = np.where((k <= q) & (k < S), 0.0, NEG).astype(np.float32)
    half = HD // 2
    freq = (1.0 / np.float32(10000.0) ** (np.arange(half, dtype=np.float32) / np.float32(half))).astype(np.float32)
    ang = np.arange(SP_, dtype=np.float32)[None, :] * freq[np.arange(128) % half][:, None]
    sign = np.where(np.arange(128) % HD < half, -1.0, 1.0).astype(np.float32)[:, None]
    cos, sin = np.cos(ang).astype(np.float32), (sign * np.sin(ang)).astype(np.float32)
    io["rope"] = np.concatenate([cos * np.float32(0.25), sin * np.float32(0.25), cos, sin], axis=1)
    io["lower"] = np.tile((np.arange(4)[None, :] < np.arange(4)[:, None]).astype(np.float32).reshape(1, -1), (128, 1))
    return {n: np.ascontiguousarray(v) for n, v in io.items()}


def kernel(**inputs):
    import numpy as _np
    import concourse.bacc as _bacc
    from concourse import mybir as _mybir
    from concourse.bass_utils import run_bass_kernel_spmd as _run

    nc = _bacc.Bacc("TRN2", target_bir_lowering=False, num_devices=1)
    io = layout(inputs, _np)
    arrays = {f"in_{n}": v for n, v in io.items()}
    aps = {n: nc.dram_tensor(f"in_{n}", list(v.shape), _mybir.dt.from_np(v.dtype), kind="ExternalInput").ap()
           for n, v in io.items()}
    out = nc.dram_tensor("out_x", [B, S, D], F32, kind="ExternalOutput").ap()
    decoder_kernel(nc, aps, out)
    r = _run(nc, [arrays], core_ids=[0])
    return r.results[0]["out_x"]
```
